# Optimizing a Trainium2 kernel written in Bass

```python
import numpy as np
import jax
import jax.numpy as jnp

def _softmax(x, axis=-1):
    return jax.nn.softmax(x, axis=axis)

def _gelu(x):
    return jax.nn.gelu(x, approximate=True)

def _silu(x):
    return jax.nn.silu(x)

def _sigmoid(x):
    return jax.nn.sigmoid(x)

def _layernorm(x, axis=-1, eps=1e-05):
    m = jnp.mean(x, axis=axis, keepdims=True)
    v = jnp.var(x, axis=axis, keepdims=True)
    return (x - m) / jnp.sqrt(v + eps)

def _scatter_add(tgt, idx, src, axis=0):
    return tgt.at[idx].add(src)

def _segment_sum(src, seg, n):
    return jax.ops.segment_sum(src, seg, n)
kernel_name = 'mk_perceiver_d2_seqx_r8_1d320a'

def setup_inputs(seed: int=0):
    np.random.seed(seed)
    _w = jnp.asarray

    def _rec_inputs():
        import jax
        import jax.numpy as jnp
        _rk = jax.random.key(seed)
        x = -0.0002928 + 1 * jax.random.normal(jax.random.fold_in(_rk, 1), (64, 64, 128), jnp.float32)
        _lenS = 64 - jax.random.randint(jax.random.fold_in(_rk, 7), (64,), 0, max(1, 64 // 4) + 1, jnp.int32)
        _lenS2 = 128 - jax.random.randint(jax.random.fold_in(_rk, 8), (64,), 0, max(1, 128 // 4) + 1, jnp.int32)
        _ctx_1024P = jax.random.normal(jax.random.fold_in(_rk, 11), (64, 16, 128), jnp.float32)
        _ctx_1024c = jax.random.dirichlet(jax.random.fold_in(_rk, 511), 0.3 * jnp.ones((16,), jnp.float32), (64, 128))
        _ctx_1024t = jnp.einsum('bsk,bkd->bsd', _ctx_1024c, _ctx_1024P)
        _ctx_1024t = _ctx_1024t * jax.lax.rsqrt(jnp.mean(jnp.square(_ctx_1024t)) + 1e-12) * 0.953939
        ctx_1024 = -1.39393e-06 + 0.999914 * (_ctx_1024t + 0.3 * jax.random.normal(jax.random.fold_in(_rk, 611), (64, 128, 128), jnp.float32))
        _validS = jnp.arange(64)[None, :] < _lenS[:, None]
        _validS2 = jnp.arange(128)[None, :] < _lenS2[:, None]
        _causal = jnp.tril(jnp.ones((64, 64), dtype=bool))
        mask_BxS2_bf1 = jnp.ones((64, 128), dtype=bool)
        return (x, ctx_1024, mask_BxS2_bf1)
    x, ctx_1024, mask_BxS2_bf1 = _rec_inputs()

    def _L0_xattn_setup():
        import jax, jax.numpy as jnp
        import numpy as np
        D_MODEL = 128
        NUM_HEADS = 16
        D_K = D_MODEL // NUM_HEADS
        SCALE = float(np.sqrt(D_K))

        def _split_heads(x):
            B, S, _ = x.shape
            return x.reshape(B, S, NUM_HEADS, D_K).transpose(0, 2, 1, 3)
        key = jax.random.key(seed)
        ks = jax.random.split(key, 11)
        B, S, D = (2, 256, D_MODEL)

        def lin(kw):
            lim = float(np.sqrt(6.0 / (D + D)))
            return jax.random.uniform(kw, (D, D), jnp.float32, -lim, lim)
        return {'q': jax.random.normal(ks[0], (B, S, D), jnp.float32), 'k': jax.random.normal(ks[1], (B, S, D), jnp.float32), 'v': jax.random.normal(ks[2], (B, S, D), jnp.float32), 'Wq': lin(ks[3]), 'bq': jnp.zeros((D,), jnp.float32), 'Wk': lin(ks[4]), 'bk': jnp.zeros((D,), jnp.float32), 'Wv': lin(ks[5]), 'bv': jnp.zeros((D,), jnp.float32), 'Wo': lin(ks[6]), 'bo': jnp.zeros((D,), jnp.float32)}
    _L0_xattn_all = _L0_xattn_setup()
    _L0_xattn_in = {k: v for k, v in _L0_xattn_all.items() if k in ('Wq', 'bq', 'Wk', 'bk', 'Wv', 'bv', 'Wo', 'bo')}
    del _L0_xattn_all

    def _L0_attn_setup():
        import jax, jax.numpy as jnp
        import numpy as np
        D_MODEL = 128
        D_FF = 512
        FFN_H = int(2 * D_FF / 3)
        B, S = (4, 512)
        LN_EPS = 1e-05
        ATTN_EPS = 1e-06

        def layer_norm(x, g, b):
            mu = jnp.mean(x, axis=-1, keepdims=True)
            var = jnp.mean(jnp.square(x - mu), axis=-1, keepdims=True)
            return (x - mu) * jax.lax.rsqrt(var + LN_EPS) * g + b
        key = jax.random.key(seed)
        ks = jax.random.split(key, 16)
        s = 0.02
        return {'x': jax.random.normal(ks[0], (B, S, D_MODEL), dtype=jnp.float32), 'Wqkv': jax.random.normal(ks[1], (D_MODEL, 3 * D_MODEL), dtype=jnp.float32) * s, 'bqkv': jnp.zeros((3 * D_MODEL,), jnp.float32), 'Wg': jax.random.normal(ks[2], (D_MODEL, FFN_H), dtype=jnp.float32) * s, 'bg': jnp.zeros((FFN_H,), jnp.float32), 'Wu': jax.random.normal(ks[3], (D_MODEL, FFN_H), dtype=jnp.float32) * s, 'bu': jnp.zeros((FFN_H,), jnp.float32), 'Wd': jax.random.normal(ks[4], (FFN_H, D_MODEL), dtype=jnp.float32) * s, 'bd': jnp.zeros((D_MODEL,), jnp.float32), 'g1': jnp.ones((D_MODEL,), jnp.float32), 'b1': jnp.zeros((D_MODEL,), jnp.float32), 'g2': jnp.ones((D_MODEL,), jnp.float32), 'b2': jnp.zeros((D_MODEL,), jnp.float32)}
    _L0_attn_all = _L0_attn_setup()
    _L0_attn_in = {k: v for k, v in _L0_attn_all.items() if k in ('Wqkv', 'bqkv', 'Wg', 'bg', 'Wu', 'bu', 'Wd', 'bd', 'g1', 'b1', 'g2', 'b2')}
    del _L0_attn_all

    def _L0_ffn_setup():
        import jax, jax.numpy as jnp
        import numpy as np
        HIDDEN = 128
        MOE_FF = 64
        SHARED_FF = 352
        NUM_EXPERTS = 16
        TOP_K = 2
        NORM_TOPK = True
        key = jax.random.key(seed)
        ks = jax.random.split(key, 8)
        s = 0.02
        return {'layer_input': jax.random.normal(ks[0], (1, 256, HIDDEN), dtype=jnp.float32), 'gate_w': jax.random.normal(ks[1], (NUM_EXPERTS, HIDDEN), dtype=jnp.float32) * s, 'w_gate_up': jax.random.normal(ks[2], (NUM_EXPERTS, HIDDEN, 2 * MOE_FF), dtype=jnp.float32) * s, 'w_down': jax.random.normal(ks[3], (NUM_EXPERTS, MOE_FF, HIDDEN), dtype=jnp.float32) * s, 'shared_w_gate': jax.random.normal(ks[4], (SHARED_FF, HIDDEN), dtype=jnp.float32) * s, 'shared_w_up': jax.random.normal(ks[5], (SHARED_FF, HIDDEN), dtype=jnp.float32) * s, 'shared_w_down': jax.random.normal(ks[6], (HIDDEN, SHARED_FF), dtype=jnp.float32) * s, 'shared_gate_w': jax.random.normal(ks[7], (1, HIDDEN), dtype=jnp.float32) * s}
    _L0_ffn_all = _L0_ffn_setup()
    _L0_ffn_in = {k: v for k, v in _L0_ffn_all.items() if k in ('gate_w', 'w_gate_up', 'w_down', 'shared_w_gate', 'shared_w_up', 'shared_w_down', 'shared_gate_w')}
    del _L0_ffn_all

    def _L1_xattn_setup():
        import jax, jax.numpy as jnp
        import numpy as np
        D_MODEL = 128
        N_HEADS = 16
        HEAD_DIM = D_MODEL // N_HEADS
        key = jax.random.key(seed)
        ks = jax.random.split(key, 11)
        B, Q, K = (4, 256, 256)
        s = 1.0 / np.sqrt(D_MODEL)
        inp = {'q': jax.random.normal(ks[0], (B, Q, D_MODEL), jnp.float32), 'k': jax.random.normal(ks[1], (B, K, D_MODEL), jnp.float32), 'v': jax.random.normal(ks[2], (B, K, D_MODEL), jnp.float32), 'kv_mask': jnp.ones((B, K), dtype=bool), 'Wq': jax.random.normal(ks[3], (D_MODEL, D_MODEL), jnp.float32) * s, 'bq': jnp.zeros((D_MODEL,), jnp.float32), 'Wk': jax.random.normal(ks[4], (D_MODEL, D_MODEL), jnp.float32) * s, 'bk': jnp.zeros((D_MODEL,), jnp.float32), 'Wv': jax.random.normal(ks[5], (D_MODEL, D_MODEL), jnp.float32) * s, 'bv': jnp.zeros((D_MODEL,), jnp.float32), 'Wo': jax.random.normal(ks[6], (D_MODEL, D_MODEL), jnp.float32) * s, 'bo': jnp.zeros((D_MODEL,), jnp.float32)}
        return inp
    _L1_xattn_all = _L1_xattn_setup()
    _L1_xattn_in = {k: v for k, v in _L1_xattn_all.items() if k in ('Wq', 'bq', 'Wk', 'bk', 'Wv', 'bv', 'Wo', 'bo')}
    del _L1_xattn_all

    def _L1_attn_setup():
        import jax, jax.numpy as jnp
        import numpy as np
        NUM_HEADS = 16
        key = jax.random.key(seed)
        x = jax.random.normal(key, (4, 256, 128), dtype=jnp.float32)
        return {'x': x}
    _L1_attn_all = _L1_attn_setup()
    _L1_attn_in = {k: v for k, v in _L1_attn_all.items() if k in ()}
    del _L1_attn_all

    def _L1_ffn_setup():
        import jax, jax.numpy as jnp
        import numpy as np
        D_MODEL, FF_DIM = (128, 256)
        N_SHARED, N_ROUTED, TOP_K = (1, 8, 2)
        BATCH, SEQ = (2, 256)
        key = jax.random.key(seed)
        ks = jax.random.split(key, 8)
        init = lambda k, shape: jax.random.normal(k, shape, jnp.float32) * 0.02
        x = jax.random.normal(ks[0], (BATCH, SEQ, D_MODEL), jnp.float32)
        Wg = init(ks[1], (D_MODEL, N_ROUTED))
        Ws1 = init(ks[2], (D_MODEL, FF_DIM))
        Ws3 = init(ks[3], (D_MODEL, FF_DIM))
        Ws2 = init(ks[4], (FF_DIM, D_MODEL))
        We1 = init(ks[5], (N_ROUTED, D_MODEL, FF_DIM))
        We3 = init(ks[6], (N_ROUTED, D_MODEL, FF_DIM))
        We2 = init(ks[7], (N_ROUTED, FF_DIM, D_MODEL))
        return {'x': x, 'Wg': Wg, 'Ws1': Ws1, 'Ws3': Ws3, 'Ws2': Ws2, 'We1': We1, 'We3': We3, 'We2': We2}
    _L1_ffn_all = _L1_ffn_setup()
    _L1_ffn_in = {k: v for k, v in _L1_ffn_all.items() if k in ('Wg', 'Ws1', 'Ws3', 'Ws2', 'We1', 'We3', 'We2')}
    del _L1_ffn_all
    return {'x': x, 'ctx_1024': ctx_1024, 'mask_BxS2_bf1': mask_BxS2_bf1, 'L0_xattn_Wq': _L0_xattn_in['Wq'], 'L0_xattn_bq': _L0_xattn_in['bq'], 'L0_xattn_Wk': _L0_xattn_in['Wk'], 'L0_xattn_bk': _L0_xattn_in['bk'], 'L0_xattn_Wv': _L0_xattn_in['Wv'], 'L0_xattn_bv': _L0_xattn_in['bv'], 'L0_xattn_Wo': _L0_xattn_in['Wo'], 'L0_xattn_bo': _L0_xattn_in['bo'], 'L0_attn_Wqkv': _L0_attn_in['Wqkv'], 'L0_attn_bqkv': _L0_attn_in['bqkv'], 'L0_attn_Wg': _L0_attn_in['Wg'], 'L0_attn_bg': _L0_attn_in['bg'], 'L0_attn_Wu': _L0_attn_in['Wu'], 'L0_attn_bu': _L0_attn_in['bu'], 'L0_attn_Wd': _L0_attn_in['Wd'], 'L0_attn_bd': _L0_attn_in['bd'], 'L0_attn_g1': _L0_attn_in['g1'], 'L0_attn_b1': _L0_attn_in['b1'], 'L0_attn_g2': _L0_attn_in['g2'], 'L0_attn_b2': _L0_attn_in['b2'], 'L0_ffn_gate_w': _L0_ffn_in['gate_w'], 'L0_ffn_w_gate_up': _L0_ffn_in['w_gate_up'], 'L0_ffn_w_down': _L0_ffn_in['w_down'], 'L0_ffn_shared_w_gate': _L0_ffn_in['shared_w_gate'], 'L0_ffn_shared_w_up': _L0_ffn_in['shared_w_up'], 'L0_ffn_shared_w_down': _L0_ffn_in['shared_w_down'], 'L0_ffn_shared_gate_w': _L0_ffn_in['shared_gate_w'], 'L1_xattn_Wq': _L1_xattn_in['Wq'], 'L1_xattn_bq': _L1_xattn_in['bq'], 'L1_xattn_Wk': _L1_xattn_in['Wk'], 'L1_xattn_bk': _L1_xattn_in['bk'], 'L1_xattn_Wv': _L1_xattn_in['Wv'], 'L1_xattn_bv': _L1_xattn_in['bv'], 'L1_xattn_Wo': _L1_xattn_in['Wo'], 'L1_xattn_bo': _L1_xattn_in['bo'], 'L1_ffn_Wg': _L1_ffn_in['Wg'], 'L1_ffn_Ws1': _L1_ffn_in['Ws1'], 'L1_ffn_Ws3': _L1_ffn_in['Ws3'], 'L1_ffn_Ws2': _L1_ffn_in['Ws2'], 'L1_ffn_We1': _L1_ffn_in['We1'], 'L1_ffn_We3': _L1_ffn_in['We3'], 'L1_ffn_We2': _L1_ffn_in['We2']}

def reference(x, ctx_1024, mask_BxS2_bf1, L0_xattn_Wq, L0_xattn_bq, L0_xattn_Wk, L0_xattn_bk, L0_xattn_Wv, L0_xattn_bv, L0_xattn_Wo, L0_xattn_bo, L0_attn_Wqkv, L0_attn_bqkv, L0_attn_Wg, L0_attn_bg, L0_attn_Wu, L0_attn_bu, L0_attn_Wd, L0_attn_bd, L0_attn_g1, L0_attn_b1, L0_attn_g2, L0_attn_b2, L0_ffn_gate_w, L0_ffn_w_gate_up, L0_ffn_w_down, L0_ffn_shared_w_gate, L0_ffn_shared_w_up, L0_ffn_shared_w_down, L0_ffn_shared_gate_w, L1_xattn_Wq, L1_xattn_bq, L1_xattn_Wk, L1_xattn_bk, L1_xattn_Wv, L1_xattn_bv, L1_xattn_Wo, L1_xattn_bo, L1_ffn_Wg, L1_ffn_Ws1, L1_ffn_Ws3, L1_ffn_Ws2, L1_ffn_We1, L1_ffn_We3, L1_ffn_We2):
    import jax
    import jax.numpy as jnp

    def _L0_xattn_ref(q, k, v, Wq, bq, Wk, bk, Wv, bv, Wo, bo):
        import jax, jax.numpy as jnp
        import numpy as np
        D_MODEL = 128
        NUM_HEADS = 16
        D_K = D_MODEL // NUM_HEADS
        SCALE = float(np.sqrt(D_K))

        def _split_heads(x):
            B, S, _ = x.shape
            return x.reshape(B, S, NUM_HEADS, D_K).transpose(0, 2, 1, 3)
        Q = _split_heads(q @ Wq.T + bq)
        K = _split_heads(k @ Wk.T + bk)
        V = _split_heads(v @ Wv.T + bv)
        scores = jnp.einsum('bhqd,bhkd->bhqk', Q, K) / SCALE
        m = jax.lax.stop_gradient(jnp.max(scores, axis=-1, keepdims=True))
        exp_scores = jnp.exp(scores - m)
        attn = exp_scores / (jnp.sum(exp_scores, axis=-1, keepdims=True) + 1e-09)
        out = jnp.einsum('bhqk,bhkd->bhqd', attn, V)
        B, H, S, dk = out.shape
        out = out.transpose(0, 2, 1, 3).reshape(B, S, H * dk)
        return out @ Wo.T + bo

    def _L0_attn_ref(x, Wqkv, bqkv, Wg, bg, Wu, bu, Wd, bd, g1, b1, g2, b2):
        import jax, jax.numpy as jnp
        import numpy as np
        D_MODEL = 128
        D_FF = 512
        FFN_H = int(2 * D_FF / 3)
        B, S = (4, 512)
        LN_EPS = 1e-05
        ATTN_EPS = 1e-06

        def layer_norm(x, g, b):
            mu = jnp.mean(x, axis=-1, keepdims=True)
            var = jnp.mean(jnp.square(x - mu), axis=-1, keepdims=True)
            return (x - mu) * jax.lax.rsqrt(var + LN_EPS) * g + b
        qkv = jnp.einsum('bsd,de->bse', x, Wqkv) + bqkv
        q, k, v = jnp.split(qkv, 3, axis=-1)
        qp = jax.nn.elu(q) + 1.0
        kp = jax.nn.elu(k) + 1.0
        kv = jnp.einsum('bsd,bse->bde', kp, v)
        num = jnp.einsum('bsd,bde->bse', qp, kv)
        k_sum = jnp.sum(kp, axis=1)
        den = jnp.einsum('bsd,bd->bs', qp, k_sum)[..., None]
        attn = num / (den + ATTN_EPS)
        x = layer_norm(x + attn, g1, b1)
        gate = jnp.einsum('bsd,dh->bsh', x, Wg) + bg
        up = jnp.einsum('bsd,dh->bsh', x, Wu) + bu
        ffn = jnp.einsum('bsh,hd->bsd', jax.nn.silu(gate) * up, Wd) + bd
        return layer_norm(x + ffn, g2, b2)

    def _L0_ffn_ref(layer_input, gate_w, w_gate_up, w_down, shared_w_gate, shared_w_up, shared_w_down, shared_gate_w):
        import jax, jax.numpy as jnp
        import numpy as np
        HIDDEN = 128
        MOE_FF = 64
        SHARED_FF = 352
        NUM_EXPERTS = 16
        TOP_K = 2
        NORM_TOPK = True
        B, S, D = layer_input.shape
        x = layer_input.reshape(-1, D)
        N = x.shape[0]
        shared = jax.nn.silu(x @ shared_w_gate.T) * (x @ shared_w_up.T) @ shared_w_down.T
        shared = shared * jax.nn.sigmoid(x @ shared_gate_w.T)
        logits = x @ gate_w.T
        probs = jax.nn.softmax(logits.astype(jnp.float32), axis=-1)
        rw, sel = jax.lax.top_k(probs, TOP_K)
        if NORM_TOPK:
            rw = rw / rw.sum(axis=-1, keepdims=True)
        rw = rw.astype(x.dtype)
        combine = jnp.zeros((N, NUM_EXPERTS), x.dtype).at[jnp.arange(N)[:, None], sel].set(rw)
        gu = jnp.einsum('nd,edf->nef', x, w_gate_up)
        g, h = jnp.split(gu, 2, axis=-1)
        h = jax.nn.silu(g) * h
        expert_out = jnp.einsum('nef,efd,ne->nd', h, w_down, combine)
        out = expert_out + shared
        return out.reshape(B, S, D)

    def _L1_xattn_ref(q, k, v, kv_mask, Wq, bq, Wk, bk, Wv, bv, Wo, bo):
        import jax, jax.numpy as jnp
        import numpy as np
        D_MODEL = 128
        N_HEADS = 16
        HEAD_DIM = D_MODEL // N_HEADS
        B, Qlen, _ = q.shape
        Klen = k.shape[1]
        qh = (q @ Wq.T + bq).reshape(B, Qlen, N_HEADS, HEAD_DIM).transpose(0, 2, 1, 3)
        kh = (k @ Wk.T + bk).reshape(B, Klen, N_HEADS, HEAD_DIM).transpose(0, 2, 1, 3)
        vh = (v @ Wv.T + bv).reshape(B, Klen, N_HEADS, HEAD_DIM).transpose(0, 2, 1, 3)
        score = jnp.einsum('bhqd,bhkd->bhqk', qh, kh) / np.sqrt(HEAD_DIM).astype(np.float32)
        score = jnp.where(kv_mask[:, None, None, :], score, jnp.float32(-10000.0))
        attn = jax.nn.softmax(score, axis=-1)
        out = jnp.einsum('bhqk,bhkd->bhqd', attn, vh)
        out = out.transpose(0, 2, 1, 3).reshape(B, Qlen, D_MODEL)
        return out @ Wo.T + bo

    def _L1_attn_ref(x):
        import jax, jax.numpy as jnp
        import numpy as np
        NUM_HEADS = 16
        B, T, D = x.shape
        H = NUM_HEADS
        hd = D // H
        xh = x.reshape(B, T, H, hd)
        x_centered = xh - jnp.mean(xh, axis=1, keepdims=True)
        corr = jnp.einsum('bthd,bThd->bhtT', x_centered, x_centered)
        corr = jax.nn.softmax(corr, axis=-1)
        out = jnp.einsum('bhtT,bThd->bthd', corr, xh)
        return out.reshape(B, T, D)

    def _L1_ffn_ref(x, Wg, Ws1, Ws3, Ws2, We1, We3, We2):
        import jax, jax.numpy as jnp
        import numpy as np
        D_MODEL, FF_DIM = (128, 256)
        N_SHARED, N_ROUTED, TOP_K = (1, 8, 2)
        BATCH, SEQ = (2, 256)
        B, S, d = x.shape
        E = Wg.shape[1]
        xf = x.reshape(-1, d)
        T = xf.shape[0]
        gates = jax.nn.sigmoid(xf @ Wg)
        vals, idx = jax.lax.top_k(gates, TOP_K)
        vals = vals / vals.sum(axis=-1, keepdims=True)
        w = jnp.zeros((T, E), x.dtype).at[jnp.arange(T)[:, None], idx].add(vals)
        shared = jax.nn.silu(xf @ Ws1) * (xf @ Ws3) @ Ws2
        h = jax.nn.silu(jnp.einsum('td,edf->tef', xf, We1)) * jnp.einsum('td,edf->tef', xf, We3)
        routed = jnp.einsum('tef,efd,te->td', h, We2, w)
        out = (shared + routed) / (N_SHARED + TOP_K)
        return out.reshape(B, S, d)
    x = x + _L0_xattn_ref(_layernorm(x, axis=-1), ctx_1024, ctx_1024, L0_xattn_Wq, L0_xattn_bq, L0_xattn_Wk, L0_xattn_bk, L0_xattn_Wv, L0_xattn_bv, L0_xattn_Wo, L0_xattn_bo)
    x = x + _L0_attn_ref(_layernorm(x, axis=-1), L0_attn_Wqkv, L0_attn_bqkv, L0_attn_Wg, L0_attn_bg, L0_attn_Wu, L0_attn_bu, L0_attn_Wd, L0_attn_bd, L0_attn_g1, L0_attn_b1, L0_attn_g2, L0_attn_b2)
    x = x + _L0_ffn_ref(_layernorm(x, axis=-1), L0_ffn_gate_w, L0_ffn_w_gate_up, L0_ffn_w_down, L0_ffn_shared_w_gate, L0_ffn_shared_w_up, L0_ffn_shared_w_down, L0_ffn_shared_gate_w)
    x = x + _L1_xattn_ref(_layernorm(x, axis=-1), ctx_1024, ctx_1024, mask_BxS2_bf1, L1_xattn_Wq, L1_xattn_bq, L1_xattn_Wk, L1_xattn_bk, L1_xattn_Wv, L1_xattn_bv, L1_xattn_Wo, L1_xattn_bo)
    x = x + _L1_attn_ref(_layernorm(x, axis=-1))
    x = x + _L1_ffn_ref(_layernorm(x, axis=-1), L1_ffn_Wg, L1_ffn_Ws1, L1_ffn_Ws3, L1_ffn_Ws2, L1_ffn_We1, L1_ffn_We3, L1_ffn_We2)
    return x

_drawn_inputs = setup_inputs


def setup_inputs(seed=0):
    import zlib

    import numpy as np

    out = dict(_drawn_inputs(seed))
    spreads = {'L0_xattn_bq': (0.0, 0.408),
     'L0_xattn_bk': (0.0, 0.8),
     'L0_xattn_bv': (0.0, 0.1),
     'L0_xattn_bo': (0.0, 0.1),
     'L0_attn_bqkv': (0.0, 0.1),
     'L0_attn_bg': (0.0, 0.8),
     'L0_attn_bu': (0.0, 0.8),
     'L0_attn_bd': (0.0, 0.1),
     'L0_attn_g1': (1.0, 0.2),
     'L0_attn_b1': (0.0, 0.1),
     'L0_attn_g2': (1.0, 0.2),
     'L0_attn_b2': (0.0, 0.1),
     'L1_xattn_bq': (0.0, 0.8),
     'L1_xattn_bk': (0.0, 0.8),
     'L1_xattn_bv': (0.0, 0.1),
     'L1_xattn_bo': (0.0, 0.1)}
    factors = {'L0_attn_Wg': 8.0,
     'L0_attn_Wu': 8.0,
     'L0_attn_Wd': 8.0,
     'L0_ffn_gate_w': 8.0,
     'L0_ffn_w_gate_up': 8.0,
     'L0_ffn_w_down': 8.0,
     'L0_ffn_shared_w_gate': 8.0,
     'L0_ffn_shared_w_up': 8.0,
     'L0_ffn_shared_w_down': 8.0,
     'L0_ffn_shared_gate_w': 8.0,
     'L1_ffn_Wg': 8.0,
     'L1_ffn_Ws1': 8.0,
     'L1_ffn_Ws3': 8.0,
     'L1_ffn_Ws2': 8.0,
     'L1_ffn_We1': 8.0,
     'L1_ffn_We3': 8.0,
     'L1_ffn_We2': 8.0}
    for name, (base, spread) in spreads.items():
        noise = np.random.default_rng([zlib.crc32(name.encode()), seed]).standard_normal(out[name].shape)
        drawn = base * np.exp(spread * noise) if base else spread * noise
        out[name] = jnp.asarray(drawn.astype(out[name].dtype))
    for name, factor in factors.items():
        out[name] = (out[name] * factor).astype(out[name].dtype)
    return out
```

```python
from contextlib import ExitStack, contextmanager

import numpy as np

import concourse.bass as bass
from concourse import mybir

F32 = mybir.dt.float32
F32R = mybir.dt.float32r
BF16 = mybir.dt.bfloat16
U8 = mybir.dt.uint8
ALU = mybir.AluOpType
ACT = mybir.ActivationFunctionType
AX = mybir.AxisListType

P = 128
B, S, D = 64, 64, 128
SK = 128
H, DH = 16, 8
T = B * S // P
CH = 512
NC = B * S // CH
TPC = CH // P
G, J = 4, 4
W32 = J * DH
PAIRS = H // 2
MASKED = -10000.0
MASKED_UNSCALED = -28288.0


def head_constants():
    sel = np.zeros((P, G, 4, P), np.float32)
    for g in range(G):
        for which, blocks in enumerate(((0, 1), (2, 3), (0, 2), (1, 3))):
            for r in blocks:
                for a in range(W32):
                    sel[W32 * g + a, g, which, W32 * r + a] = 1.0
    selm = np.zeros((64, PAIRS, P), np.float32)
    for i in range(PAIRS):
        selm[i, i] = selm[32 + i, i] = 1.0
    mask4 = np.zeros((P, J), np.float32)
    for row in range(P):
        mask4[row, row % W32 // DH] = 1.0
    return sel.reshape(P, -1), selm.reshape(64, -1), mask4


def spread_constants(experts_of_block):
    m = np.zeros((P, len(experts_of_block), P), np.float32)
    for f, row in enumerate(experts_of_block):
        for col, e in enumerate(row):
            m[e, f, col] = m[32 + e, f, col] = 1.0
    return m.reshape(P, -1)


L0_E, L0_F, L0_SHARED = 16, 64, 352
L0_SPREAD = [[2 * f] * 64 + [2 * f + 1] * 64 for f in range(8)] + [[16] * P] * 3
L1_E, L1_F = 8, 256
L1_SPREAD = [[e] * P for e in range(8)]
L0_H = 341


def after(eng, sem, count):
    if not isinstance(count, int) or count > 0:
        eng.wait_ge(sem, count)


def in_pairs(eng, n, step, peel=1):
    for p in range(peel):
        step(2 * p, 0)
        step(2 * p + 1, 1)
    with eng.Fori(peel, n // 2 - peel) as p:
        step(p * 2, 0)
        step(p * 2 + 1, 1)
    for p in range(n // 2 - peel, n // 2):
        step(2 * p, 0)
        step(2 * p + 1, 1)


def span(start, n):
    return slice(start, start + n) if isinstance(start, int) else bass.ds(start, n)


def cols(ap, at, n):
    ap = ap.unsqueeze(at)
    shape = list(ap.shape)
    shape[at] = n
    return ap.broadcast_to(shape)


def f32(ap):
    return ap.bitcast(F32)


class Mem:

    def __init__(self, nc, stack, name):
        self.nc, self.stack, self.name, self.sems = nc, stack, name, []

    def sb(self, name, shape, dt=F32):
        return self.stack.enter_context(self.nc.sbuf_tensor(f"{self.name}_{name}", shape, dt))

    def ps(self, name, shape, dt=F32):
        return self.stack.enter_context(self.nc.psum_tensor(f"{self.name}_{name}", shape, dt))

    def sem(self, name):
        s = self.nc.alloc_semaphore(f"{self.name}_{name}")
        self.sems.append(s)
        return s


@contextmanager
def phase(nc, name):
    with ExitStack() as stack:
        mem = Mem(nc, stack, name)
        yield mem
        nc.clear_and_free_semaphores(mem.sems)
        nc.all_engine_barrier()


def layernorm(nc, name, src, eps, ident, xnT=None, nat=None, gain=None, shift=None, add_to=None):
    with phase(nc, name) as m:
        stats = m.sb("stats", [P, T, 6])
        meanvar = m.sb("meanvar", [P, T, 2])
        ve = m.sb("ve", [P, T])
        power = m.sb("power", [P, T])
        rstd = m.sb("rstd", [P, T])
        work = m.sb("work", [P, 2, TPC, D])
        bank = m.ps("bank", [P, 2, CH])
        stats_done, aggr_done = m.sem("stats_done"), m.sem("aggr_done")
        pool_step, rstd_ready = m.sem("pool_step"), m.sem("rstd_ready")
        xn_ready, normed, scaled = m.sem("xn_ready"), m.sem("normed"), m.sem("scaled")
        turned, evacuated, kept = m.sem("turned"), m.sem("evacuated"), m.sem("kept")

        with nc.Block() as block:
            @block.vector
            def _(dve):
                with dve.Fori(0, T) as t:
                    dve.bn_stats(stats[:, t, :], src[:, t, :]).then_inc(stats_done, 1)
                for t in range(T):
                    dve.wait_ge(stats_done, t + 1)
                    dve.bn_aggr(meanvar[:, t, :], stats[:, t, :]).then_inc(aggr_done, 1)
                dve.wait_ge(rstd_ready, 1)

                def chunk(k, par):
                    if xnT is not None:
                        after(dve, turned, k - 1)
                    if nat is not None:
                        after(dve, kept, k - 1)
                    for i in range(TPC):
                        t = k * TPC + i
                        op = dve.tensor_scalar(work[:, par, i, :], src[:, t, :], meanvar[:, t, 0:1],
                                               rstd[:, span(t, 1)], ALU.subtract, ALU.mult)
                    op.then_inc(normed if gain is not None else xn_ready, 1)
                    o = work[:, par]
                    if gain is not None:
                        dve.wait_ge(normed, k + 1)
                        dve.tensor_tensor(o, o, cols(gain[:, :], 1, TPC), ALU.mult).then_inc(scaled, 1)
                        dve.wait_ge(scaled, k + 1)
                        dve.tensor_tensor(o, o, cols(shift[:, :], 1, TPC), ALU.add).then_inc(xn_ready, 1)
                    if add_to is not None:
                        dve.wait_ge(xn_ready, k + 1)
                        y = add_to[:, span(k * TPC, TPC), :]
                        dve.tensor_tensor(y, y, o, ALU.add)
                in_pairs(dve, NC, chunk)

            @block.gpsimd
            def _(pool):
                pool.memset(power[:, :], -0.5).then_inc(pool_step, 1)
                pool.wait_ge(aggr_done, T)
                pool.tensor_scalar(ve[:, :], meanvar[:, :, 1], eps, None, ALU.add).then_inc(pool_step, 1)
                pool.wait_ge(pool_step, 2)
                pool.tensor_tensor(rstd[:, :], ve[:, :], power[:, :], ALU.pow).then_inc(rstd_ready, 1)

                def chunk(k, par):
                    pool.wait_ge(xn_ready, k + 1)
                    pool.tensor_copy(nat[:, span(k * TPC, TPC), :], work[:, par]).then_inc(kept, 1)
                if nat is not None:
                    in_pairs(pool, NC, chunk)

            if xnT is not None:
                @block.tensor
                def _(pe):
                    def chunk(k, par):
                        pe.wait_ge(xn_ready, k + 1)
                        after(pe, evacuated, k - 1)
                        for i in range(TPC):
                            op = pe.transpose(bank[:, par, P * i:P * i + P], work[:, par, i, :], ident[:, :])
                        op.then_inc(turned, 1)
                    in_pairs(pe, NC, chunk)

                @block.scalar
                def _(act):
                    def chunk(k, par):
                        act.wait_ge(turned, k + 1)
                        act.activation(xnT[:, span(k * CH, CH)], bank[:, par, :], ACT.Copy)\
                           .then_inc(evacuated, 1)
                    in_pairs(act, NC, chunk)


def load(nc, name, pairs):
    with phase(nc, name) as m:
        loaded = m.sem("loaded")
        with nc.Block() as block:
            @block.sync
            def _(sp):
                for dst, src in pairs[0::2]:
                    sp.dma_start(dst, src).then_inc(loaded, 16)
                sp.wait_ge(loaded, 16 * len(pairs))

            @block.scalar
            def _(act):
                for dst, src in pairs[1::2]:
                    act.dma_start(dst, src).then_inc(loaded, 16)


def transpose_all(nc, name, jobs, ident):
    with phase(nc, name) as m:
        bank = m.ps("bank", [P, 2, TPC, P])
        turned, evacuated = m.sem("turned"), m.sem("evacuated")
        groups = [jobs[i:i + TPC] for i in range(0, len(jobs), TPC)]
        with nc.Block() as block:
            @block.tensor
            def _(pe):
                for n, group in enumerate(groups):
                    after(pe, evacuated, sum(map(len, groups[:n - 1])) if n > 1 else 0)
                    for i, (dst, src) in enumerate(group):
                        p, q = src.shape
                        op = pe.transpose(bank[0:q, n % 2, i, 0:p], src, ident[0:p, 0:p])
                    op.then_inc(turned, 1)

            @block.vector
            def _(dve):
                for n, group in enumerate(groups):
                    dve.wait_ge(turned, n + 1)
                    for i, (dst, src) in enumerate(group):
                        p, q = src.shape
                        dve.tensor_copy(dst, bank[0:q, n % 2, i, 0:p]).then_inc(evacuated, 1)


def split(nc, name, jobs):
    with phase(nc, name) as m:
        hi_done = m.sem("hi_done")
        with nc.Block() as block:
            @block.vector
            def _(dve):
                for n, (hi, lo, a) in enumerate(jobs):
                    dve.tensor_copy(hi, a).then_inc(hi_done, 1)
                for n, (hi, lo, a) in enumerate(jobs):
                    if lo is not None:
                        dve.wait_ge(hi_done, n + 1)
                        dve.tensor_tensor(lo, a, f32(hi), ALU.subtract)


def keys_values(nc, name, ctx, Kh, Kl, V, WkT, WvT, bk, bv_all, ident, mask=None):
    n = B * SK // CH
    per = CH // SK
    with phase(nc, name) as m:
        ctx_nat = m.sb("ctx_nat", [P, 2, per, D])
        ctxT = m.sb("ctxT", [P, 2, CH])
        keep = m.sb("keep", [P, 2, CH], U8)
        y = m.sb("y", [P, 2, CH])
        bank_t, bank_k, bank_v = m.ps("bank_t", [P, 2, CH]), m.ps("bank_k", [P, 2, CH]), m.ps("bank_v", [P, 2, CH])
        ctx_in = [m.sem("ctx_in0"), m.sem("ctx_in1")]
        turned, ctxT_ready, k_done, v_done = m.sem("turned"), m.sem("ctxT_ready"), m.sem("k_done"), m.sem("v_done")
        y_ready, hi_ready, lo_ready, v_stored = m.sem("y_ready"), m.sem("hi_ready"), m.sem("lo_ready"), m.sem("v_stored")
        loads = 2 if mask is not None else 1
        with nc.Block() as block:
            @block.sync
            def _(sp):
                def chunk(c, par):
                    after(sp, turned, c - 1)
                    if mask is not None:
                        after(sp, y_ready, c - 1)
                    sp.dma_start(ctx_nat[:, par], ctx[span(c * per, per), :, :].rearrange("b k d -> k b d"))\
                      .then_inc(ctx_in[par], 16)
                    if mask is not None:
                        rows = mask[span(c * per, per), :].rearrange("b k -> (b k)").unsqueeze(0)
                        sp.dma_start(keep[:, par], rows.broadcast_to([P, CH])).then_inc(ctx_in[par], 16)
                in_pairs(sp, n, chunk)

            @block.tensor
            def _(pe):
                def chunk(c, par):
                    pe.wait_ge(ctx_in[par], half(c, par) * 16 * loads)
                    after(pe, ctxT_ready, c - 1)
                    for i in range(per):
                        op = pe.transpose(bank_t[:, par, P * i:P * i + P], ctx_nat[:, par, i, :], ident[:, :])
                    op.then_inc(turned, 1)
                    pe.wait_ge(ctxT_ready, c + 1)
                    after(pe, y_ready, c - 1)
                    pe.matmul(bank_k[:, par, :], WkT[:, :], ctxT[:, par, :], start=True, stop=True).then_inc(k_done, 1)
                    after(pe, v_stored, c - 1)
                    for i in range(per):
                        op = pe.matmul(bank_v[:, par, P * i:P * i + P], ctxT[:, par, P * i:P * i + P], WvT[:, :],
                                       start=True, stop=True)
                    op.then_inc(v_done, 1)
                in_pairs(pe, n, chunk)

            @block.scalar
            def _(act):
                def chunk(c, par):
                    act.wait_ge(turned, c + 1)
                    after(act, v_done, c - 1)
                    act.activation(ctxT[:, par, :], bank_t[:, par, :], ACT.Copy).then_inc(ctxT_ready, 1)
                    act.wait_ge(y_ready, c + 1)
                    act.activation(Kh[:, span(c * CH, CH)], y[:, par, :], ACT.Copy).then_inc(hi_ready, 1)
                in_pairs(act, n, chunk)

            @block.vector
            def _(dve):
                def chunk(c, par):
                    dve.wait_ge(k_done, c + 1)
                    after(dve, hi_ready, c - 1)
                    if mask is not None:
                        dve.wait_ge(ctx_in[par], half(c, par) * 16 * loads)
                        dve.scalar_tensor_tensor(out=y[:, par, :], in0=bank_k[:, par, :], scalar=bk[:, 0:1],
                                                 in1=keep[:, par, :], op0=ALU.add, op1=ALU.mult).then_inc(y_ready, 1)
                    else:
                        dve.tensor_scalar(y[:, par, :], bank_k[:, par, :], bk[:, 0:1], None, ALU.add).then_inc(y_ready, 1)
                    dve.wait_ge(v_done, c + 1)
                    dve.tensor_tensor(V[:, span(c * per, per), :],
                                      bank_v[:, par, :].rearrange("p (i d) -> p i d", d=D),
                                      cols(bv_all[:, :], 1, per), ALU.add).then_inc(v_stored, 1)
                    dve.wait_ge(hi_ready, c + 1)
                    dve.tensor_tensor(Kl[:, span(c * CH, CH)], y[:, par, :], f32(Kh[:, span(c * CH, CH)]),
                                      ALU.subtract).then_inc(lo_ready, 1)
                in_pairs(dve, n, chunk)


def half(c, par):
    return (c - par) // 2 + 1


def queries(nc, name, xnT, Qh, Ql, WqT, bq):
    with phase(nc, name) as m:
        bank = m.ps("bank", [P, 2, CH])
        y = m.sb("y", [P, 2, CH])
        q_done, y_ready, hi_ready, lo_ready = m.sem("q_done"), m.sem("y_ready"), m.sem("hi_ready"), m.sem("lo_ready")
        with nc.Block() as block:
            @block.tensor
            def _(pe):
                def chunk(k, par):
                    after(pe, y_ready, k - 1)
                    pe.matmul(bank[:, par, :], WqT[:, :], xnT[:, span(k * CH, CH)], start=True, stop=True)\
                      .then_inc(q_done, 1)
                in_pairs(pe, NC, chunk)

            @block.scalar
            def _(act):
                def chunk(k, par):
                    act.wait_ge(q_done, k + 1)
                    after(act, lo_ready, k - 1)
                    act.activation(y[:, par, :], bank[:, par, :], ACT.Identity, bias=bq[:, 0:1]).then_inc(y_ready, 1)
                in_pairs(act, NC, chunk)

            @block.vector
            def _(dve):
                def chunk(k, par):
                    dve.wait_ge(y_ready, k + 1)
                    dve.tensor_copy(Qh[:, span(k * CH, CH)], y[:, par, :]).then_inc(hi_ready, 1)
                    dve.wait_ge(hi_ready, k + 1)
                    dve.tensor_tensor(Ql[:, span(k * CH, CH)], y[:, par, :], f32(Qh[:, span(k * CH, CH)]),
                                      ALU.subtract).then_inc(lo_ready, 1)
                in_pairs(dve, NC, chunk)


def attention(nc, name, Kh, Kl, V, Qh, Ql, AT, con, nk, scale, den_eps=None, mask=None, mask_bias=None):
    own = nk < P
    n = B
    ident, sel, selm, mask4 = con["ident"], con["sel"], con["selm"], con["mask4"]
    with phase(nc, name) as m:
        Kst = m.sb("Kst", [P, 2, G, P], F32R)
        Qst = m.sb("Qst", [P, 2, G, J, S], F32R)
        Pr = m.sb("Pr", [P, 2, G, J * S])
        Vb = m.sb("Vb", [P, 2, D])
        mneg = m.sb("mneg", [P, 2, P])
        mx = m.sb("mx", [P, 2, PAIRS])
        mt2 = m.sb("mt2", [64, 2, P], F32R)
        rec = m.sb("rec", [P, 2, J, S])
        recm = m.sb("recm", [P, 2, J, S])
        on = m.sb("on", [P, 2, J, S])
        ones = m.sb("ones", [P, W32])
        ps_m = m.ps("ps_m", [P, PAIRS, P])
        ps_s = m.ps("ps_s", [P, PAIRS, P])
        ps_k, ps_q = m.ps("ps_k", [P, G, P]), m.ps("ps_q", [P, G, S])
        ps_o = m.ps("ps_o", [P, 2, J, S])
        ps_t = m.ps("ps_t", [P, P])
        kq_done, k_copied, q_copied = m.sem("kq_done"), m.sem("k_copied"), m.sem("q_copied")
        mp_done, mx_done, mneg_ready = m.sem("mp_done"), m.sem("mx_done"), m.sem("mneg_ready")
        mt_done, mt_hi, mt_ready = m.sem("mt_done"), m.sem("mt_hi"), m.sem("mt_ready")
        st_done, addm_done, exp_done = m.sem("st_done"), m.sem("addm_done"), m.sem("exp_done")
        pv_done, den_read, rec_ready = m.sem("pv_done"), m.sem("den_read"), m.sem("rec_ready")
        recm_ready, on_ready, at_ready = m.sem("recm_ready"), m.sem("on_ready"), m.sem("at_ready")
        v_copied, set_up = m.sem("v_copied"), m.sem("set_up")
        if mask is not None:
            mrow8 = m.sb("mrow8", [1, 2, P], U8)
            mrow = m.sb("mrow", [1, 2, P], BF16)
            ones_row = m.sb("ones_row", [1, P], BF16)
            mask_in, mrow_ready = [m.sem("mask_in0"), m.sem("mask_in1")], m.sem("mrow_ready")

        def keys_at(u, par):
            return (u - par) * S if own else u * SK

        def part(par):
            return slice(nk * par, nk * par + nk) if own else slice(0, P)

        with nc.Block() as block:
            @block.tensor
            def _(pe):
                def stack(u, par):
                    after(pe, k_copied, u)
                    after(pe, q_copied, u)
                    kc = keys_at(u, par)
                    for g in range(G):
                        pe.matmul(ps_k[:, g, :], sel[:, g, 0, :], Kh[:, span(kc, P)], start=True, stop=False)
                        pe.matmul(ps_k[:, g, :], sel[:, g, 1, :], Kl[:, span(kc, P)], start=False, stop=True)
                    for g in range(G):
                        pe.matmul(ps_q[:, g, :], sel[:, g, 2, :], Qh[:, span(u * S, S)], start=True, stop=False)
                        op = pe.matmul(ps_q[:, g, :], sel[:, g, 3, :], Ql[:, span(u * S, S)], start=False, stop=True)
                    op.then_inc(kq_done, 1)

                def scores_for_max(u, par):
                    pe.wait_ge(k_copied, u + 1)
                    pe.wait_ge(q_copied, u + 1)
                    after(pe, mx_done, u)
                    if mask is not None:
                        pe.wait_ge(mrow_ready, u + 1)
                    for i in range(PAIRS):
                        q = Qst[:, par, i // 2, 2 * (i % 2):2 * (i % 2) + 2, :]
                        first = i % 4 == 0
                        op = pe.matmul(ps_m[:, i, 0:nk], q, Kst[:, par, i // 2, part(par)],
                                       start=first or mask is None, stop=mask is None, skip_group_check=True)
                        if mask is not None and i % 4 == 3:
                            op = pe.matmul(ps_m[:, i - 3:i + 1, :], ones_row[:, :], cols(mrow[:, par, :], 1, 4),
                                           start=False, stop=True, skip_group_check=True)
                    op.then_inc(mp_done, 1)

                def unit(u, par):
                    pe.wait_ge(mneg_ready, u + 1)
                    pe.transpose(ps_t[:, :], mneg[:, par, :], ident[:, :]).then_inc(mt_done, 1)
                    after(pe, exp_done, u)
                    for g in range(G):
                        op = pe.matmul(ps_s[:, 2 * g:2 * g + 2, :], Kst[:, par, g, :], Qst[:, par, g, :, :],
                                       start=g % 2 == 0, stop=False, skip_group_check=True)
                    op.then_inc(st_done, 1)
                    if not (isinstance(u, int) and u == 0):
                        weigh(u - 1, 1 - par)
                    pe.wait_ge(mt_ready, u + 1)
                    for i in range(PAIRS):
                        op = pe.matmul(ps_s[:, i, :], selm[:, i, :], mt2[:, par, :], start=False,
                                       stop=i % 4 == 3, skip_group_check=True)
                    op.then_inc(addm_done, 1)
                    if not (isinstance(u, int) and u + 1 >= n):
                        scores_for_max(u + 1, 1 - par)
                    if not (isinstance(u, int) and u + 2 >= n):
                        stack(u + 2, par)

                def weigh(u, par):
                    pe.wait_ge(exp_done, u + 1)
                    pe.wait_ge(v_copied, u + 1)
                    after(pe, on_ready, u)
                    for g in range(G):
                        pe.matmul(ps_o[W32 * g:W32 * g + W32, 0, :, :], Vb[:, par, W32 * g:W32 * g + W32],
                                  Pr[:, par, g, :], start=True, stop=True)
                    for g in range(G):
                        op = pe.matmul(ps_o[W32 * g:W32 * g + W32, 1, :, :], ones[:, :], Pr[:, par, g, :],
                                       start=True, stop=True)
                    op.then_inc(pv_done, 1)

                pe.wait_ge(set_up, 3 if own or mask is not None else 2)
                stack(0, 0)
                scores_for_max(0, 0)
                stack(1, 1)
                in_pairs(pe, n, unit)
                weigh(n - 1, 1)

            @block.scalar
            def _(act):
                def spread(u, par):
                    act.wait_ge(kq_done, u + 1)
                    after(act, st_done, u - 1)
                    for j in range(J):
                        op = act.activation(Qst[:, par, :, j, :], ps_q[:, :, :], ACT.Copy, scale=mask4[:, j:j + 1])
                    op.then_inc(q_copied, 1)

                def load_mask(u, par):
                    after(act, mrow_ready, u - 1)
                    act.dma_start(mrow8[:, par], mask[span(u, 1), :]).then_inc(mask_in[par], 16)

                def unit(u, par):
                    if mask is not None and not (isinstance(u, int) and u + 3 >= n):
                        load_mask(u + 3, 1 - par)
                    act.wait_ge(addm_done, u + 1)
                    after(act, pv_done, u - 1)
                    k = part(par)
                    out, src = Pr[k, par], ps_s[k, :, :]
                    if mask_bias is not None:
                        act.activation(out, src, ACT.Exp, scale=scale, bias=mask_bias[:, span(u, 1)]).then_inc(exp_done, 1)
                    else:
                        act.activation(out, src, ACT.Exp, scale=scale).then_inc(exp_done, 1)
                    if not (isinstance(u, int) and u + 2 >= n):
                        spread(u + 2, par)

                if own:
                    act.wait_ge(set_up, 3)
                if mask is not None:
                    load_mask(0, 0)
                    load_mask(1, 1)
                spread(0, 0)
                if mask is not None:
                    load_mask(2, 0)
                spread(1, 1)
                in_pairs(act, n, unit, peel=2)

            @block.gpsimd
            def _(pool):
                pool.memset(ones[:, :], 1.0).then_inc(set_up, 1)
                pool.memset(mneg[:, :, :], 0.0).then_inc(set_up, 1)
                if own:
                    pool.memset(Pr[:, :, :, :], 0.0).then_inc(set_up, 1)
                if mask is not None:
                    pool.memset(ones_row[:, :], 1.0).then_inc(set_up, 1)

                def values(u, par):
                    pool.tensor_copy(Vb[:, par, :], V[:, (u - par) // 2 if own else u, :]).then_inc(v_copied, 1)

                def unit(u, par):
                    pool.wait_ge(rec_ready, u + 1)
                    after(pool, on_ready, u - 1)
                    pool.tensor_tensor(recm[:, par], rec[:, par], cols(mask4[:, :], 2, S), ALU.mult)\
                        .then_inc(recm_ready, 1)
                    if not (isinstance(u, int) and u + 2 >= n):
                        values(u + 2, par)

                values(0, 0)
                values(1, 1)
                in_pairs(pool, n, unit)

            @block.vector
            def _(dve):
                def keys(u, par):
                    if mask is not None:
                        dve.wait_ge(mask_in[par], half(u, par) * 16)
                        after(dve, mp_done, u - 1)
                        dve.tensor_scalar(mrow[:, par], mrow8[:, par], -MASKED_UNSCALED, MASKED_UNSCALED,
                                          ALU.mult, ALU.add).then_inc(mrow_ready, 1)
                    dve.wait_ge(kq_done, u + 1)
                    after(dve, st_done, u - 1)
                    dve.tensor_copy(Kst[:, par], ps_k[:, :, :]).then_inc(k_copied, 1)

                def maxima(u, par):
                    dve.wait_ge(mp_done, u + 1)
                    dve.tensor_reduce(mx[:, par], ps_m[:, :, 0:nk], AX.X, ALU.max).then_inc(mx_done, 1)
                    dve.wait_ge(mx_done, u + 1)
                    after(dve, mt_done, u - 1)
                    dve.tensor_scalar(mneg[:, par, 0:64].rearrange("p (a b) -> p a b", a=2)[:, :, 0:PAIRS],
                                      cols(mx[:, par], 1, 2), -1.0, None, ALU.mult).then_inc(mneg_ready, 1)

                def minus_max(u, par):
                    dve.wait_ge(mt_done, u + 1)
                    after(dve, addm_done, u - 1)
                    dve.tensor_copy(mt2[:, par], ps_t[0:64, :]).then_inc(mt_hi, 1)
                    dve.wait_ge(mt_hi, u + 1)
                    dve.tensor_tensor(mt2[32:64, par], ps_t[32:64, :], f32(mt2[32:64, par]), ALU.subtract)\
                       .then_inc(mt_ready, 1)

                def reciprocals(u, par):
                    dve.wait_ge(pv_done, u + 1)
                    after(dve, recm_ready, u - 1)
                    dve.tensor_scalar(rec[:, par], ps_o[:, 1], den_eps or 0.0, None, ALU.add).then_inc(den_read, 1)
                    dve.wait_ge(den_read, u + 1)
                    dve.reciprocal(rec[:, par], rec[:, par]).then_inc(rec_ready, 1)

                def outputs(u, par):
                    dve.wait_ge(recm_ready, u + 1)
                    dve.tensor_tensor(on[:, par], ps_o[:, 0], recm[:, par], ALU.mult).then_inc(on_ready, 1)
                    dve.wait_ge(on_ready, u + 1)
                    dve.tensor_reduce(AT[:, span(u * S, S)], on[:, par].rearrange("p j q -> p q j"), AX.X, ALU.add)\
                       .then_inc(at_ready, 1)

                def unit(u, par):
                    minus_max(u, par)
                    if not (isinstance(u, int) and u == 0):
                        reciprocals(u - 1, 1 - par)
                    if not (isinstance(u, int) and u + 1 >= n):
                        maxima(u + 1, 1 - par)
                    if not (isinstance(u, int) and u == 0):
                        outputs(u - 1, 1 - par)
                    if not (isinstance(u, int) and u + 2 >= n):
                        keys(u + 2, par)

                dve.wait_ge(set_up, 2)
                keys(0, 0)
                maxima(0, 0)
                keys(1, 1)
                in_pairs(dve, n, unit)
                reciprocals(n - 1, 1)
                outputs(n - 1, 1)


def project_add(nc, name, AT, x, ident, WT=None, bias=None):
    with phase(nc, name) as m:
        bank, bank_t = m.ps("bank", [P, 2, CH]), m.ps("bank_t", [P, 2, TPC, D])
        y = m.sb("y", [P, 2, CH])
        projected, y_ready, turned, added = m.sem("projected"), m.sem("y_ready"), m.sem("turned"), m.sem("added")
        with nc.Block() as block:
            @block.tensor
            def _(pe):
                def chunk(k, par):
                    if WT is not None:
                        after(pe, y_ready, k - 1)
                        pe.matmul(bank[:, par, :], WT[:, :], AT[:, span(k * CH, CH)], start=True, stop=True)\
                          .then_inc(projected, 1)
                    pe.wait_ge(y_ready, k + 1)
                    after(pe, added, k - 1)
                    for i in range(TPC):
                        op = pe.transpose(bank_t[:, par, i, :], y[:, par, P * i:P * i + P], ident[:, :])
                    op.then_inc(turned, 1)
                in_pairs(pe, NC, chunk)

            @block.scalar
            def _(act):
                def chunk(k, par):
                    after(act, turned, k - 1)
                    if WT is not None:
                        act.wait_ge(projected, k + 1)
                        act.activation(y[:, par, :], bank[:, par, :], ACT.Identity, bias=bias[:, 0:1]).then_inc(y_ready, 1)
                    else:
                        act.activation(y[:, par, :], AT[:, span(k * CH, CH)], ACT.Copy).then_inc(y_ready, 1)
                in_pairs(act, NC, chunk)

            @block.vector
            def _(dve):
                def chunk(k, par):
                    dve.wait_ge(turned, k + 1)
                    xs = x[:, span(k * TPC, TPC), :]
                    dve.tensor_tensor(xs, xs, bank_t[:, par], ALU.add).then_inc(added, 1)
                in_pairs(dve, NC, chunk)


def route(nc, name, xnT, gateT, E, combT, ident, sigmoid_gate, shared_gate):
    EX = E + 1 if shared_gate else E
    LOW, HIT = -3.0e38, 3.2e38
    with phase(nc, name) as m:
        bank, bank_t = m.ps("bank", [P, 2, CH]), m.ps("bank_t", [P, 2, TPC, P])
        bank_c = m.ps("bank_c", [P, 2, CH])
        lT = m.sb("lT", [P, 2, CH])
        L = m.sb("L", [P, T, EX])
        vals = m.sb("vals", [P, T, E + 8])
        best = m.sb("best", [P, T, 8])
        found = m.sb("found", [P, T, 8])
        marked = m.sb("marked", [P, T, E + 8])
        e1 = m.sb("e1", [P, T, EX])
        gap = m.sb("gap", [P, T, 1])
        den = m.sb("den", [P, T, 1])
        C = m.sb("C", [P, T, P])
        logits_done, lT_ready, turned, L_ready = m.sem("logits_done"), m.sem("lT_ready"), m.sem("turned"), m.sem("L_ready")
        step, act_step, best_done, marked_done = m.sem("step"), m.sem("act_step"), m.sem("best_done"), m.sem("marked_done")
        prepared, comb_ready, c_turned, c_hi, c_lo = (m.sem("prepared"), m.sem("comb_ready"), m.sem("c_turned"),
                                                      m.sem("c_hi"), m.sem("c_lo"))
        with nc.Block() as block:
            @block.gpsimd
            def _(pool):
                pool.memset(vals[:, :, E:], LOW).then_inc(prepared, 1)
                pool.memset(found[:, :, :], LOW).then_inc(prepared, 1)
                pool.memset(C[:, :, :], 0.0).then_inc(prepared, 1)

            @block.tensor
            def _(pe):
                def chunk(k, par):
                    after(pe, lT_ready, k - 1)
                    pe.matmul(bank[:, par, :], gateT[:, :], xnT[:, span(k * CH, CH)], start=True, stop=True)\
                      .then_inc(logits_done, 1)
                    pe.wait_ge(lT_ready, k + 1)
                    after(pe, L_ready, k - 1)
                    for i in range(TPC):
                        op = pe.transpose(bank_t[:, par, i, :], lT[:, par, P * i:P * i + P], ident[:, :])
                    op.then_inc(turned, 1)
                in_pairs(pe, NC, chunk)
                pe.wait_ge(comb_ready, 3 if shared_gate else 2)
                for k in range(NC):
                    after(pe, c_lo, k - 1)
                    for i in range(TPC):
                        op = pe.transpose(bank_c[:, k % 2, P * i:P * i + P], C[:, TPC * k + i, :], ident[:, :])
                    op.then_inc(c_turned, 1)

            @block.scalar
            def _(act):
                def chunk(k, par):
                    act.wait_ge(logits_done, k + 1)
                    after(act, turned, k - 1)
                    act.activation(lT[:, par, :], bank[:, par, :], ACT.Copy).then_inc(lT_ready, 1)
                in_pairs(act, NC, chunk)
                if sigmoid_gate:
                    act.wait_ge(L_ready, NC)
                    act.activation(e1[:, :, :], L[:, :, :], ACT.Exp, scale=-1.0).then_inc(act_step, 1)
                else:
                    act.wait_ge(step, 3)
                    act.activation(e1[:, :, 0:E], e1[:, :, 0:E], ACT.Exp).then_inc(act_step, 1)
                    act.activation(e1[:, :, E:EX], L[:, :, E:EX], ACT.Exp, scale=-1.0).then_inc(act_step, 1)
                    act.activation(gap[:, :, :], gap[:, :, :], ACT.Exp).then_inc(act_step, 1)

            @block.vector
            def _(dve):
                count = [0]

                def chain(op):
                    count[0] += 1
                    op.then_inc(step, 1)

                def chained():
                    dve.wait_ge(step, count[0])

                def chunk(k, par):
                    dve.wait_ge(turned, k + 1)
                    dve.tensor_copy(L[:, span(k * TPC, TPC), :], bank_t[:, par, :, 0:EX]).then_inc(L_ready, 1)
                in_pairs(dve, NC, chunk)
                dve.wait_ge(L_ready, NC)
                dve.wait_ge(prepared, 3)
                if sigmoid_gate:
                    dve.wait_ge(act_step, 1)
                    chain(dve.tensor_scalar(e1[:, :, :], e1[:, :, :], 1.0, None, ALU.add))
                    chained()
                    chain(dve.reciprocal(vals[:, :, 0:E], e1[:, :, 0:E]))
                else:
                    chain(dve.tensor_copy(vals[:, :, 0:E], L[:, :, 0:E]))
                chained()
                for t in range(T):
                    dve.max(best[:, t, :], vals[:, t, 0:E]).then_inc(best_done, 1)
                dve.wait_ge(best_done, T)
                dve.tensor_copy(found[:, :, 0:2], best[:, :, 0:2]).then_inc(best_done, 1)
                dve.wait_ge(best_done, T + 1)
                for t in range(T):
                    dve.match_replace(marked[:, t, :], found[:, t, :], vals[:, t, :], HIT).then_inc(marked_done, 1)
                if sigmoid_gate:
                    chain(dve.tensor_tensor(den[:, :, :], best[:, :, 0:1], best[:, :, 1:2], ALU.add))
                    numerators = vals[:, :, 0:E]
                else:
                    chain(dve.tensor_tensor(e1[:, :, 0:E], L[:, :, 0:E], best[:, :, 0:1].broadcast_to([P, T, E]),
                                            ALU.subtract))
                    chain(dve.tensor_tensor(gap[:, :, :], best[:, :, 1:2], best[:, :, 0:1], ALU.subtract))
                    dve.wait_ge(act_step, 3)
                    chain(dve.tensor_scalar(den[:, :, :], gap[:, :, :], 1.0, None, ALU.add))
                    numerators = e1[:, :, 0:E]
                chained()
                chain(dve.reciprocal(den[:, :, :], den[:, :, :]))
                dve.wait_ge(marked_done, T)
                chain(dve.scalar_tensor_tensor(out=marked[:, :, 0:E], in0=marked[:, :, 0:E], scalar=HIT,
                                               in1=numerators, op0=ALU.is_equal, op1=ALU.mult))
                chained()
                for at in (0, 32):
                    dve.tensor_tensor(C[:, :, at:at + E], marked[:, :, 0:E], den[:, :, 0:1].broadcast_to([P, T, E]),
                                      ALU.mult).then_inc(comb_ready, 1)
                if shared_gate:
                    chain(dve.tensor_scalar(e1[:, :, E:EX], e1[:, :, E:EX], 1.0, None, ALU.add))
                    chained()
                    chain(dve.reciprocal(e1[:, :, E:EX], e1[:, :, E:EX]))
                    chained()
                    dve.tensor_copy(C[:, :, 0:64].rearrange("p t (a e) -> p t a e", a=2)[:, :, :, E:EX],
                                    cols(e1[:, :, E:EX], 2, 2)).then_inc(comb_ready, 1)
                for k in range(NC):
                    dve.wait_ge(c_turned, k + 1)
                    out = combT[:, span(k * CH, CH)]
                    dve.tensor_copy(out, bank_c[:, k % 2, :]).then_inc(c_hi, 1)
                    dve.wait_ge(c_hi, k + 1)
                    dve.tensor_tensor(out[32:64], bank_c[32:64, k % 2, :], f32(out)[32:64], ALU.subtract).then_inc(c_lo, 1)


def gated_ffn(nc, name, xnT, blocks, x, ident, combT=None, out_bias=None, out_scale=1.0):
    F = len(blocks)
    weighted = [f for f in range(F) if blocks[f][6] is not None]
    NW = len(weighted)
    with phase(nc, name) as m:
        Xh, Xl = m.sb("Xh", [P, 2, CH], F32R), m.sb("Xl", [P, 2, CH], F32R)
        sg, hm, h = m.sb("sg", [P, 2, CH]), m.sb("hm", [P, 2, CH]), m.sb("h", [P, 2, CH])
        y = m.sb("y", [P, 2, CH])
        ps_g, ps_u, ps_w = m.ps("ps_g", [P, 2, CH]), m.ps("ps_u", [P, 2, CH]), m.ps("ps_w", [P, CH])
        ps_o, ps_t = m.ps("ps_o", [P, 2, CH]), m.ps("ps_t", [P, TPC, D])
        xh_ready, x_ready = m.sem("xh_ready"), m.sem("x_ready")
        g_done, u_done, w_done, down_done = m.sem("g_done"), m.sem("u_done"), m.sem("w_done"), m.sem("down_done")
        sg_ready, hm_ready, h_ready = m.sem("sg_ready"), m.sem("hm_ready"), m.sem("h_ready")
        y_ready, turned, added = m.sem("y_ready"), m.sem("turned"), m.sem("added")

        def slot(f, par):
            return (par * F + f) % 2

        with nc.Block() as block:
            @block.tensor
            def _(pe):
                def gates(k, par, f):
                    gh, gl, uh, ul, _, r, spread, _, _ = blocks[f]
                    b = slot(f, par)
                    n = k * F + f
                    if f == 0:
                        pe.wait_ge(x_ready, k + 1)
                    after(pe, sg_ready, n - 1)
                    for w, xs, start in ((gh, Xh, True), (gl, Xh, False), (gh, Xl, False)):
                        op = pe.matmul(ps_g[0:r, b, :], w, xs[:, par, :], start=start, stop=not start and xs is Xl)
                    op.then_inc(g_done, 1)
                    after(pe, hm_ready, n - 1)
                    for w, xs, start in ((uh, Xh, True), (ul, Xh, False), (uh, Xl, False)):
                        op = pe.matmul(ps_u[0:r, b, :], w, xs[:, par, :], start=start, stop=not start and xs is Xl)
                    op.then_inc(u_done, 1)
                    if spread is not None:
                        if f == weighted[0]:
                            after(pe, h_ready, (k - 1) * F + weighted[-1] + 1)
                        else:
                            after(pe, h_ready, n)
                        pe.matmul(ps_w[0:r, :], spread[:, 0:r], combT[:, span(k * CH, CH)], start=True, stop=True)\
                          .then_inc(w_done, 1)

                def down(k, par, f):
                    _, _, _, _, wd, r, _, _, _ = blocks[f]
                    if f == 0:
                        after(pe, y_ready, k - 1)
                    pe.wait_ge(h_ready, k * F + f + 1)
                    pe.matmul(ps_o[:, par, :], wd, h[0:r, slot(f, par), :], start=f == 0, stop=f == F - 1)\
                      .then_inc(down_done, 1)

                def turn(k, par):
                    pe.wait_ge(y_ready, k + 1)
                    after(pe, added, k)
                    for i in range(TPC):
                        op = pe.transpose(ps_t[:, i, :], y[:, par, P * i:P * i + P], ident[:, :])
                    op.then_inc(turned, 1)

                def chunk(k, par):
                    for f in range(F):
                        gates(k, par, f)
                        if f > 0:
                            down(k, par, f - 1)
                        if f == 1 and not (isinstance(k, int) and k == 0):
                            turn(k - 1, 1 - par)
                    down(k, par, F - 1)
                in_pairs(pe, NC, chunk)
                turn(NC - 1, 1)

            @block.scalar
            def _(act):
                def chunk(k, par):
                    for f in range(F):
                        r, bg = blocks[f][5], blocks[f][7]
                        b = slot(f, par)
                        act.wait_ge(g_done, k * F + f + 1)
                        after(act, hm_ready, k * F + f - 1)
                        if bg is None:
                            op = act.activation(sg[0:r, b, :], ps_g[0:r, b, :], ACT.Silu)
                        else:
                            op = act.activation(sg[0:r, b, :], ps_g[0:r, b, :], ACT.Silu, bias=bg)
                        op.then_inc(sg_ready, 1)
                        if f == 0 and not (isinstance(k, int) and k == 0):
                            finish(k - 1, 1 - par)

                def finish(k, par):
                    act.wait_ge(down_done, (k + 1) * F)
                    after(act, turned, k - 1)
                    if out_bias is None:
                        op = act.activation(y[:, par, :], ps_o[:, par, :], ACT.Copy)
                    else:
                        op = act.activation(y[:, par, :], ps_o[:, par, :], ACT.Identity, bias=out_bias[:, 0:1])
                    op.then_inc(y_ready, 1)
                in_pairs(act, NC, chunk)
                finish(NC - 1, 1)

            @block.vector
            def _(dve):
                def halves(k, par):
                    after(dve, u_done, (k - 1) * F)
                    src = xnT[:, span(k * CH, CH)]
                    dve.tensor_copy(Xh[:, par, :], src).then_inc(xh_ready, 1)
                    dve.wait_ge(xh_ready, k + 1)
                    dve.tensor_tensor(Xl[:, par, :], src, f32(Xh[:, par, :]), ALU.subtract).then_inc(x_ready, 1)

                def weight(k, par, f):
                    r, b, n = blocks[f][5], slot(f, par), k * F + f
                    dve.wait_ge(hm_ready, n + 1)
                    if blocks[f][6] is not None:
                        dve.wait_ge(w_done, k * NW + weighted.index(f) + 1)
                        after(dve, down_done, n - 1)
                        dve.tensor_tensor(h[0:r, b, :], hm[0:r, b, :], ps_w[0:r, :], ALU.mult).then_inc(h_ready, 1)

                def chunk(k, par):
                    for f in range(F):
                        r, bu, b, n = blocks[f][5], blocks[f][8], slot(f, par), k * F + f
                        dve.wait_ge(sg_ready, n + 1)
                        dve.wait_ge(u_done, n + 1)
                        plain = blocks[f][6] is None
                        if plain:
                            after(dve, down_done, n - 1)
                        dst = (h if plain else hm)[0:r, b, :]
                        if bu is None:
                            op = dve.tensor_tensor(dst, sg[0:r, b, :], ps_u[0:r, b, :], ALU.mult)
                        else:
                            op = dve.scalar_tensor_tensor(out=dst, in0=ps_u[0:r, b, :], scalar=bu,
                                                          in1=sg[0:r, b, :], op0=ALU.add, op1=ALU.mult)
                        op.then_inc(hm_ready, 1)
                        if plain:
                            dve.wait_ge(hm_ready, n + 1)
                            dve.sem_inc(h_ready, 1)
                        else:
                            weight(k, par, f)
                        if f == 2 and not (isinstance(k, int) and k == 0):
                            add(k - 1)
                    if not (isinstance(k, int) and k + 1 >= NC):
                        halves(k + 1, 1 - par)

                def add(k):
                    dve.wait_ge(turned, k + 1)
                    xs = x[:, span(k * TPC, TPC), :]
                    dve.scalar_tensor_tensor(out=xs, in0=ps_t[:, :, :], scalar=out_scale, in1=xs,
                                             op0=ALU.mult, op1=ALU.add).then_inc(added, 1)
                halves(0, 0)
                in_pairs(dve, NC, chunk)
                add(NC - 1)


def linear_attention(nc, name, xn, xnT, x1, Wq, Wkv, bq, bkv_all):
    with phase(nc, name) as m:
        tT = m.sb("tT", [P, 2, P])
        qa, qb, qe, qp = (m.sb(s, [P, 2, P]) for s in ("qa", "qb", "qe", "qp"))
        kv = m.sb("kv", [P, 2, 2 * D + 1])
        ka, ke, kp = (m.sb(s, [P, 2, D]) for s in ("ka", "ke", "kp"))
        state = m.sb("state", [P, 2, 2, D + 1])
        den = m.sb("den", [P, 2, 1])
        ps_q, ps_kv = m.ps("ps_q", [P, 2, 512]), m.ps("ps_kv", [P, 2, 512])
        ps_s, ps_n = m.ps("ps_s", [P, 2, 512]), m.ps("ps_n", [P, 2, 512])
        set_up, tT_ready, qkv_done = m.sem("set_up"), m.sem("tT_ready"), m.sem("qkv_done")
        q_min, q_max, kv_read, k_min = m.sem("q_min"), m.sem("q_max"), m.sem("kv_read"), m.sem("k_min")
        exp_done, features, state_done = m.sem("exp_done"), m.sem("features"), m.sem("state_done")
        state_ready, num_done, den_step, x1_ready = (m.sem("state_ready"), m.sem("num_done"), m.sem("den_step"),
                                                     m.sem("x1_ready"))
        with nc.Block() as block:
            @block.gpsimd
            def _(pool):
                pool.memset(kv[:, :, 2 * D:], 1.0).then_inc(set_up, 1)

                def tile(t, par):
                    after(pool, qkv_done, t - 1)
                    pool.wait_ge(set_up, 1)
                    pool.tensor_copy(tT[:, par, :], xnT[:, span(t * P, P)]).then_inc(tT_ready, 1)
                in_pairs(pool, T, tile)

            @block.tensor
            def _(pe):
                def project(t, par):
                    pe.wait_ge(tT_ready, t + 1)
                    after(pe, q_max, t - 1)
                    after(pe, kv_read, t - 1)
                    pe.matmul(ps_q[:, par, 0:P], Wq, tT[:, par, :], start=True, stop=True)
                    pe.matmul(ps_kv[:, par, 0:2 * D], tT[:, par, :], Wkv, start=True, stop=True).then_inc(qkv_done, 1)

                def tile(t, par):
                    if not (isinstance(t, int) and t + 1 >= T):
                        project(t + 1, 1 - par)
                    pe.wait_ge(features, t + 1)
                    after(pe, state_ready, t)
                    for s in range(2):
                        rows = slice(S * s, S * s + S)
                        op = pe.matmul(ps_s[:, s, 0:D + 1], kp[rows, par, :], kv[rows, par, D:], start=True, stop=True)
                    op.then_inc(state_done, 1)
                    pe.wait_ge(state_ready, t + 1)
                    after(pe, x1_ready, t - 1)
                    for s in range(2):
                        op = pe.matmul(ps_n[S * s:S * s + S, par, 0:D + 1], qp[:, par, S * s:S * s + S],
                                       state[:, par, s, :], start=True, stop=True)
                    op.then_inc(num_done, 1)
                pe.wait_ge(set_up, 1)
                project(0, 0)
                in_pairs(pe, T, tile)

            @block.scalar
            def _(act):
                def tile(t, par):
                    act.wait_ge(q_min, t + 1)
                    after(act, features, t - 1)
                    act.activation(qe[:, par, :], qa[:, par, :], ACT.Exp).then_inc(exp_done, 1)
                    act.wait_ge(k_min, t + 1)
                    act.activation(ke[:, par, :], ka[:, par, :], ACT.Exp).then_inc(exp_done, 1)
                    act.wait_ge(state_done, t + 1)
                    after(act, num_done, t - 1)
                    act.activation(state[:, par, :, :], ps_s[:, :, 0:D + 1], ACT.Copy).then_inc(state_ready, 1)
                in_pairs(act, T, tile)

            @block.vector
            def _(dve):
                def inputs(t, par):
                    dve.wait_ge(qkv_done, t + 1)
                    after(dve, num_done, t - 1)
                    after(dve, exp_done, 2 * (t - 1))
                    dve.tensor_tensor(kv[:, par, 0:2 * D], ps_kv[:, par, 0:2 * D], bkv_all[:, :], ALU.add)\
                       .then_inc(kv_read, 1)
                    dve.tensor_scalar(qa[:, par, :], ps_q[:, par, 0:P], bq[:, 0:1], 0.0, ALU.add, ALU.min)\
                       .then_inc(q_min, 1)
                    dve.tensor_scalar(qb[:, par, :], ps_q[:, par, 0:P], bq[:, 0:1], 0.0, ALU.add, ALU.max)\
                       .then_inc(q_max, 1)
                    dve.wait_ge(kv_read, t + 1)
                    dve.tensor_scalar(ka[:, par, :], kv[:, par, 0:D], 0.0, None, ALU.min).then_inc(k_min, 1)

                def feature_maps(t, par):
                    dve.wait_ge(q_max, t + 1)
                    dve.wait_ge(exp_done, 2 * t + 2)
                    dve.tensor_tensor(qp[:, par, :], qb[:, par, :], qe[:, par, :], ALU.add)
                    dve.scalar_tensor_tensor(out=kp[:, par, :], in0=kv[:, par, 0:D], scalar=0.0, in1=ke[:, par, :],
                                             op0=ALU.max, op1=ALU.add).then_inc(features, 1)

                def divide(t, par):
                    dve.wait_ge(num_done, t + 1)
                    dve.tensor_scalar(den[:, par, :], ps_n[:, par, D:D + 1], 1e-6, None, ALU.add).then_inc(den_step, 1)
                    dve.wait_ge(den_step, 2 * t + 1)
                    dve.reciprocal(den[:, par, :], den[:, par, :]).then_inc(den_step, 1)
                    dve.wait_ge(den_step, 2 * t + 2)
                    dve.scalar_tensor_tensor(out=x1[:, t, :], in0=ps_n[:, par, 0:D], scalar=den[:, par, 0:1],
                                             in1=xn[:, t, :], op0=ALU.mult, op1=ALU.add).then_inc(x1_ready, 1)

                def tile(t, par):
                    feature_maps(t, par)
                    if not (isinstance(t, int) and t + 1 >= T):
                        inputs(t + 1, 1 - par)
                    divide(t, par)
                dve.wait_ge(set_up, 1)
                inputs(0, 0)
                in_pairs(dve, T, tile)


def centre(nc, name, xnT, hi, lo):
    with phase(nc, name) as m:
        mean = m.sb("mean", [P, B])
        y = m.sb("y", [P, 2, CH])
        per = CH // S
        step, summed, y_ready, hi_ready, lo_ready = (m.sem("step"), m.sem("summed"), m.sem("y_ready"),
                                                     m.sem("hi_ready"), m.sem("lo_ready"))
        with nc.Block() as block:
            @block.vector
            def _(dve):
                for k in range(NC):
                    dve.tensor_reduce(mean[:, span(k * per, per)],
                                      xnT[:, span(k * CH, CH)].rearrange("p (b s) -> p b s", s=S),
                                      AX.X, ALU.add).then_inc(summed, 1)
                dve.wait_ge(summed, NC)
                dve.tensor_scalar(mean[:, :], mean[:, :], 1.0 / S, None, ALU.mult).then_inc(step, 1)
                dve.wait_ge(step, 1)
                for k in range(NC):
                    after(dve, lo_ready, k - 1)
                    yk = y[:, k % 2, :]
                    dve.tensor_tensor(yk.rearrange("p (b s) -> p b s", s=S),
                                      xnT[:, span(k * CH, CH)].rearrange("p (b s) -> p b s", s=S),
                                      cols(mean[:, span(k * per, per)], 2, S), ALU.subtract).then_inc(y_ready, 1)
                    dve.wait_ge(y_ready, k + 1)
                    dve.tensor_copy(hi[:, span(k * CH, CH)], yk).then_inc(hi_ready, 1)
                    dve.wait_ge(hi_ready, k + 1)
                    dve.tensor_tensor(lo[:, span(k * CH, CH)], yk, f32(hi[:, span(k * CH, CH)]), ALU.subtract)\
                       .then_inc(lo_ready, 1)


def store(nc, name, out, x):
    with phase(nc, name) as m:
        stored = m.sem("stored")
        with nc.Block() as block:
            @block.sync
            def _(sp):
                for k in range(NC):
                    sp.dma_start(out[:, span(k * TPC, TPC), :], x[:, span(k * TPC, TPC), :]).then_inc(stored, 16)
                sp.wait_ge(stored, 16 * NC)


def cross_attention(nc, tag, a, x, con, attn_eps, den_eps, mask=None):
    with ExitStack() as stack:
        def sb(name, shape, dt=F32):
            return stack.enter_context(nc.sbuf_tensor(f"{tag}_{name}", shape, dt))

        WT = {w: sb(f"{w}T", [P, D]) for w in ("Wq", "Wk", "Wv", "Wo")}
        bq, bk, bo, bv_all = sb("bq", [P, 1]), sb("bk", [P, 1]), sb("bo", [P, 1]), sb("bv_all", [P, D])
        mask_bias = sb("mask_bias", [P, B]) if mask is not None else None
        with ExitStack() as early:
            raw = early.enter_context(nc.sbuf_tensor(f"{tag}_raw", [P, 4, D], F32))
            jobs = [(raw[:, i, :], a[f"{tag}_{w}"]) for i, w in enumerate(WT)]
            jobs += [(b[:, :], a[f"{tag}_{n}"].unsqueeze(1)) for n, b in (("bq", bq), ("bk", bk), ("bo", bo))]
            jobs += [(bv_all[:, :], a[f"{tag}_bv"].unsqueeze(0).broadcast_to([P, D]))]
            turns = [(t[:, :], raw[:, i, :]) for i, t in enumerate(WT.values())]
            if mask is not None:
                keep8 = early.enter_context(nc.sbuf_tensor(f"{tag}_keep8", [B, SK], U8))
                keep = early.enter_context(nc.sbuf_tensor(f"{tag}_keep", [B, SK], F32))
                jobs += [(keep8[:, :], mask)]
                turns += [(mask_bias[:, :], keep[:, :])]
            load(nc, f"{tag}_load", jobs)
            if mask is not None:
                elementwise(nc, f"{tag}_keep_bias", lambda dve: dve.tensor_scalar(
                    keep[:, :], keep8[:, :], -MASKED, MASKED, ALU.mult, ALU.add))
            transpose_all(nc, f"{tag}_turn", turns, con["ident"])
        xnT = sb("xnT", [P, B * S])
        layernorm(nc, f"{tag}_ln", x, 1e-5, con["ident"], xnT=xnT)
        Kh, Kl = sb("Kh", [P, B * SK], F32R), sb("Kl", [P, B * SK], F32R)
        V = sb("V", [P, B, D])
        keys_values(nc, f"{tag}_kv", a["ctx_1024"], Kh, Kl, V, WT["Wk"], WT["Wv"], bk, bv_all, con["ident"], mask)
        Qh, Ql = sb("Qh", [P, B * S], F32R), sb("Ql", [P, B * S], F32R)
        queries(nc, f"{tag}_q", xnT, Qh, Ql, WT["Wq"], bq)
        attention(nc, f"{tag}_att", Kh, Kl, V, Qh, Ql, xnT, con, SK, float(DH) ** -0.5, den_eps, mask, mask_bias)
        project_add(nc, f"{tag}_out", xnT, x, con["ident"], WT["Wo"], bo)


def elementwise(nc, name, op):
    with nc.Block() as block:
        @block.vector
        def _(dve):
            op(dve)


def linear_block(nc, a, x, con):
    pre = "L0_attn_"
    with ExitStack() as stack:
        def sb(name, shape, dt=F32):
            return stack.enter_context(nc.sbuf_tensor(f"la_{name}", shape, dt))

        rows = [P, P, L0_H - 2 * P]
        Wqkv = sb("Wqkv", [P, 3 * D])
        Wg, Wu, Wd = sb("Wg", [P, L0_H]), sb("Wu", [P, L0_H]), sb("Wd", [P, 3, D])
        gh, gl, uh, ul = (sb(n, [P, L0_H], F32R) for n in ("gh", "gl", "uh", "ul"))
        bq, bkv_all = sb("bq", [P, 1]), sb("bkv_all", [P, 2 * D])
        bg, bu, bd = sb("bg", [P, 3]), sb("bu", [P, 3]), sb("bd", [P, 1])
        vecs = {n: sb(n, [P, D]) for n in ("g1", "b1", "g2", "b2")}
        jobs = [(Wqkv[:, :], a[pre + "Wqkv"]), (Wg[:, :], a[pre + "Wg"]), (Wu[:, :], a[pre + "Wu"]),
                (bq[:, :], a[pre + "bqkv"][0:D].unsqueeze(1)),
                (bkv_all[:, :], a[pre + "bqkv"][D:3 * D].unsqueeze(0).broadcast_to([P, 2 * D])),
                (bd[:, :], a[pre + "bd"].unsqueeze(1))]
        for i, r in enumerate(rows):
            at = slice(P * i, P * i + r)
            jobs += [(Wd[0:r, i, :], a[pre + "Wd"][at, :]), (bg[0:r, i:i + 1], a[pre + "bg"][at].unsqueeze(1)),
                     (bu[0:r, i:i + 1], a[pre + "bu"][at].unsqueeze(1))]
        jobs += [(v[:, :], a[pre + n].unsqueeze(0).broadcast_to([P, D])) for n, v in vecs.items()]
        load(nc, "la_load", jobs)
        split(nc, "la_split", [(gh[:, :], gl[:, :], Wg[:, :]), (uh[:, :], ul[:, :], Wu[:, :])])
        xn, xnT, x1 = sb("xn", [P, T, D]), sb("xnT", [P, B * S]), sb("x1", [P, T, D])
        layernorm(nc, "la_ln", x, 1e-5, con["ident"], xnT=xnT, nat=xn)
        linear_attention(nc, "la_att", xn, xnT, x1, Wqkv[:, 0:D], Wqkv[:, D:3 * D], bq, bkv_all)
        layernorm(nc, "la_ln1", x1, 1e-5, con["ident"], xnT=xnT, nat=xn, gain=vecs["g1"], shift=vecs["b1"])
        blocks = []
        for i, r in enumerate(rows):
            at = slice(P * i, P * i + r)
            blocks.append((gh[:, at], gl[:, at], uh[:, at], ul[:, at], Wd[0:r, i, :], r, None,
                           bg[0:r, i:i + 1], bu[0:r, i:i + 1]))
        gated_ffn(nc, "la_ffn", xnT, blocks, xn, con["ident"], out_bias=bd)
        layernorm(nc, "la_ln2", xn, 1e-5, con["ident"], gain=vecs["g2"], shift=vecs["b2"], add_to=x)


def moe0(nc, a, x, con):
    pre = "L0_ffn_"
    NB = L0_E * L0_F // P
    rows = [P, P, L0_SHARED - 2 * P]
    with ExitStack() as stack:
        def sb(name, shape, dt=F32):
            return stack.enter_context(nc.sbuf_tensor(f"m0_{name}", shape, dt))

        gh, gl, uh, ul = (sb(n, [P, NB + 3, P], F32R) for n in ("gh", "gl", "uh", "ul"))
        wd = sb("wd", [P, NB + 3, D])
        gateT = sb("gateT", [P, P])
        spread = sb("spread", [P, len(L0_SPREAD), P], F32R)
        with ExitStack() as early:
            def eb(name, shape, dt=F32):
                return early.enter_context(nc.sbuf_tensor(f"m0_{name}", shape, dt))

            wgu = eb("wgu", [P, L0_E, 2 * L0_F])
            raw = eb("raw", [P, 3, 2, D])
            rawd = eb("rawd", [P, L0_SHARED])
            shT = eb("shT", [P, 2, 3 * P])
            gates = eb("gates", [P, D])
            spread_raw = eb("spread_raw", [P, len(L0_SPREAD) * P])
            jobs = [(wgu[:, :, :], a[pre + "w_gate_up"].rearrange("e d f -> d e f")),
                    (wd[:, 0:NB, :], a[pre + "w_down"].rearrange("(b e) f d -> (e f) b d", e=2)
                     if False else a[pre + "w_down"].rearrange("e f d -> (e f) d").rearrange("(b r) d -> r b d", r=P)),
                    (rawd[:, :], a[pre + "shared_w_down"]),
                    (gates[0:L0_E, :], a[pre + "gate_w"]), (gates[L0_E:L0_E + 1, :], a[pre + "shared_gate_w"]),
                    (spread_raw[:, :], a["c_spread0"])]
            for i, r in enumerate(rows):
                at = slice(P * i, P * i + r)
                jobs += [(raw[0:r, i, 0, :], a[pre + "shared_w_gate"][at, :]),
                         (raw[0:r, i, 1, :], a[pre + "shared_w_up"][at, :])]
            elementwise(nc, "m0_zero", lambda dve: dve.memset(gates[:, :], 0.0))
            load(nc, "m0_load", jobs)
            turns = [(gateT[:, :], gates[:, :])]
            for i, r in enumerate(rows):
                at = slice(P * i, P * i + r)
                turns += [(shT[:, 0, at], raw[0:r, i, 0, :]), (shT[:, 1, at], raw[0:r, i, 1, :]),
                          (wd[0:r, NB + i, :], rawd[:, at])]
            transpose_all(nc, "m0_turn", turns, con["ident"])
            pick = wgu[:, :, :].rearrange("p (b e) (s f) -> p s b e f", e=2, s=2)
            jobs = []
            for b in range(NB):
                for s, (hi, lo) in enumerate(((gh, gl), (uh, ul))):
                    jobs.append((hi[:, b, :].rearrange("p (e f) -> p e f", e=2),
                                 lo[:, b, :].rearrange("p (e f) -> p e f", e=2), pick[:, s, b]))
            for s, (hi, lo) in enumerate(((gh, gl), (uh, ul))):
                flat = [v[:, NB:, :].rearrange("p b r -> p (b r)")[:, 0:L0_SHARED] for v in (hi, lo)]
                jobs.append((flat[0], flat[1], shT[:, s, 0:L0_SHARED]))
            jobs.append((spread[:, :, :].rearrange("p b r -> p (b r)"), None, spread_raw[:, :]))
            split(nc, "m0_split", jobs)
        xnT = sb("xnT", [P, B * S])
        combT = sb("combT", [P, B * S], F32R)
        layernorm(nc, "m0_ln", x, 1e-5, con["ident"], xnT=xnT)
        route(nc, "m0_route", xnT, gateT, L0_E, combT, con["ident"], False, True)
        blocks = [(gh[:, f, 0:r], gl[:, f, 0:r], uh[:, f, 0:r], ul[:, f, 0:r], wd[0:r, f, :], r, spread[:, f, :],
                   None, None) for f, r in enumerate([P] * NB + rows)]
        gated_ffn(nc, "m0_ffn", xnT, blocks, x, con["ident"], combT=combT)


def moe1(nc, a, x, con):
    pre = "L1_ffn_"
    FB = L1_F // P
    NB = L1_E * FB
    with ExitStack() as stack:
        def sb(name, shape, dt=F32):
            return stack.enter_context(nc.sbuf_tensor(f"m1_{name}", shape, dt))

        gh, gl, uh, ul = (sb(n, [P, NB + FB, P], F32R) for n in ("gh", "gl", "uh", "ul"))
        wd = sb("wd", [P, NB + FB, D])
        gateT = sb("gateT", [P, P])
        spread = sb("spread", [P, L1_E, P], F32R)
        with ExitStack() as early:
            def eb(name, shape, dt=F32):
                return early.enter_context(nc.sbuf_tensor(f"m1_{name}", shape, dt))

            raw_g, raw_u = eb("raw_g", [P, NB + FB, P]), eb("raw_u", [P, NB + FB, P])
            spread_raw = eb("spread_raw", [P, L1_E * P])
            jobs = [(gateT[:, 0:L1_E], a[pre + "Wg"]), (spread_raw[:, :], a["c_spread1"])]
            for raw, we, ws in ((raw_g, "We1", "Ws1"), (raw_u, "We3", "Ws3")):
                v = raw[:, :, :].rearrange("p (e b) r -> p e (b r)", b=FB)
                jobs += [(v[:, 0:L1_E, :], a[pre + we].rearrange("e d f -> d e f")), (v[:, L1_E, :], a[pre + ws])]
            jobs += [(wd[:, 0:NB, :], a[pre + "We2"].rearrange("e f d -> (e f) d").rearrange("(b r) d -> r b d", r=P)),
                     (wd[:, NB:, :], a[pre + "Ws2"].rearrange("(b r) d -> r b d", r=P))]
            elementwise(nc, "m1_zero", lambda dve: dve.memset(gateT[:, :], 0.0))
            load(nc, "m1_load", jobs)
            split(nc, "m1_split", [(gh[:, :, :], gl[:, :, :], raw_g[:, :, :]), (uh[:, :, :], ul[:, :, :], raw_u[:, :, :]),
                                   (spread[:, :, :].rearrange("p b r -> p (b r)"), None, spread_raw[:, :])])
        xnT = sb("xnT", [P, B * S])
        combT = sb("combT", [P, B * S], F32R)
        layernorm(nc, "m1_ln", x, 1e-5, con["ident"], xnT=xnT)
        route(nc, "m1_route", xnT, gateT, L1_E, combT, con["ident"], True, False)
        blocks = [(gh[:, f, :], gl[:, f, :], uh[:, f, :], ul[:, f, :], wd[:, f, :], P,
                   spread[:, f // FB, :] if f < NB else None, None, None) for f in range(NB + FB)]
        gated_ffn(nc, "m1_ffn", xnT, blocks, x, con["ident"], combT=combT, out_scale=1.0 / 3.0)


def self_attention(nc, x, con):
    with ExitStack() as stack:
        def sb(name, shape, dt=F32):
            return stack.enter_context(nc.sbuf_tensor(f"sa_{name}", shape, dt))

        xn, xnT, AT = sb("xn", [P, T, D]), sb("xnT", [P, B * S]), sb("AT", [P, B * S])
        hi, lo = sb("hi", [P, B * S], F32R), sb("lo", [P, B * S], F32R)
        layernorm(nc, "sa_ln", x, 1e-5, con["ident"], xnT=xnT, nat=xn)
        centre(nc, "sa_centre", xnT, hi, lo)
        attention(nc, "sa_att", hi, lo, xn, hi, lo, AT, con, S, 1.0)
        project_add(nc, "sa_out", AT, x, con["ident"])


STAGES = 6


def perceiver_kernel(nc, a, out, stages=STAGES):
    x_dram = a["x"].rearrange("b s d -> (b s) d").rearrange("(t p) d -> p t d", p=P)
    out_dram = out.rearrange("b s d -> (b s) d").rearrange("(t p) d -> p t d", p=P)
    with ExitStack() as stack:
        def sb(name, shape, dt=F32):
            return stack.enter_context(nc.sbuf_tensor(name, shape, dt))

        x = sb("x", [P, T, D])
        ident = sb("ident", [P, P])
        mask4 = sb("mask4", [P, J])
        sel, selm = sb("sel", [P, G, 4, P], F32R), sb("selm", [64, PAIRS, P], F32R)
        with nc.sbuf_tensor("sel_raw", [P, G * 4 * P], F32) as sel_raw, \
                nc.sbuf_tensor("selm_raw", [64, PAIRS * P], F32) as selm_raw:
            load(nc, "first", [(x[:, :, :], x_dram), (ident[:, :], a["c_ident"]), (mask4[:, :], a["c_mask4"]),
                               (sel_raw[:, :], a["c_sel"]), (selm_raw[:, :], a["c_selm"])])
            split(nc, "sels", [(sel[:, :, :, :].rearrange("p a b c -> p (a b c)"), None, sel_raw[:, :]),
                               (selm[:, :, :].rearrange("p a b -> p (a b)"), None, selm_raw[:, :])])
        con = {"ident": ident, "sel": sel, "selm": selm, "mask4": mask4}
        steps = [lambda: cross_attention(nc, "L0_xattn", a, x, con, None, 1e-9),
                 lambda: linear_block(nc, a, x, con),
                 lambda: moe0(nc, a, x, con),
                 lambda: cross_attention(nc, "L1_xattn", a, x, con, None, None, a["mask_BxS2_bf1"]),
                 lambda: self_attention(nc, x, con),
                 lambda: moe1(nc, a, x, con)]
        for step in steps[:stages]:
            step()
        store(nc, "last", out_dram, x)


_INS = ['x', 'ctx_1024', 'mask_BxS2_bf1', 'L0_xattn_Wq', 'L0_xattn_bq', 'L0_xattn_Wk', 'L0_xattn_bk',
        'L0_xattn_Wv', 'L0_xattn_bv', 'L0_xattn_Wo', 'L0_xattn_bo', 'L0_attn_Wqkv', 'L0_attn_bqkv', 'L0_attn_Wg',
        'L0_attn_bg', 'L0_attn_Wu', 'L0_attn_bu', 'L0_attn_Wd', 'L0_attn_bd', 'L0_attn_g1', 'L0_attn_b1',
        'L0_attn_g2', 'L0_attn_b2', 'L0_ffn_gate_w', 'L0_ffn_w_gate_up', 'L0_ffn_w_down', 'L0_ffn_shared_w_gate',
        'L0_ffn_shared_w_up', 'L0_ffn_shared_w_down', 'L0_ffn_shared_gate_w', 'L1_xattn_Wq', 'L1_xattn_bq',
        'L1_xattn_Wk', 'L1_xattn_bk', 'L1_xattn_Wv', 'L1_xattn_bv', 'L1_xattn_Wo', 'L1_xattn_bo', 'L1_ffn_Wg',
        'L1_ffn_Ws1', 'L1_ffn_Ws3', 'L1_ffn_Ws2', 'L1_ffn_We1', 'L1_ffn_We3', 'L1_ffn_We2']


def kernel(**inputs):
    import numpy as _np
    import concourse.bacc as _bacc
    from concourse import mybir as _mybir
    from concourse.bass_utils import run_bass_kernel_spmd as _run

    nc = _bacc.Bacc("TRN2", target_bir_lowering=False, num_devices=1)
    sel, selm, mask4 = head_constants()
    constants = {"c_ident": _np.eye(P, dtype=_np.float32), "c_sel": sel, "c_selm": selm, "c_mask4": mask4,
                 "c_spread0": spread_constants(L0_SPREAD), "c_spread1": spread_constants(L1_SPREAD)}
    arrays, args = {}, {}
    for name in _INS:
        v = _np.ascontiguousarray(inputs[name])
        if v.dtype == _np.bool_:
            v = v.view(_np.uint8)
        arrays[f"in_{name}_dram"] = v
        args[name] = nc.dram_tensor(f"in_{name}_dram", v.shape, _mybir.dt.from_np(v.dtype), kind="ExternalInput").ap()
    for name, v in constants.items():
        arrays[f"in_{name}_dram"] = v
        args[name] = nc.dram_tensor(f"in_{name}_dram", v.shape, _mybir.dt.from_np(v.dtype), kind="ExternalInput").ap()
    out = nc.dram_tensor("out_0_dram", (B, S, D), F32, kind="ExternalOutput").ap()
    perceiver_kernel(nc, args, out)
    r = _run(nc, [arrays], core_ids=[0])
    return r.results[0]["out_0_dram"]
```

```python
from contextlib import ExitStack, contextmanager

import numpy as np

import concourse.bass as bass
from concourse import mybir

F32 = mybir.dt.float32
F32R = mybir.dt.float32r
BF16 = mybir.dt.bfloat16
U8 = mybir.dt.uint8
ALU = mybir.AluOpType
ACT = mybir.ActivationFunctionType
AX = mybir.AxisListType

P = 128
B, S, D = 64, 64, 128
SK = 128
H, DH = 16, 8
T = B * S // P
CH = 512
NC = B * S // CH
TPC = CH // P
G, J = 4, 4
W32 = J * DH
PAIRS = H // 2
MASKED = -10000.0
MASKED_UNSCALED = -28288.0


def head_constants():
    sel = np.zeros((P, G, 4, P), np.float32)
    for g in range(G):
        for which, blocks in enumerate(((0, 1), (2, 3), (0, 2), (1, 3))):
            for r in blocks:
                for a in range(W32):
                    sel[W32 * g + a, g, which, W32 * r + a] = 1.0
    selm = np.zeros((64, PAIRS, P), np.float32)
    for i in range(PAIRS):
        selm[i, i] = selm[32 + i, i] = 1.0
    mask4 = np.zeros((P, J), np.float32)
    for row in range(P):
        mask4[row, row % W32 // DH] = 1.0
    return sel.reshape(P, -1), selm.reshape(64, -1), mask4


def spread_constants(experts_of_block):
    m = np.zeros((P, len(experts_of_block), P), np.float32)
    for f, row in enumerate(experts_of_block):
        for col, e in enumerate(row):
            m[e, f, col] = m[32 + e, f, col] = 1.0
    return m.reshape(P, -1)


L0_E, L0_F, L0_SHARED = 16, 64, 352
L0_SPREAD = [[2 * f] * 64 + [2 * f + 1] * 64 for f in range(8)] + [[16] * P]
L1_E, L1_F = 8, 256
L1_SPREAD = [[e] * P for e in range(8)]
L0_H = 341


def after(eng, sem, count):
    if not isinstance(count, int) or count > 0:
        eng.wait_ge(sem, count)


def in_pairs(eng, n, step, peel=1):
    for p in range(peel):
        step(2 * p, 0)
        step(2 * p + 1, 1)
    with eng.Fori(peel, n // 2 - peel) as p:
        step(p * 2, 0)
        step(p * 2 + 1, 1)
    for p in range(n // 2 - peel, n // 2):
        step(2 * p, 0)
        step(2 * p + 1, 1)


def in_fours(eng, n, step):
    for u in range(4):
        step(u, u, u // 2)
    with eng.Fori(1, n // 4 - 1) as r:
        for i in range(4):
            step(r * 4 + i, i, r * 2 + i // 2)
    for u in range(n - 4, n):
        step(u, u % 4, u // 2)


def span(start, n):
    return slice(start, start + n) if isinstance(start, int) else bass.ds(start, n)


def cols(ap, at, n):
    ap = ap.unsqueeze(at)
    shape = list(ap.shape)
    shape[at] = n
    return ap.broadcast_to(shape)


def f32(ap):
    return ap.bitcast(F32)


class Mem:

    def __init__(self, nc, stack, name):
        self.nc, self.stack, self.name, self.sems = nc, stack, name, []

    def sb(self, name, shape, dt=F32):
        return self.stack.enter_context(self.nc.sbuf_tensor(f"{self.name}_{name}", shape, dt))

    def ps(self, name, shape, dt=F32):
        return self.stack.enter_context(self.nc.psum_tensor(f"{self.name}_{name}", shape, dt))

    def sem(self, name):
        s = self.nc.alloc_semaphore(f"{self.name}_{name}")
        self.sems.append(s)
        return s


@contextmanager
def phase(nc, name):
    with ExitStack() as stack:
        mem = Mem(nc, stack, name)
        yield mem
        nc.clear_and_free_semaphores(mem.sems)
        nc.all_engine_barrier()


def layernorm(nc, name, src, eps, ident, xnT=None, nat=None, gain=None, shift=None, add_to=None):
    with phase(nc, name) as m:
        stats = m.sb("stats", [P, T, 6])
        meanvar = m.sb("meanvar", [P, T, 2])
        ve = m.sb("ve", [P, T])
        power = m.sb("power", [P, TPC])
        rstd = m.sb("rstd", [P, T])
        shifts = m.sb("shifts", [P, T])
        work = None if nat is not None else m.sb("work", [P, 2, TPC, D])
        bank = m.ps("bank", [P, NC, CH])
        stats_done, aggr_done = m.sem("stats_done"), m.sem("aggr_done")
        power_set, ve_ready, rstd_ready = m.sem("power_set"), m.sem("ve_ready"), m.sem("rstd_ready")
        shifts_ready, normed, scaled, xn_ready = (m.sem("shifts_ready"), m.sem("normed"), m.sem("scaled"),
                                                  m.sem("xn_ready"))
        turned, added = m.sem("turned"), m.sem("added")

        def tiles(k):
            return slice(k * TPC, k * TPC + TPC)

        def xn(k):
            return nat[:, tiles(k), :] if nat is not None else work[:, k % 2]

        with nc.Block() as block:
            @block.vector
            def _(dve):
                def shift_of(k):
                    dve.wait_ge(rstd_ready, k + 1)
                    dve.scalar_tensor_tensor(out=shifts[:, tiles(k)], in0=meanvar[:, tiles(k), 0], scalar=-1.0,
                                             in1=rstd[:, tiles(k)], op0=ALU.mult, op1=ALU.mult).then_inc(shifts_ready, 1)

                def scale(k):
                    dve.wait_ge(normed, k + 1)
                    dve.tensor_tensor(xn(k), xn(k), cols(gain[:, :], 1, TPC), ALU.mult).then_inc(scaled, 1)
                    dve.wait_ge(scaled, k + 1)
                    dve.tensor_tensor(xn(k), xn(k), cols(shift[:, :], 1, TPC), ALU.add).then_inc(xn_ready, 1)
                    if add_to is not None:
                        dve.wait_ge(xn_ready, k + 1)
                        y = add_to[:, tiles(k), :]
                        dve.tensor_tensor(y, y, xn(k), ALU.add).then_inc(added, 1)

                def evacuate(k):
                    dve.wait_ge(turned, k + 1)
                    dve.tensor_copy(xnT[:, k * CH:k * CH + CH], bank[:, k, :])

                for t in range(T + 2):
                    if t < T:
                        dve.bn_stats(stats[:, t, :], src[:, t, :]).then_inc(stats_done, 1)
                    if t >= 2:
                        dve.wait_ge(stats_done, t - 1)
                        dve.bn_aggr(meanvar[:, t - 2, :], stats[:, t - 2, :]).then_inc(aggr_done, 1)
                    if t % TPC == 3 and t // TPC >= 2:
                        shift_of(t // TPC - 2)
                shift_of(NC - 2)
                for k in range(NC):
                    if k == 1:
                        shift_of(NC - 1)
                    if gain is not None:
                        scale(k)
                    if xnT is not None and k > 0:
                        evacuate(k - 1)
                if xnT is not None:
                    evacuate(NC - 1)

            @block.gpsimd
            def _(pool):
                pool.memset(power[:, :], -0.5).then_inc(power_set, 1)
                for k in range(NC):
                    pool.wait_ge(aggr_done, k * TPC + TPC)
                    pool.tensor_scalar(ve[:, tiles(k)], meanvar[:, tiles(k), 1], eps, None, ALU.add).then_inc(ve_ready, 1)
                    pool.wait_ge(ve_ready, k + 1)
                    pool.wait_ge(power_set, 1)
                    pool.tensor_tensor(rstd[:, tiles(k)], ve[:, tiles(k)], power[:, :], ALU.pow).then_inc(rstd_ready, 1)

            @block.scalar
            def _(act):
                for k in range(NC):
                    act.wait_ge(shifts_ready, k + 1)
                    if nat is None and xnT is not None:
                        after(act, turned, k - 1)
                    if nat is None and add_to is not None:
                        after(act, added, k - 1)
                    for i in range(TPC):
                        t = k * TPC + i
                        op = act.activation(xn(k)[:, i, :], src[:, t, :], ACT.Identity,
                                            scale=rstd[:, t:t + 1], bias=shifts[:, t:t + 1])
                    op.then_inc(normed, 1)

            if xnT is not None:
                @block.tensor
                def _(pe):
                    for k in range(NC):
                        pe.wait_ge(xn_ready if gain is not None else normed, k + 1)
                        for i in range(TPC):
                            op = pe.transpose(bank[:, k, P * i:P * i + P], xn(k)[:, i, :], ident[:, :])
                        op.then_inc(turned, 1)


def load(nc, name, pairs):
    with phase(nc, name) as m:
        loaded = m.sem("loaded")
        with nc.Block() as block:
            @block.sync
            def _(sp):
                for dst, src in pairs[0::2]:
                    sp.dma_start(dst, src).then_inc(loaded, 16)
                sp.wait_ge(loaded, 16 * len(pairs))

            @block.scalar
            def _(act):
                for dst, src in pairs[1::2]:
                    act.dma_start(dst, src).then_inc(loaded, 16)


def transpose_all(nc, name, jobs, ident):
    with phase(nc, name) as m:
        bank = m.ps("bank", [P, 2, TPC, P])
        turned, evacuated = m.sem("turned"), m.sem("evacuated")
        groups = [jobs[i:i + TPC] for i in range(0, len(jobs), TPC)]
        with nc.Block() as block:
            @block.tensor
            def _(pe):
                for n, group in enumerate(groups):
                    after(pe, evacuated, sum(map(len, groups[:n - 1])) if n > 1 else 0)
                    for i, (dst, src) in enumerate(group):
                        p, q = src.shape
                        op = pe.transpose(bank[0:q, n % 2, i, 0:p], src, ident[0:p, 0:p])
                    op.then_inc(turned, 1)

            @block.vector
            def _(dve):
                for n, group in enumerate(groups):
                    dve.wait_ge(turned, n + 1)
                    for i, (dst, src) in enumerate(group):
                        p, q = src.shape
                        dve.tensor_copy(dst, bank[0:q, n % 2, i, 0:p]).then_inc(evacuated, 1)


def split(nc, name, jobs):
    with phase(nc, name) as m:
        hi_done = m.sem("hi_done")
        with nc.Block() as block:
            @block.vector
            def _(dve):
                for n, (hi, lo, a) in enumerate(jobs):
                    dve.tensor_copy(hi, a).then_inc(hi_done, 1)
                for n, (hi, lo, a) in enumerate(jobs):
                    if lo is not None:
                        dve.wait_ge(hi_done, n + 1)
                        dve.tensor_tensor(lo, a, f32(hi), ALU.subtract)


def keys_values(nc, name, ctx, Kh, Kl, V, WkT, WvT, bk, bv_all, ident, mask=None):
    n = B * SK // CH
    per = CH // SK
    with phase(nc, name) as m:
        ctx_nat = m.sb("ctx_nat", [P, 2, per, D])
        ctxT = m.sb("ctxT", [P, 2, CH])
        keep = m.sb("keep", [P, 2, CH], U8)
        y = m.sb("y", [P, 2, CH])
        bank_t, bank_k, bank_v = m.ps("bank_t", [P, 2, CH]), m.ps("bank_k", [P, 2, CH]), m.ps("bank_v", [P, 2, CH])
        ctx_in = [m.sem("ctx_in0"), m.sem("ctx_in1")]
        turned, ctxT_ready, k_done, v_done = m.sem("turned"), m.sem("ctxT_ready"), m.sem("k_done"), m.sem("v_done")
        y_ready, hi_ready, lo_ready, v_stored = m.sem("y_ready"), m.sem("hi_ready"), m.sem("lo_ready"), m.sem("v_stored")
        keep_in = [m.sem("keep_in0"), m.sem("keep_in1")]
        with nc.Block() as block:
            @block.sync
            def _(sp):
                def chunk(c, par):
                    after(sp, turned, c - 1)
                    sp.dma_start(ctx_nat[:, par], ctx[span(c * per, per), :, :].rearrange("b k d -> k b d"))\
                      .then_inc(ctx_in[par], 16)
                in_pairs(sp, n, chunk)

            @block.tensor
            def _(pe):
                def turn(c, par):
                    pe.wait_ge(ctx_in[par], half(c, par) * 16)
                    after(pe, ctxT_ready, c - 1)
                    for i in range(per):
                        op = pe.transpose(bank_t[:, par, P * i:P * i + P], ctx_nat[:, par, i, :], ident[:, :])
                    op.then_inc(turned, 1)

                def chunk(c, par):
                    if not (isinstance(c, int) and c + 1 >= n):
                        turn(c + 1, 1 - par)
                    pe.wait_ge(ctxT_ready, c + 1)
                    after(pe, y_ready, c - 1)
                    pe.matmul(bank_k[:, par, :], WkT[:, :], ctxT[:, par, :], start=True, stop=True).then_inc(k_done, 1)
                    after(pe, v_stored, c - 1)
                    for i in range(per):
                        op = pe.matmul(bank_v[:, par, P * i:P * i + P], ctxT[:, par, P * i:P * i + P], WvT[:, :],
                                       start=True, stop=True)
                    op.then_inc(v_done, 1)
                turn(0, 0)
                in_pairs(pe, n, chunk)

            @block.scalar
            def _(act):
                def chunk(c, par):
                    act.wait_ge(turned, c + 1)
                    after(act, v_done, c - 1)
                    act.activation(ctxT[:, par, :], bank_t[:, par, :], ACT.Copy).then_inc(ctxT_ready, 1)
                    if not (isinstance(c, int) and c == 0):
                        high(c - 1, 1 - par)
                    if mask is not None and not (isinstance(c, int) and c + 1 >= n):
                        load_keep(c + 1, 1 - par)

                def load_keep(c, par):
                    after(act, y_ready, c - 1)
                    rows = mask[span(c * per, per), :].rearrange("b k -> (b k)").unsqueeze(0)
                    act.dma_start(keep[:, par], rows.broadcast_to([P, CH])).then_inc(keep_in[par], 16)

                def high(c, par):
                    act.wait_ge(y_ready, c + 1)
                    act.activation(Kh[:, span(c * CH, CH)], y[:, par, :], ACT.Copy).then_inc(hi_ready, 1)
                if mask is not None:
                    load_keep(0, 0)
                in_pairs(act, n, chunk)
                high(n - 1, 1)

            @block.vector
            def _(dve):
                def chunk(c, par):
                    dve.wait_ge(k_done, c + 1)
                    after(dve, hi_ready, c - 1)
                    after(dve, lo_ready, c - 1)
                    if mask is not None:
                        dve.wait_ge(keep_in[par], half(c, par) * 16)
                        dve.scalar_tensor_tensor(out=y[:, par, :], in0=bank_k[:, par, :], scalar=bk[:, 0:1],
                                                 in1=keep[:, par, :], op0=ALU.add, op1=ALU.mult).then_inc(y_ready, 1)
                    else:
                        dve.tensor_scalar(y[:, par, :], bank_k[:, par, :], bk[:, 0:1], None, ALU.add).then_inc(y_ready, 1)
                    dve.wait_ge(v_done, c + 1)
                    dve.tensor_tensor(V[:, span(c * per, per), :],
                                      bank_v[:, par, :].rearrange("p (i d) -> p i d", d=D),
                                      cols(bv_all[:, :], 1, per), ALU.add).then_inc(v_stored, 1)
                    if not (isinstance(c, int) and c == 0):
                        low(c - 1, 1 - par)

                def low(c, par):
                    dve.wait_ge(hi_ready, c + 1)
                    dve.tensor_tensor(Kl[:, span(c * CH, CH)], y[:, par, :], f32(Kh[:, span(c * CH, CH)]),
                                      ALU.subtract).then_inc(lo_ready, 1)
                in_pairs(dve, n, chunk)
                low(n - 1, 1)


def half(c, par):
    return (c - par) // 2 + 1


def queries(nc, name, xnT, Qh, Ql, WqT, bq):
    with phase(nc, name) as m:
        bank = m.ps("bank", [P, 2, CH])
        y = m.sb("y", [P, 2, CH])
        q_done, y_ready, hi_ready, lo_ready = m.sem("q_done"), m.sem("y_ready"), m.sem("hi_ready"), m.sem("lo_ready")
        with nc.Block() as block:
            @block.tensor
            def _(pe):
                def chunk(k, par):
                    after(pe, y_ready, k - 1)
                    pe.matmul(bank[:, par, :], WqT[:, :], xnT[:, span(k * CH, CH)], start=True, stop=True)\
                      .then_inc(q_done, 1)
                in_pairs(pe, NC, chunk)

            @block.scalar
            def _(act):
                def chunk(k, par):
                    act.wait_ge(q_done, k + 1)
                    after(act, lo_ready, k - 1)
                    act.activation(y[:, par, :], bank[:, par, :], ACT.Identity, bias=bq[:, 0:1]).then_inc(y_ready, 1)
                in_pairs(act, NC, chunk)

            @block.vector
            def _(dve):
                def chunk(k, par):
                    dve.wait_ge(y_ready, k + 1)
                    dve.tensor_copy(Qh[:, span(k * CH, CH)], y[:, par, :]).then_inc(hi_ready, 1)
                    dve.wait_ge(hi_ready, k + 1)
                    dve.tensor_tensor(Ql[:, span(k * CH, CH)], y[:, par, :], f32(Qh[:, span(k * CH, CH)]),
                                      ALU.subtract).then_inc(lo_ready, 1)
                in_pairs(dve, NC, chunk)


def attention(nc, name, Kh, Kl, V, Qh, Ql, AT, con, nk, scale, den_eps=None, mask=None, mask_bias=None):
    own = nk < P
    n = B
    NKD = 2 * nk
    GH = CH // NKD
    KS = G // GH
    ident, sel, selm, mask4 = con["ident"], con["sel"], con["selm"], con["mask4"]
    with phase(nc, name) as m:
        Kst = m.sb("Kst", [P, 2, G, NKD], F32R)
        Qst = m.sb("Qst", [P, 2, G, J, S], F32R)
        Pr = m.sb("Pr", [P, 2, G, J * S])
        Vb = m.sb("Vb", [P, 2, D])
        mneg = m.sb("mneg", [P, 2, P])
        mx = m.sb("mx", [P, 2, PAIRS])
        mt2 = m.sb("mt2", [64, 2, P], BF16)
        on = m.sb("on", [P, 2, J, S])
        sums = m.sb("sums", [P, 2, 2, S])
        ones = m.sb("ones", [P, W32])
        ps_m = m.ps("ps_m", [P, PAIRS, P])
        ps_s = m.ps("ps_s", [P, PAIRS, P])
        ps_k, ps_q = m.ps("ps_k", [P, GH, NKD]), m.ps("ps_q", [P, G, 2 * S])
        ps_o = m.ps("ps_o", [P, 2, J, S])
        ps_t = m.ps("ps_t", [P, P])
        k_done, q_done, k_copied, q_copied = m.sem("k_done"), m.sem("q_done"), m.sem("k_copied"), m.sem("q_copied")
        mp_done, mx_done, mneg_ready = m.sem("mp_done"), m.sem("mx_done"), m.sem("mneg_ready")
        mt_done, mt_hi, mt_ready = m.sem("mt_done"), m.sem("mt_hi"), m.sem("mt_ready")
        st_done, addm_done, exp_done = m.sem("st_done"), m.sem("addm_done"), m.sem("exp_done")
        pv_done, own_ready, summed = m.sem("pv_done"), m.sem("own_ready"), m.sem("summed")
        eps_added, inverted, at_ready = m.sem("eps_added"), m.sem("inverted"), m.sem("at_ready")
        v_copied, set_up = m.sem("v_copied"), m.sem("set_up")
        if mask is not None:
            mrow8 = m.sb("mrow8", [1, 2, P], U8)
            mrow = m.sb("mrow", [P, 2, P], BF16)
            ones_row = m.sb("ones_row", [P, P], BF16)
            mask_in, mrow_ready = [m.sem("mask_in0"), m.sem("mask_in1")], m.sem("mrow_ready")

        def keys_of(i):
            return slice(nk * (i % 2), nk * (i % 2) + nk)

        def part(i):
            return keys_of(i) if own else slice(0, P)

        def is_first(u, few=1):
            return isinstance(u, int) and u < few

        def exists(u, count=n):
            return not isinstance(u, int) or u < count

        with nc.Block() as block:
            @block.tensor
            def _(pe):
                def key_stack(e, q, step):
                    after(pe, k_copied, e * KS + step)
                    for gi in range(GH):
                        g = step * GH + gi
                        keys = span(e * NKD, NKD)
                        pe.matmul(ps_k[:, gi, :], sel[:, g, 0, :], Kh[:, keys], start=True, stop=False)
                        op = pe.matmul(ps_k[:, gi, :], sel[:, g, 1, :], Kl[:, keys], start=False, stop=True)
                    op.then_inc(k_done, 1)

                def query_stack(e):
                    after(pe, q_copied, e * 2)
                    for g in range(G):
                        tokens = span(e * 2 * S, 2 * S)
                        pe.matmul(ps_q[:, g, :], sel[:, g, 2, :], Qh[:, tokens], start=True, stop=False)
                        op = pe.matmul(ps_q[:, g, :], sel[:, g, 3, :], Ql[:, tokens], start=False, stop=True)
                    op.then_inc(q_done, 1)

                def scores_for_max(u, i, e):
                    pe.wait_ge(k_copied, e * KS + KS)
                    pe.wait_ge(q_copied, u + 1)
                    after(pe, mx_done, u)
                    if mask is not None:
                        pe.wait_ge(mrow_ready, u + 1)
                    for p in range(PAIRS):
                        q = Qst[:, i % 2, p // 2, 2 * (p % 2):2 * (p % 2) + 2, :]
                        first = p % 4 == 0
                        op = pe.matmul(ps_m[:, p, 0:nk], q, Kst[:, i // 2 % 2, p // 2, keys_of(i)],
                                       start=first or mask is None, stop=mask is None, skip_group_check=True)
                        if mask is not None and p % 4 == 3:
                            op = pe.matmul(ps_m[:, p - 3:p + 1, :], ones_row[:, :], cols(mrow[:, i % 2, :], 1, 4),
                                           start=False, stop=True, skip_group_check=True)
                    op.then_inc(mp_done, 1)

                def unit(u, i, e):
                    pe.wait_ge(mneg_ready, u + 1)
                    pe.transpose(ps_t[:, :], mneg[:, i % 2, :], ident[:, :]).then_inc(mt_done, 1)
                    after(pe, exp_done, u)
                    for g in range(G):
                        k = Kst[:, i // 2 % 2, g, :] if own else Kst[:, i // 2 % 2, g, keys_of(i)]
                        op = pe.matmul(ps_s[:, 2 * g:2 * g + 2, :], k, Qst[:, i % 2, g, :, :],
                                       start=g % 2 == 0, stop=False, skip_group_check=True)
                    op.then_inc(st_done, 1)
                    if exists(u + 1):
                        scores_for_max(u + 1, i + 1, e + i % 2)
                    pe.wait_ge(mt_ready, u + 1)
                    for p in range(PAIRS):
                        op = pe.matmul(ps_s[:, p, :], selm[:, p, :], mt2[:, i % 2, :], start=False,
                                       stop=p % 4 == 3, skip_group_check=True)
                    op.then_inc(addm_done, 1)
                    if i % 2 == 0 and exists(e + 1, n // 2):
                        query_stack(e + 1)
                        if KS == 2:
                            key_stack(e + 1, 1 - i // 2, 1)
                    if i % 2 == 1 and exists(e + 2, n // 2):
                        key_stack(e + 2, i // 2, 0)
                    if not is_first(u):
                        weigh(u - 1, i - 1, e - 1 + i % 2)

                def weigh(u, i, e):
                    pe.wait_ge(exp_done, u + 1)
                    pe.wait_ge(v_copied, e + 1 if own else u + 1)
                    vb = i // 2 % 2 if own else i % 2
                    after(pe, own_ready, u)
                    for g in range(G):
                        pe.matmul(ps_o[W32 * g:W32 * g + W32, 0, :, :], Vb[:, vb, W32 * g:W32 * g + W32],
                                  Pr[:, i % 2, g, :], start=True, stop=True)
                    for g in range(G):
                        op = pe.matmul(ps_o[W32 * g:W32 * g + W32, 1, :, :], ones[:, :], Pr[:, i % 2, g, :],
                                       start=True, stop=True)
                    op.then_inc(pv_done, 1)

                pe.wait_ge(set_up, 3 if own else 4 if mask is not None else 2)
                for step in range(KS):
                    key_stack(0, 0, step)
                query_stack(0)
                key_stack(1, 1, 0)
                scores_for_max(0, 0, 0)
                in_fours(pe, n, unit)
                weigh(n - 1, 3, n // 2 - 1)

            @block.scalar
            def _(act):
                def copy_keys(e, q, step):
                    act.wait_ge(k_done, e * KS + step + 1)
                    after(act, st_done, (e - 1) * 2)
                    act.activation(Kst[:, q, step * GH:step * GH + GH, :], ps_k[:, :, :], ACT.Copy)\
                       .then_inc(k_copied, 1)

                def spread(u, i, e):
                    act.wait_ge(q_done, e + 1)
                    after(act, st_done, u - 1)
                    for j in range(J):
                        op = act.activation(Qst[:, i % 2, :, j, :], ps_q[:, :, S * (i % 2):S * (i % 2) + S],
                                            ACT.Copy, scale=mask4[:, j:j + 1])
                    op.then_inc(q_copied, 1)

                def load_mask(u, i):
                    after(act, mrow_ready, u - 1)
                    act.dma_start(mrow8[:, i % 2], mask[span(u, 1), :]).then_inc(mask_in[i % 2], 16)

                def unit(u, i, e):
                    if mask is not None and exists(u + 3):
                        load_mask(u + 3, i + 3)
                    if i % 2 == 1 and exists(u + 2):
                        spread(u + 2, i + 2, e + 1)
                    act.wait_ge(addm_done, u + 1)
                    after(act, pv_done, u - 1)
                    k = part(i)
                    out, src = Pr[k, i % 2], ps_s[k, :, :]
                    if mask_bias is not None:
                        act.activation(out, src, ACT.Exp, scale=scale, bias=mask_bias[:, span(u, 1)]).then_inc(exp_done, 1)
                    else:
                        act.activation(out, src, ACT.Exp, scale=scale).then_inc(exp_done, 1)
                    if i % 2 == 0 and exists(u + 2):
                        spread(u + 2, i + 2, e + 1)
                    if KS == 2 and i % 2 == 0 and exists(e + 1, n // 2):
                        copy_keys(e + 1, 1 - i // 2, 1)
                    if i % 2 == 1 and exists(e + 2, n // 2):
                        copy_keys(e + 2, i // 2, 0)

                if own:
                    act.wait_ge(set_up, 3)
                if mask is not None:
                    for u in range(3):
                        load_mask(u, u)
                for step in range(KS):
                    copy_keys(0, 0, step)
                spread(0, 0, 0)
                copy_keys(1, 1, 0)
                spread(1, 1, 0)
                in_fours(act, n, unit)

            @block.gpsimd
            def _(pool):
                pool.memset(ones[:, :], 1.0).then_inc(set_up, 1)
                pool.memset(mneg[:, :, :], 0.0).then_inc(set_up, 1)
                if own:
                    pool.memset(Pr[:, :, :, :], 0.0).then_inc(set_up, 1)
                if mask is not None:
                    pool.memset(ones_row[:, :], 1.0).then_inc(set_up, 1)
                    pool.memset(mrow[:, :, :], 0.0).then_inc(set_up, 1)

                def values(u, i, e):
                    if own and i % 2 == 0:
                        after(pool, pv_done, u - 2)
                        pool.tensor_copy(Vb[:, i // 2, :], V[:, e, :]).then_inc(v_copied, 1)
                    if not own:
                        after(pool, pv_done, u - 1)
                        pool.tensor_copy(Vb[:, i % 2, :], V[:, u, :]).then_inc(v_copied, 1)
                in_fours(pool, n, values)

            @block.vector
            def _(dve):
                def mask_row(u, i):
                    dve.wait_ge(mask_in[i % 2], half(u, i % 2) * 16)
                    after(dve, mp_done, u - 1)
                    dve.tensor_scalar(mrow[0:1, i % 2], mrow8[:, i % 2], -MASKED_UNSCALED, MASKED_UNSCALED,
                                      ALU.mult, ALU.add).then_inc(mrow_ready, 1)

                def maxima(u, i):
                    dve.wait_ge(mp_done, u + 1)
                    dve.tensor_reduce(mx[:, i % 2], ps_m[:, :, 0:nk], AX.X, ALU.max).then_inc(mx_done, 1)

                def negate(u, i):
                    dve.wait_ge(mx_done, u + 1)
                    after(dve, mt_done, u - 1)
                    dve.tensor_scalar(mneg[:, i % 2, 0:64].rearrange("p (a b) -> p a b", a=2)[:, :, 0:PAIRS],
                                      cols(mx[:, i % 2], 1, 2), -1.0, None, ALU.mult).then_inc(mneg_ready, 1)

                def minus_max_hi(u, i):
                    dve.wait_ge(mt_done, u + 1)
                    after(dve, addm_done, u - 1)
                    dve.tensor_copy(mt2[:, i % 2], ps_t[0:64, :]).then_inc(mt_hi, 1)

                def minus_max_lo(u, i):
                    dve.wait_ge(mt_hi, u + 1)
                    dve.tensor_tensor(mt2[32:64, i % 2], ps_t[32:64, :], mt2[32:64, i % 2], ALU.subtract)\
                       .then_inc(mt_ready, 1)

                def own_heads(u):
                    dve.wait_ge(pv_done, u + 1)
                    after(dve, summed, u)
                    dve.tensor_tensor(on[:, :], ps_o[:, :], cols(cols(mask4[:, :], 2, S), 1, 2), ALU.mult)\
                       .then_inc(own_ready, 1)

                def add_heads(u, i):
                    dve.wait_ge(own_ready, u + 1)
                    dve.tensor_reduce(sums[:, i % 2], on[:, :].rearrange("p a j q -> p a q j"), AX.X, ALU.add)\
                       .then_inc(summed, 1)

                def add_eps(u, i):
                    dve.wait_ge(summed, u + 1)
                    d = sums[:, i % 2, 1]
                    if den_eps is not None:
                        dve.tensor_scalar(d, d, den_eps, None, ALU.add).then_inc(eps_added, 1)

                def invert(u, i):
                    if den_eps is not None:
                        dve.wait_ge(eps_added, u + 1)
                    dve.reciprocal(sums[:, i % 2, 1], sums[:, i % 2, 1]).then_inc(inverted, 1)

                def outputs(u, i):
                    dve.wait_ge(inverted, u + 1)
                    dve.tensor_tensor(AT[:, span(u * S, S)], sums[:, i % 2, 0], sums[:, i % 2, 1], ALU.mult)\
                       .then_inc(at_ready, 1)

                def unit(u, i, e):
                    past = not is_first(u, 2)
                    minus_max_hi(u, i)
                    if past:
                        own_heads(u - 2)
                    minus_max_lo(u, i)
                    if past:
                        add_heads(u - 2, i)
                    if mask is not None and exists(u + 2):
                        mask_row(u + 2, i)
                    if exists(u + 1):
                        maxima(u + 1, i + 1)
                    if past:
                        add_eps(u - 2, i)
                    if exists(u + 1):
                        negate(u + 1, i + 1)
                    if past:
                        invert(u - 2, i)
                        outputs(u - 2, i)

                dve.wait_ge(set_up, 4 if mask is not None else 2)
                if mask is not None:
                    mask_row(0, 0)
                    mask_row(1, 1)
                maxima(0, 0)
                negate(0, 0)
                in_fours(dve, n, unit)
                for u in (n - 2, n - 1):
                    own_heads(u)
                    add_heads(u, u)
                    add_eps(u, u)
                    invert(u, u)
                    outputs(u, u)


def project_add(nc, name, AT, x, ident, WT=None, bias=None):
    with phase(nc, name) as m:
        bank, bank_t = m.ps("bank", [P, 2, CH]), m.ps("bank_t", [P, 2, TPC, D])
        y = m.sb("y", [P, 2, CH])
        projected, y_ready, turned, added = m.sem("projected"), m.sem("y_ready"), m.sem("turned"), m.sem("added")
        with nc.Block() as block:
            @block.tensor
            def _(pe):
                def chunk(k, par):
                    if WT is not None:
                        after(pe, y_ready, k - 1)
                        pe.matmul(bank[:, par, :], WT[:, :], AT[:, span(k * CH, CH)], start=True, stop=True)\
                          .then_inc(projected, 1)
                    pe.wait_ge(y_ready, k + 1)
                    after(pe, added, k - 1)
                    for i in range(TPC):
                        op = pe.transpose(bank_t[:, par, i, :], y[:, par, P * i:P * i + P], ident[:, :])
                    op.then_inc(turned, 1)
                in_pairs(pe, NC, chunk)

            @block.scalar
            def _(act):
                def chunk(k, par):
                    after(act, turned, k - 1)
                    if WT is not None:
                        act.wait_ge(projected, k + 1)
                        act.activation(y[:, par, :], bank[:, par, :], ACT.Identity, bias=bias[:, 0:1]).then_inc(y_ready, 1)
                    else:
                        act.activation(y[:, par, :], AT[:, span(k * CH, CH)], ACT.Copy).then_inc(y_ready, 1)
                in_pairs(act, NC, chunk)

            @block.vector
            def _(dve):
                def chunk(k, par):
                    dve.wait_ge(turned, k + 1)
                    xs = x[:, span(k * TPC, TPC), :]
                    dve.tensor_tensor(xs, xs, bank_t[:, par], ALU.add).then_inc(added, 1)
                in_pairs(dve, NC, chunk)


def route(nc, name, xnT, gateT, E, combT, ident, sigmoid_gate, shared_gate):
    EX = E + 1 if shared_gate else E
    LOW, HIT = -3.0e38, 3.2e38
    with phase(nc, name) as m:
        bank, bank_t = m.ps("bank", [P, 2, CH]), m.ps("bank_t", [P, 2, TPC, P])
        bank_c = m.ps("bank_c", [P, 2, CH])
        lT = m.sb("lT", [P, 2, CH])
        L = m.sb("L", [P, T, EX])
        vals = m.sb("vals", [P, T, E + 8])
        best = m.sb("best", [P, T, 8])
        found = m.sb("found", [P, T, 8])
        marked = m.sb("marked", [P, T, E + 8])
        e1 = m.sb("e1", [P, T, EX])
        gap = m.sb("gap", [P, T, 1])
        den = m.sb("den", [P, T, 1])
        C = m.sb("C", [P, T, P])
        logits_done, lT_ready, turned, L_ready = m.sem("logits_done"), m.sem("lT_ready"), m.sem("turned"), m.sem("L_ready")
        step, act_step, best_done, marked_done = m.sem("step"), m.sem("act_step"), m.sem("best_done"), m.sem("marked_done")
        prepared, comb_ready, c_turned, c_hi, c_lo = (m.sem("prepared"), m.sem("comb_ready"), m.sem("c_turned"),
                                                      m.sem("c_hi"), m.sem("c_lo"))
        with nc.Block() as block:
            @block.gpsimd
            def _(pool):
                pool.memset(vals[:, :, E:], LOW).then_inc(prepared, 1)
                pool.memset(found[:, :, :], LOW).then_inc(prepared, 1)
                pool.memset(C[:, :, :], 0.0).then_inc(prepared, 1)

            @block.tensor
            def _(pe):
                def chunk(k, par):
                    after(pe, lT_ready, k - 1)
                    pe.matmul(bank[:, par, :], gateT[:, :], xnT[:, span(k * CH, CH)], start=True, stop=True)\
                      .then_inc(logits_done, 1)
                    pe.wait_ge(lT_ready, k + 1)
                    after(pe, L_ready, k - 1)
                    for i in range(TPC):
                        op = pe.transpose(bank_t[:, par, i, :], lT[:, par, P * i:P * i + P], ident[:, :])
                    op.then_inc(turned, 1)
                in_pairs(pe, NC, chunk)
                pe.wait_ge(comb_ready, 3 if shared_gate else 2)
                for k in range(NC):
                    after(pe, c_lo, k - 1)
                    for i in range(TPC):
                        op = pe.transpose(bank_c[:, k % 2, P * i:P * i + P], C[:, TPC * k + i, :], ident[:, :])
                    op.then_inc(c_turned, 1)

            @block.scalar
            def _(act):
                def chunk(k, par):
                    act.wait_ge(logits_done, k + 1)
                    after(act, turned, k - 1)
                    act.activation(lT[:, par, :], bank[:, par, :], ACT.Copy).then_inc(lT_ready, 1)
                in_pairs(act, NC, chunk)
                if sigmoid_gate:
                    act.wait_ge(L_ready, NC)
                    act.activation(e1[:, :, :], L[:, :, :], ACT.Exp, scale=-1.0).then_inc(act_step, 1)
                else:
                    act.wait_ge(step, 3)
                    act.activation(e1[:, :, 0:E], e1[:, :, 0:E], ACT.Exp).then_inc(act_step, 1)
                    act.activation(e1[:, :, E:EX], L[:, :, E:EX], ACT.Exp, scale=-1.0).then_inc(act_step, 1)
                    act.activation(gap[:, :, :], gap[:, :, :], ACT.Exp).then_inc(act_step, 1)

            @block.vector
            def _(dve):
                count = [0]

                def chain(op):
                    count[0] += 1
                    op.then_inc(step, 1)

                def chained():
                    dve.wait_ge(step, count[0])

                def chunk(k, par):
                    dve.wait_ge(turned, k + 1)
                    dve.tensor_copy(L[:, span(k * TPC, TPC), :], bank_t[:, par, :, 0:EX]).then_inc(L_ready, 1)
                in_pairs(dve, NC, chunk)
                dve.wait_ge(L_ready, NC)
                dve.wait_ge(prepared, 3)
                if sigmoid_gate:
                    dve.wait_ge(act_step, 1)
                    chain(dve.tensor_scalar(e1[:, :, :], e1[:, :, :], 1.0, None, ALU.add))
                    chained()
                    chain(dve.reciprocal(vals[:, :, 0:E], e1[:, :, 0:E]))
                else:
                    chain(dve.tensor_copy(vals[:, :, 0:E], L[:, :, 0:E]))
                chained()
                for t in range(T):
                    dve.max(best[:, t, :], vals[:, t, 0:E]).then_inc(best_done, 1)
                dve.wait_ge(best_done, T)
                dve.tensor_copy(found[:, :, 0:2], best[:, :, 0:2]).then_inc(best_done, 1)
                dve.wait_ge(best_done, T + 1)
                for t in range(T):
                    dve.match_replace(marked[:, t, :], found[:, t, :], vals[:, t, :], HIT).then_inc(marked_done, 1)
                if sigmoid_gate:
                    chain(dve.tensor_tensor(den[:, :, :], best[:, :, 0:1], best[:, :, 1:2], ALU.add))
                    numerators = vals[:, :, 0:E]
                else:
                    chain(dve.tensor_tensor(e1[:, :, 0:E], L[:, :, 0:E], best[:, :, 0:1].broadcast_to([P, T, E]),
                                            ALU.subtract))
                    chain(dve.tensor_tensor(gap[:, :, :], best[:, :, 1:2], best[:, :, 0:1], ALU.subtract))
                    dve.wait_ge(act_step, 3)
                    chain(dve.tensor_scalar(den[:, :, :], gap[:, :, :], 1.0, None, ALU.add))
                    numerators = e1[:, :, 0:E]
                chained()
                chain(dve.reciprocal(den[:, :, :], den[:, :, :]))
                dve.wait_ge(marked_done, T)
                chain(dve.scalar_tensor_tensor(out=marked[:, :, 0:E], in0=marked[:, :, 0:E], scalar=HIT,
                                               in1=numerators, op0=ALU.is_equal, op1=ALU.mult))
                chained()
                for at in (0, 32):
                    dve.tensor_tensor(C[:, :, at:at + E], marked[:, :, 0:E], den[:, :, 0:1].broadcast_to([P, T, E]),
                                      ALU.mult).then_inc(comb_ready, 1)
                if shared_gate:
                    chain(dve.tensor_scalar(e1[:, :, E:EX], e1[:, :, E:EX], 1.0, None, ALU.add))
                    chained()
                    chain(dve.reciprocal(e1[:, :, E:EX], e1[:, :, E:EX]))
                    chained()
                    dve.tensor_copy(C[:, :, 0:64].rearrange("p t (a e) -> p t a e", a=2)[:, :, :, E:EX],
                                    cols(e1[:, :, E:EX], 2, 2)).then_inc(comb_ready, 1)
                for k in range(NC):
                    dve.wait_ge(c_turned, k + 1)
                    out = combT[:, span(k * CH, CH)]
                    dve.tensor_copy(out, bank_c[:, k % 2, :]).then_inc(c_hi, 1)
                    dve.wait_ge(c_hi, k + 1)
                    dve.tensor_tensor(out[32:64], bank_c[32:64, k % 2, :], f32(out)[32:64], ALU.subtract).then_inc(c_lo, 1)


def gated_ffn(nc, name, xnT, blocks, x, ident, combT=None, out_bias=None, out_scale=1.0):
    F = len(blocks)
    weighted = [f for f in range(F) if blocks[f][7] is not None]
    makers = [f for f in weighted if f == 0 or blocks[f][7] is not blocks[f - 1][7]]
    NM = len(makers)
    with phase(nc, name) as m:
        Xh, Xl = m.sb("Xh", [P, 2, CH], F32R), m.sb("Xl", [P, 2, CH], F32R)
        sg, hm, h = m.sb("sg", [P, 2, CH]), m.sb("hm", [P, 2, CH]), m.sb("h", [P, 2, CH])
        Hh, Hl = m.sb("Hh", [P, 2, CH], F32R), m.sb("Hl", [P, 2, CH], F32R)
        y = m.sb("y", [P, CH])
        ps_g, ps_u, ps_w = m.ps("ps_g", [P, 2, CH]), m.ps("ps_u", [P, 2, CH]), m.ps("ps_w", [P, CH])
        ps_o, ps_t = m.ps("ps_o", [P, 2, CH]), m.ps("ps_t", [P, TPC, D])
        xh_ready, x_ready = m.sem("xh_ready"), m.sem("x_ready")
        g_done, u_done, w_done, down_done = m.sem("g_done"), m.sem("u_done"), m.sem("w_done"), m.sem("down_done")
        sg_ready, hm_ready, h_ready = m.sem("sg_ready"), m.sem("hm_ready"), m.sem("h_ready")
        h_hi, h_lo = m.sem("h_hi"), m.sem("h_lo")
        y_ready, turned, added = m.sem("y_ready"), m.sem("turned"), m.sem("added")

        def slot(f, par):
            return (par * F + f) % 2

        def before(k, par, f, lag):
            if f >= lag:
                return k, par, f - lag
            return None if isinstance(k, int) and k == 0 else (k - 1, 1 - par, f - lag + F)

        with nc.Block() as block:
            @block.tensor
            def _(pe):
                def gates(k, par, f):
                    gh, gl, uh, ul, _, _, r, _, _, _ = blocks[f]
                    b = slot(f, par)
                    n = k * F + f
                    if f == 0:
                        pe.wait_ge(x_ready, k + 1)
                    after(pe, sg_ready, n - 1)
                    for w, xs, start in ((gh, Xh, True), (gl, Xh, False), (gh, Xl, False)):
                        op = pe.matmul(ps_g[0:r, b, :], w, xs[:, par, :], start=start, stop=not start and xs is Xl)
                    op.then_inc(g_done, 1)
                    after(pe, hm_ready, n - 1)
                    for w, xs, start in ((uh, Xh, True), (ul, Xh, False), (uh, Xl, False)):
                        op = pe.matmul(ps_u[0:r, b, :], w, xs[:, par, :], start=start, stop=not start and xs is Xl)
                    op.then_inc(u_done, 1)

                def weights(k, f):
                    if f == makers[0]:
                        after(pe, h_ready, (k - 1) * F + weighted[-1] + 1)
                    else:
                        after(pe, h_ready, k * F + f)
                    pe.matmul(ps_w[:, :], blocks[f][7], combT[:, span(k * CH, CH)], start=True, stop=True)\
                      .then_inc(w_done, 1)

                def down(k, par, f):
                    _, _, _, _, dh, dl, r, _, _, _ = blocks[f]
                    b = slot(f, par)
                    if f == 0:
                        after(pe, y_ready, k - 1)
                    pe.wait_ge(h_lo, k * F + f + 1)
                    pe.matmul(ps_o[:, par, :], dh, Hh[0:r, b, :], start=f == 0, stop=False)
                    pe.matmul(ps_o[:, par, :], dl, Hh[0:r, b, :], start=False, stop=False)
                    pe.matmul(ps_o[:, par, :], dh, Hl[0:r, b, :], start=False, stop=f == F - 1)\
                      .then_inc(down_done, 1)

                def turn(k):
                    pe.wait_ge(y_ready, k + 1)
                    after(pe, added, k)
                    for i in range(TPC):
                        op = pe.transpose(ps_t[:, i, :], y[:, P * i:P * i + P], ident[:, :])
                    op.then_inc(turned, 1)

                def chunk(k, par):
                    for f in range(F):
                        gates(k, par, f)
                        old = before(k, par, f, 2)
                        if old is not None:
                            down(*old)
                        if f in makers:
                            weights(k, f)
                        if f == 2 and not (isinstance(k, int) and k == 0):
                            turn(k - 1)
                in_pairs(pe, NC, chunk)
                down(NC - 1, 1, F - 2)
                down(NC - 1, 1, F - 1)
                turn(NC - 1)

            @block.scalar
            def _(act):
                def chunk(k, par):
                    for f in range(F):
                        r, bg = blocks[f][6], blocks[f][8]
                        b = slot(f, par)
                        act.wait_ge(g_done, k * F + f + 1)
                        after(act, hm_ready, k * F + f - 1)
                        if bg is None:
                            op = act.activation(sg[0:r, b, :], ps_g[0:r, b, :], ACT.Silu)
                        else:
                            op = act.activation(sg[0:r, b, :], ps_g[0:r, b, :], ACT.Silu, bias=bg)
                        op.then_inc(sg_ready, 1)
                        old = before(k, par, f, 1)
                        if old is not None:
                            high(*old)
                        if f == 1 and not (isinstance(k, int) and k == 0):
                            finish(k - 1, 1 - par)

                def high(k, par, f):
                    r, b, n = blocks[f][6], slot(f, par), k * F + f
                    act.wait_ge(h_ready, n + 1)
                    after(act, down_done, n - 1)
                    act.activation(Hh[0:r, b, :], h[0:r, b, :], ACT.Copy).then_inc(h_hi, 1)

                def finish(k, par):
                    act.wait_ge(down_done, (k + 1) * F)
                    after(act, turned, k)
                    if out_bias is None:
                        op = act.activation(y[:, :], ps_o[:, par, :], ACT.Copy)
                    else:
                        op = act.activation(y[:, :], ps_o[:, par, :], ACT.Identity, bias=out_bias[:, 0:1])
                    op.then_inc(y_ready, 1)
                in_pairs(act, NC, chunk)
                high(NC - 1, 1, F - 1)
                finish(NC - 1, 1)

            @block.vector
            def _(dve):
                def halves(k, par):
                    after(dve, u_done, (k - 1) * F)
                    src = xnT[:, span(k * CH, CH)]
                    dve.tensor_copy(Xh[:, par, :], src).then_inc(xh_ready, 1)
                    dve.wait_ge(xh_ready, k + 1)
                    dve.tensor_tensor(Xl[:, par, :], src, f32(Xh[:, par, :]), ALU.subtract).then_inc(x_ready, 1)

                def low(k, par, f):
                    r, b, n = blocks[f][6], slot(f, par), k * F + f
                    dve.wait_ge(h_hi, n + 1)
                    after(dve, down_done, n - 1)
                    dve.tensor_tensor(Hl[0:r, b, :], h[0:r, b, :], f32(Hh[0:r, b, :]), ALU.subtract).then_inc(h_lo, 1)

                def chunk(k, par):
                    for f in range(F):
                        r, bu, b, n = blocks[f][6], blocks[f][9], slot(f, par), k * F + f
                        old = before(k, par, f, 1)
                        plain = blocks[f][7] is None
                        dve.wait_ge(sg_ready, n + 1)
                        dve.wait_ge(u_done, n + 1)
                        after(dve, h_lo, n - 1)
                        dst = h[0:r, b, :] if plain else hm[0:r, b, :]
                        if bu is None:
                            op = dve.tensor_tensor(dst, sg[0:r, b, :], ps_u[0:r, b, :], ALU.mult)
                        else:
                            op = dve.scalar_tensor_tensor(out=dst, in0=ps_u[0:r, b, :], scalar=bu,
                                                          in1=sg[0:r, b, :], op0=ALU.add, op1=ALU.mult)
                        op.then_inc(hm_ready, 1)
                        if old is not None:
                            low(*old)
                        dve.wait_ge(hm_ready, n + 1)
                        if plain:
                            dve.sem_inc(h_ready, 1)
                        else:
                            made = sum(mk <= f for mk in makers)
                            dve.wait_ge(w_done, k * NM + made)
                            dve.tensor_tensor(h[0:r, b, :], hm[0:r, b, :], ps_w[0:r, :], ALU.mult).then_inc(h_ready, 1)
                        if f == 0 and not (isinstance(k, int) and k + 1 >= NC):
                            halves(k + 1, 1 - par)
                        if f == 2 and not (isinstance(k, int) and k == 0):
                            add(k - 1)

                def add(k):
                    dve.wait_ge(turned, k + 1)
                    xs = x[:, span(k * TPC, TPC), :]
                    dve.scalar_tensor_tensor(out=xs, in0=ps_t[:, :, :], scalar=out_scale, in1=xs,
                                             op0=ALU.mult, op1=ALU.add).then_inc(added, 1)
                halves(0, 0)
                in_pairs(dve, NC, chunk)
                low(NC - 1, 1, F - 1)
                add(NC - 1)


def linear_attention(nc, name, xn, xnT, x1, Wq, Wkv, bq, bkv_all):
    with phase(nc, name) as m:
        tT = m.sb("tT", [P, 2, P])
        qa, qb, qe, qp = (m.sb(s, [P, 2, P]) for s in ("qa", "qb", "qe", "qp"))
        kv = m.sb("kv", [P, 2, 2 * D + 1])
        ka, ke, kp = (m.sb(s, [P, 2, D]) for s in ("ka", "ke", "kp"))
        state = m.sb("state", [P, 2, 2, D + 1])
        den = m.sb("den", [P, 2, 1])
        ps_q, ps_kv = m.ps("ps_q", [P, 2, 512]), m.ps("ps_kv", [P, 2, 512])
        ps_s, ps_n = m.ps("ps_s", [P, 2, 512]), m.ps("ps_n", [P, 2, 512])
        set_up, tT_ready, qkv_done = m.sem("set_up"), m.sem("tT_ready"), m.sem("qkv_done")
        q_min, q_max, kv_read, k_min = m.sem("q_min"), m.sem("q_max"), m.sem("kv_read"), m.sem("k_min")
        exp_done, features, state_done = m.sem("exp_done"), m.sem("features"), m.sem("state_done")
        state_ready, num_done, den_step, x1_ready = (m.sem("state_ready"), m.sem("num_done"), m.sem("den_step"),
                                                     m.sem("x1_ready"))
        with nc.Block() as block:
            @block.gpsimd
            def _(pool):
                pool.memset(kv[:, :, 2 * D:], 1.0).then_inc(set_up, 1)

                def tile(t, par):
                    after(pool, qkv_done, t - 1)
                    pool.wait_ge(set_up, 1)
                    pool.tensor_copy(tT[:, par, :], xnT[:, span(t * P, P)]).then_inc(tT_ready, 1)
                in_pairs(pool, T, tile)

            @block.tensor
            def _(pe):
                def project(t, par):
                    pe.wait_ge(tT_ready, t + 1)
                    after(pe, q_max, t - 1)
                    after(pe, kv_read, t - 1)
                    pe.matmul(ps_q[:, par, 0:P], Wq, tT[:, par, :], start=True, stop=True)
                    pe.matmul(ps_kv[:, par, 0:2 * D], tT[:, par, :], Wkv, start=True, stop=True).then_inc(qkv_done, 1)

                def tile(t, par):
                    if not (isinstance(t, int) and t + 1 >= T):
                        project(t + 1, 1 - par)
                    pe.wait_ge(features, t + 1)
                    after(pe, state_ready, t)
                    for s in range(2):
                        rows = slice(S * s, S * s + S)
                        op = pe.matmul(ps_s[:, s, 0:D + 1], kp[rows, par, :], kv[rows, par, D:], start=True, stop=True)
                    op.then_inc(state_done, 1)
                    pe.wait_ge(state_ready, t + 1)
                    after(pe, x1_ready, t - 1)
                    for s in range(2):
                        op = pe.matmul(ps_n[S * s:S * s + S, par, 0:D + 1], qp[:, par, S * s:S * s + S],
                                       state[:, par, s, :], start=True, stop=True)
                    op.then_inc(num_done, 1)
                pe.wait_ge(set_up, 1)
                project(0, 0)
                in_pairs(pe, T, tile)

            @block.scalar
            def _(act):
                def tile(t, par):
                    act.wait_ge(q_min, t + 1)
                    after(act, features, t - 1)
                    act.activation(qe[:, par, :], qa[:, par, :], ACT.Exp).then_inc(exp_done, 1)
                    act.wait_ge(k_min, t + 1)
                    act.activation(ke[:, par, :], ka[:, par, :], ACT.Exp).then_inc(exp_done, 1)
                    act.wait_ge(state_done, t + 1)
                    after(act, num_done, t - 1)
                    act.activation(state[:, par, :, :], ps_s[:, :, 0:D + 1], ACT.Copy).then_inc(state_ready, 1)
                in_pairs(act, T, tile)

            @block.vector
            def _(dve):
                def inputs(t, par):
                    dve.wait_ge(qkv_done, t + 1)
                    after(dve, num_done, t - 1)
                    after(dve, exp_done, 2 * (t - 1))
                    dve.tensor_tensor(kv[:, par, 0:2 * D], ps_kv[:, par, 0:2 * D], bkv_all[:, :], ALU.add)\
                       .then_inc(kv_read, 1)
                    dve.tensor_scalar(qa[:, par, :], ps_q[:, par, 0:P], bq[:, 0:1], 0.0, ALU.add, ALU.min)\
                       .then_inc(q_min, 1)
                    dve.tensor_scalar(qb[:, par, :], ps_q[:, par, 0:P], bq[:, 0:1], 0.0, ALU.add, ALU.max)\
                       .then_inc(q_max, 1)
                    dve.wait_ge(kv_read, t + 1)
                    dve.tensor_scalar(ka[:, par, :], kv[:, par, 0:D], 0.0, None, ALU.min).then_inc(k_min, 1)

                def feature_maps(t, par):
                    dve.wait_ge(q_max, t + 1)
                    dve.wait_ge(exp_done, 2 * t + 2)
                    dve.tensor_tensor(qp[:, par, :], qb[:, par, :], qe[:, par, :], ALU.add)
                    dve.scalar_tensor_tensor(out=kp[:, par, :], in0=kv[:, par, 0:D], scalar=0.0, in1=ke[:, par, :],
                                             op0=ALU.max, op1=ALU.add).then_inc(features, 1)

                def divide(t, par):
                    dve.wait_ge(num_done, t + 1)
                    dve.tensor_scalar(den[:, par, :], ps_n[:, par, D:D + 1], 1e-6, None, ALU.add).then_inc(den_step, 1)
                    dve.wait_ge(den_step, 2 * t + 1)
                    dve.reciprocal(den[:, par, :], den[:, par, :]).then_inc(den_step, 1)
                    dve.wait_ge(den_step, 2 * t + 2)
                    dve.scalar_tensor_tensor(out=x1[:, t, :], in0=ps_n[:, par, 0:D], scalar=den[:, par, 0:1],
                                             in1=xn[:, t, :], op0=ALU.mult, op1=ALU.add).then_inc(x1_ready, 1)

                def tile(t, par):
                    feature_maps(t, par)
                    if not (isinstance(t, int) and t + 1 >= T):
                        inputs(t + 1, 1 - par)
                    divide(t, par)
                dve.wait_ge(set_up, 1)
                inputs(0, 0)
                in_pairs(dve, T, tile)


def centre(nc, name, xnT, hi, lo):
    with phase(nc, name) as m:
        mean = m.sb("mean", [P, B])
        y = m.sb("y", [P, 2, CH])
        per = CH // S
        step, summed, y_ready, hi_ready, lo_ready = (m.sem("step"), m.sem("summed"), m.sem("y_ready"),
                                                     m.sem("hi_ready"), m.sem("lo_ready"))
        with nc.Block() as block:
            @block.vector
            def _(dve):
                for k in range(NC):
                    dve.tensor_reduce(mean[:, span(k * per, per)],
                                      xnT[:, span(k * CH, CH)].rearrange("p (b s) -> p b s", s=S),
                                      AX.X, ALU.add).then_inc(summed, 1)
                dve.wait_ge(summed, NC)
                dve.tensor_scalar(mean[:, :], mean[:, :], 1.0 / S, None, ALU.mult).then_inc(step, 1)
                dve.wait_ge(step, 1)
                for k in range(NC):
                    after(dve, lo_ready, k - 1)
                    yk = y[:, k % 2, :]
                    dve.tensor_tensor(yk.rearrange("p (b s) -> p b s", s=S),
                                      xnT[:, span(k * CH, CH)].rearrange("p (b s) -> p b s", s=S),
                                      cols(mean[:, span(k * per, per)], 2, S), ALU.subtract).then_inc(y_ready, 1)
                    dve.wait_ge(y_ready, k + 1)
                    dve.tensor_copy(hi[:, span(k * CH, CH)], yk).then_inc(hi_ready, 1)
                    dve.wait_ge(hi_ready, k + 1)
                    dve.tensor_tensor(lo[:, span(k * CH, CH)], yk, f32(hi[:, span(k * CH, CH)]), ALU.subtract)\
                       .then_inc(lo_ready, 1)


def store(nc, name, out, x):
    with phase(nc, name) as m:
        stored = m.sem("stored")
        with nc.Block() as block:
            @block.sync
            def _(sp):
                for k in range(NC):
                    sp.dma_start(out[:, span(k * TPC, TPC), :], x[:, span(k * TPC, TPC), :]).then_inc(stored, 16)
                sp.wait_ge(stored, 16 * NC)


def cross_attention(nc, tag, a, x, con, attn_eps, den_eps, mask=None):
    with ExitStack() as stack:
        def sb(name, shape, dt=F32):
            return stack.enter_context(nc.sbuf_tensor(f"{tag}_{name}", shape, dt))

        WT = {w: sb(f"{w}T", [P, D]) for w in ("Wq", "Wk", "Wv", "Wo")}
        bq, bk, bo, bv_all = sb("bq", [P, 1]), sb("bk", [P, 1]), sb("bo", [P, 1]), sb("bv_all", [P, D])
        mask_bias = sb("mask_bias", [P, B]) if mask is not None else None
        with ExitStack() as early:
            raw = early.enter_context(nc.sbuf_tensor(f"{tag}_raw", [P, 4, D], F32))
            jobs = [(raw[:, i, :], a[f"{tag}_{w}"]) for i, w in enumerate(WT)]
            jobs += [(b[:, :], a[f"{tag}_{n}"].unsqueeze(1)) for n, b in (("bq", bq), ("bk", bk), ("bo", bo))]
            jobs += [(bv_all[:, :], a[f"{tag}_bv"].unsqueeze(0).broadcast_to([P, D]))]
            turns = [(t[:, :], raw[:, i, :]) for i, t in enumerate(WT.values())]
            if mask is not None:
                keep8 = early.enter_context(nc.sbuf_tensor(f"{tag}_keep8", [B, SK], U8))
                keep = early.enter_context(nc.sbuf_tensor(f"{tag}_keep", [B, SK], F32))
                jobs += [(keep8[:, :], mask)]
                turns += [(mask_bias[:, :], keep[:, :])]
            load(nc, f"{tag}_load", jobs)
            if mask is not None:
                elementwise(nc, f"{tag}_keep_bias", lambda dve: dve.tensor_scalar(
                    keep[:, :], keep8[:, :], -MASKED, MASKED, ALU.mult, ALU.add))
            transpose_all(nc, f"{tag}_turn", turns, con["ident"])
        xnT = sb("xnT", [P, B * S])
        layernorm(nc, f"{tag}_ln", x, 1e-5, con["ident"], xnT=xnT)
        Kh, Kl = sb("Kh", [P, B * SK], F32R), sb("Kl", [P, B * SK], F32R)
        V = sb("V", [P, B, D])
        keys_values(nc, f"{tag}_kv", a["ctx_1024"], Kh, Kl, V, WT["Wk"], WT["Wv"], bk, bv_all, con["ident"], mask)
        Qh, Ql = sb("Qh", [P, B * S], F32R), sb("Ql", [P, B * S], F32R)
        queries(nc, f"{tag}_q", xnT, Qh, Ql, WT["Wq"], bq)
        attention(nc, f"{tag}_att", Kh, Kl, V, Qh, Ql, xnT, con, SK, float(DH) ** -0.5, den_eps, mask, mask_bias)
        project_add(nc, f"{tag}_out", xnT, x, con["ident"], WT["Wo"], bo)


def elementwise(nc, name, op):
    with nc.Block() as block:
        @block.vector
        def _(dve):
            op(dve)


def linear_block(nc, a, x, con):
    pre = "L0_attn_"
    with ExitStack() as stack:
        def sb(name, shape, dt=F32):
            return stack.enter_context(nc.sbuf_tensor(f"la_{name}", shape, dt))

        rows = [P, P, L0_H - 2 * P]
        Wqkv = sb("Wqkv", [P, 3 * D])
        Wg, Wu, Wd = sb("Wg", [P, L0_H]), sb("Wu", [P, L0_H]), sb("Wd", [P, 3, D])
        dh, dl = sb("dh", [P, 3, D], F32R), sb("dl", [P, 3, D], F32R)
        gh, gl, uh, ul = (sb(n, [P, L0_H], F32R) for n in ("gh", "gl", "uh", "ul"))
        bq, bkv_all = sb("bq", [P, 1]), sb("bkv_all", [P, 2 * D])
        bg, bu, bd = sb("bg", [P, 3]), sb("bu", [P, 3]), sb("bd", [P, 1])
        vecs = {n: sb(n, [P, D]) for n in ("g1", "b1", "g2", "b2")}
        jobs = [(Wqkv[:, :], a[pre + "Wqkv"]), (Wg[:, :], a[pre + "Wg"]), (Wu[:, :], a[pre + "Wu"]),
                (bq[:, :], a[pre + "bqkv"][0:D].unsqueeze(1)),
                (bkv_all[:, :], a[pre + "bqkv"][D:3 * D].unsqueeze(0).broadcast_to([P, 2 * D])),
                (bd[:, :], a[pre + "bd"].unsqueeze(1))]
        for i, r in enumerate(rows):
            at = slice(P * i, P * i + r)
            jobs += [(Wd[0:r, i, :], a[pre + "Wd"][at, :]), (bg[0:r, i:i + 1], a[pre + "bg"][at].unsqueeze(1)),
                     (bu[0:r, i:i + 1], a[pre + "bu"][at].unsqueeze(1))]
        jobs += [(v[:, :], a[pre + n].unsqueeze(0).broadcast_to([P, D])) for n, v in vecs.items()]
        load(nc, "la_load", jobs)
        split(nc, "la_split", [(gh[:, :], gl[:, :], Wg[:, :]), (uh[:, :], ul[:, :], Wu[:, :])] +
              [(dh[0:r, i, :], dl[0:r, i, :], Wd[0:r, i, :]) for i, r in enumerate(rows)])
        xn, xnT, x1 = sb("xn", [P, T, D]), sb("xnT", [P, B * S]), sb("x1", [P, T, D])
        layernorm(nc, "la_ln", x, 1e-5, con["ident"], xnT=xnT, nat=xn)
        linear_attention(nc, "la_att", xn, xnT, x1, Wqkv[:, 0:D], Wqkv[:, D:3 * D], bq, bkv_all)
        layernorm(nc, "la_ln1", x1, 1e-5, con["ident"], xnT=xnT, nat=xn, gain=vecs["g1"], shift=vecs["b1"])
        blocks = []
        for i, r in enumerate(rows):
            at = slice(P * i, P * i + r)
            blocks.append((gh[:, at], gl[:, at], uh[:, at], ul[:, at], dh[0:r, i, :], dl[0:r, i, :], r, None,
                           bg[0:r, i:i + 1], bu[0:r, i:i + 1]))
        gated_ffn(nc, "la_ffn", xnT, blocks, xn, con["ident"], out_bias=bd)
        layernorm(nc, "la_ln2", xn, 1e-5, con["ident"], gain=vecs["g2"], shift=vecs["b2"], add_to=x)


def moe0(nc, a, x, con):
    pre = "L0_ffn_"
    NB = L0_E * L0_F // P
    rows = [P, P, L0_SHARED - 2 * P]
    with ExitStack() as stack:
        def sb(name, shape, dt=F32):
            return stack.enter_context(nc.sbuf_tensor(f"m0_{name}", shape, dt))

        gh, gl, uh, ul = (sb(n, [P, NB + 3, P], F32R) for n in ("gh", "gl", "uh", "ul"))
        dh, dl = sb("dh", [P, NB + 3, D], F32R), sb("dl", [P, NB + 3, D], F32R)
        gateT = sb("gateT", [P, P])
        spread = sb("spread", [P, len(L0_SPREAD), P], F32R)
        with ExitStack() as early:
            def eb(name, shape, dt=F32):
                return early.enter_context(nc.sbuf_tensor(f"m0_{name}", shape, dt))

            wgu = eb("wgu", [P, L0_E, 2 * L0_F])
            wd = eb("wd", [P, NB + 3, D])
            raw = eb("raw", [P, 3, 2, D])
            rawd = eb("rawd", [P, L0_SHARED])
            shT = eb("shT", [P, 2, 3 * P])
            gates = eb("gates", [P, D])
            spread_raw = eb("spread_raw", [P, len(L0_SPREAD) * P])
            jobs = [(wgu[:, :, :], a[pre + "w_gate_up"].rearrange("e d f -> d e f")),
                    (wd[:, 0:NB, :], a[pre + "w_down"].rearrange("e f d -> (e f) d").rearrange("(b r) d -> r b d", r=P)),
                    (rawd[:, :], a[pre + "shared_w_down"]),
                    (gates[0:L0_E, :], a[pre + "gate_w"]), (gates[L0_E:L0_E + 1, :], a[pre + "shared_gate_w"]),
                    (spread_raw[:, :], a["c_spread0"])]
            for i, r in enumerate(rows):
                at = slice(P * i, P * i + r)
                jobs += [(raw[0:r, i, 0, :], a[pre + "shared_w_gate"][at, :]),
                         (raw[0:r, i, 1, :], a[pre + "shared_w_up"][at, :])]
            elementwise(nc, "m0_zero", lambda dve: dve.memset(gates[:, :], 0.0))
            load(nc, "m0_load", jobs)
            turns = [(gateT[:, :], gates[:, :])]
            for i, r in enumerate(rows):
                at = slice(P * i, P * i + r)
                turns += [(shT[:, 0, at], raw[0:r, i, 0, :]), (shT[:, 1, at], raw[0:r, i, 1, :]),
                          (wd[0:r, NB + i, :], rawd[:, at])]
            transpose_all(nc, "m0_turn", turns, con["ident"])
            pick = wgu[:, :, :].rearrange("p (b e) (s f) -> p s b e f", e=2, s=2)
            jobs = []
            for b in range(NB):
                for s, (hi, lo) in enumerate(((gh, gl), (uh, ul))):
                    jobs.append((hi[:, b, :].rearrange("p (e f) -> p e f", e=2),
                                 lo[:, b, :].rearrange("p (e f) -> p e f", e=2), pick[:, s, b]))
            for s, (hi, lo) in enumerate(((gh, gl), (uh, ul))):
                flat = [v[:, NB:, :].rearrange("p b r -> p (b r)")[:, 0:L0_SHARED] for v in (hi, lo)]
                jobs.append((flat[0], flat[1], shT[:, s, 0:L0_SHARED]))
            jobs.append((spread[:, :, :].rearrange("p b r -> p (b r)"), None, spread_raw[:, :]))
            jobs += [(dh[:, 0:NB, :], dl[:, 0:NB, :], wd[:, 0:NB, :])]
            jobs += [(dh[0:r, NB + i, :], dl[0:r, NB + i, :], wd[0:r, NB + i, :]) for i, r in enumerate(rows)]
            split(nc, "m0_split", jobs)
        xnT = sb("xnT", [P, B * S])
        combT = sb("combT", [P, B * S], F32R)
        layernorm(nc, "m0_ln", x, 1e-5, con["ident"], xnT=xnT)
        route(nc, "m0_route", xnT, gateT, L0_E, combT, con["ident"], False, True)
        spreads = [spread[:, f, :] for f in range(NB + 1)]
        blocks = [(gh[:, f, 0:r], gl[:, f, 0:r], uh[:, f, 0:r], ul[:, f, 0:r], dh[0:r, f, :], dl[0:r, f, :], r,
                   spreads[min(f, NB)], None, None) for f, r in enumerate([P] * NB + rows)]
        gated_ffn(nc, "m0_ffn", xnT, blocks, x, con["ident"], combT=combT)


def moe1(nc, a, x, con):
    pre = "L1_ffn_"
    FB = L1_F // P
    NB = L1_E * FB
    with ExitStack() as stack:
        def sb(name, shape, dt=F32):
            return stack.enter_context(nc.sbuf_tensor(f"m1_{name}", shape, dt))

        gh, gl, uh, ul = (sb(n, [P, NB + FB, P], F32R) for n in ("gh", "gl", "uh", "ul"))
        dh, dl = sb("dh", [P, NB + FB, D], F32R), sb("dl", [P, NB + FB, D], F32R)
        gateT = sb("gateT", [P, P])
        spread = sb("spread", [P, L1_E, P], F32R)
        with ExitStack() as early:
            def eb(name, shape, dt=F32):
                return early.enter_context(nc.sbuf_tensor(f"m1_{name}", shape, dt))

            raw_g, raw_u = eb("raw_g", [P, NB + FB, P]), eb("raw_u", [P, NB + FB, P])
            wd = eb("wd", [P, NB + FB, D])
            spread_raw = eb("spread_raw", [P, L1_E * P])
            jobs = [(gateT[:, 0:L1_E], a[pre + "Wg"]), (spread_raw[:, :], a["c_spread1"])]
            for raw, we, ws in ((raw_g, "We1", "Ws1"), (raw_u, "We3", "Ws3")):
                v = raw[:, :, :].rearrange("p (e b) r -> p e (b r)", b=FB)
                jobs += [(v[:, 0:L1_E, :], a[pre + we].rearrange("e d f -> d e f")), (v[:, L1_E, :], a[pre + ws])]
            jobs += [(wd[:, 0:NB, :], a[pre + "We2"].rearrange("e f d -> (e f) d").rearrange("(b r) d -> r b d", r=P)),
                     (wd[:, NB:, :], a[pre + "Ws2"].rearrange("(b r) d -> r b d", r=P))]
            elementwise(nc, "m1_zero", lambda dve: dve.memset(gateT[:, :], 0.0))
            load(nc, "m1_load", jobs)
            split(nc, "m1_split", [(gh[:, :, :], gl[:, :, :], raw_g[:, :, :]), (uh[:, :, :], ul[:, :, :], raw_u[:, :, :]),
                                   (dh[:, :, :], dl[:, :, :], wd[:, :, :]),
                                   (spread[:, :, :].rearrange("p b r -> p (b r)"), None, spread_raw[:, :])])
        xnT = sb("xnT", [P, B * S])
        combT = sb("combT", [P, B * S], F32R)
        layernorm(nc, "m1_ln", x, 1e-5, con["ident"], xnT=xnT)
        route(nc, "m1_route", xnT, gateT, L1_E, combT, con["ident"], True, False)
        spreads = [spread[:, e, :] for e in range(L1_E)] + [None]
        blocks = [(gh[:, f, :], gl[:, f, :], uh[:, f, :], ul[:, f, :], dh[:, f, :], dl[:, f, :], P,
                   spreads[f // FB], None, None) for f in range(NB + FB)]
        gated_ffn(nc, "m1_ffn", xnT, blocks, x, con["ident"], combT=combT, out_scale=1.0 / 3.0)


def self_attention(nc, x, con):
    with ExitStack() as stack:
        def sb(name, shape, dt=F32):
            return stack.enter_context(nc.sbuf_tensor(f"sa_{name}", shape, dt))

        xn, xnT, AT = sb("xn", [P, T, D]), sb("xnT", [P, B * S]), sb("AT", [P, B * S])
        hi, lo = sb("hi", [P, B * S], F32R), sb("lo", [P, B * S], F32R)
        layernorm(nc, "sa_ln", x, 1e-5, con["ident"], xnT=xnT, nat=xn)
        centre(nc, "sa_centre", xnT, hi, lo)
        attention(nc, "sa_att", hi, lo, xn, hi, lo, AT, con, S, 1.0)
        project_add(nc, "sa_out", AT, x, con["ident"])


STAGES = 6


def perceiver_kernel(nc, a, out, stages=STAGES):
    x_dram = a["x"].rearrange("b s d -> (b s) d").rearrange("(t p) d -> p t d", p=P)
    out_dram = out.rearrange("b s d -> (b s) d").rearrange("(t p) d -> p t d", p=P)
    with ExitStack() as stack:
        def sb(name, shape, dt=F32):
            return stack.enter_context(nc.sbuf_tensor(name, shape, dt))

        x = sb("x", [P, T, D])
        ident = sb("ident", [P, P])
        mask4 = sb("mask4", [P, J])
        sel, selm = sb("sel", [P, G, 4, P], F32R), sb("selm", [64, PAIRS, P], BF16)
        with nc.sbuf_tensor("sel_raw", [P, G * 4 * P], F32) as sel_raw, \
                nc.sbuf_tensor("selm_raw", [64, PAIRS * P], F32) as selm_raw:
            load(nc, "first", [(x[:, :, :], x_dram), (ident[:, :], a["c_ident"]), (mask4[:, :], a["c_mask4"]),
                               (sel_raw[:, :], a["c_sel"]), (selm_raw[:, :], a["c_selm"])])
            split(nc, "sels", [(sel[:, :, :, :].rearrange("p a b c -> p (a b c)"), None, sel_raw[:, :]),
                               (selm[:, :, :].rearrange("p a b -> p (a b)"), None, selm_raw[:, :])])
        con = {"ident": ident, "sel": sel, "selm": selm, "mask4": mask4}
        steps = [lambda: cross_attention(nc, "L0_xattn", a, x, con, None, 1e-9),
                 lambda: linear_block(nc, a, x, con),
                 lambda: moe0(nc, a, x, con),
                 lambda: cross_attention(nc, "L1_xattn", a, x, con, None, None, a["mask_BxS2_bf1"]),
                 lambda: self_attention(nc, x, con),
                 lambda: moe1(nc, a, x, con)]
        for step in steps[:stages]:
            step()
        store(nc, "last", out_dram, x)


_INS = ['x', 'ctx_1024', 'mask_BxS2_bf1', 'L0_xattn_Wq', 'L0_xattn_bq', 'L0_xattn_Wk', 'L0_xattn_bk',
        'L0_xattn_Wv', 'L0_xattn_bv', 'L0_xattn_Wo', 'L0_xattn_bo', 'L0_attn_Wqkv', 'L0_attn_bqkv', 'L0_attn_Wg',
        'L0_attn_bg', 'L0_attn_Wu', 'L0_attn_bu', 'L0_attn_Wd', 'L0_attn_bd', 'L0_attn_g1', 'L0_attn_b1',
        'L0_attn_g2', 'L0_attn_b2', 'L0_ffn_gate_w', 'L0_ffn_w_gate_up', 'L0_ffn_w_down', 'L0_ffn_shared_w_gate',
        'L0_ffn_shared_w_up', 'L0_ffn_shared_w_down', 'L0_ffn_shared_gate_w', 'L1_xattn_Wq', 'L1_xattn_bq',
        'L1_xattn_Wk', 'L1_xattn_bk', 'L1_xattn_Wv', 'L1_xattn_bv', 'L1_xattn_Wo', 'L1_xattn_bo', 'L1_ffn_Wg',
        'L1_ffn_Ws1', 'L1_ffn_Ws3', 'L1_ffn_Ws2', 'L1_ffn_We1', 'L1_ffn_We3', 'L1_ffn_We2']


def kernel(**inputs):
    import numpy as _np
    import concourse.bacc as _bacc
    from concourse import mybir as _mybir
    from concourse.bass_utils import run_bass_kernel_spmd as _run

    nc = _bacc.Bacc("TRN2", target_bir_lowering=False, num_devices=1)
    sel, selm, mask4 = head_constants()
    constants = {"c_ident": _np.eye(P, dtype=_np.float32), "c_sel": sel, "c_selm": selm, "c_mask4": mask4,
                 "c_spread0": spread_constants(L0_SPREAD), "c_spread1": spread_constants(L1_SPREAD)}
    arrays, args = {}, {}
    for name in _INS:
        v = _np.ascontiguousarray(inputs[name])
        if v.dtype == _np.bool_:
            v = v.view(_np.uint8)
        arrays[f"in_{name}_dram"] = v
        args[name] = nc.dram_tensor(f"in_{name}_dram", v.shape, _mybir.dt.from_np(v.dtype), kind="ExternalInput").ap()
    for name, v in constants.items():
        arrays[f"in_{name}_dram"] = v
        args[name] = nc.dram_tensor(f"in_{name}_dram", v.shape, _mybir.dt.from_np(v.dtype), kind="ExternalInput").ap()
    out = nc.dram_tensor("out_0_dram", (B, S, D), F32, kind="ExternalOutput").ap()
    perceiver_kernel(nc, args, out)
    r = _run(nc, [arrays], core_ids=[0])
    return r.results[0]["out_0_dram"]
```

```python
from contextlib import ExitStack, contextmanager

import numpy as np

import concourse.bass as bass
from concourse import mybir

F32 = mybir.dt.float32
F32R = mybir.dt.float32r
BF16 = mybir.dt.bfloat16
U8 = mybir.dt.uint8
ALU = mybir.AluOpType
ACT = mybir.ActivationFunctionType
AX = mybir.AxisListType

P = 128
B, S, D = 64, 64, 128
SK = 128
H, DH = 16, 8
T = B * S // P
CH = 512
NC = B * S // CH
TPC = CH // P
G, J = 4, 4
W32 = J * DH
PAIRS = H // 2
MASKED = -10000.0
MASKED_UNSCALED = -28288.0


def hi_rows(v):
    return slice(64 * v, 64 * v + 64)


def lo_rows(v):
    return hi_rows(1 - v)


def head_constants():
    sel = np.zeros((P, G, 2, P), np.float32)
    for g in range(G):
        hi, lo = hi_rows(g // 2).start + W32 * (g % 2), lo_rows(g // 2).start + W32 * (g % 2)
        for which, (hi_blocks, lo_blocks) in enumerate((((0, 1), (2, 3)), ((0, 2), (1, 3)))):
            for start, blocks in ((hi, hi_blocks), (lo, lo_blocks)):
                for r in blocks:
                    for a in range(W32):
                        sel[start + a, g, which, W32 * r + a] = 1.0
    selm = np.zeros((64, PAIRS, P), np.float32)
    for i in range(PAIRS):
        selm[i, i] = selm[32 + i, i] = 1.0
    mask4 = np.zeros((P, J), np.float32)
    for row in range(P):
        mask4[row, row % W32 // DH] = 1.0
    return sel.reshape(P, -1), selm.reshape(64, -1), mask4


def spread_constants(experts_of_block):
    m = np.zeros((P, len(experts_of_block), P), np.float32)
    for f, row in enumerate(experts_of_block):
        for col, e in enumerate(row):
            m[e, f, col] = m[32 + e, f, col] = 1.0
    return m.reshape(P, -1)


L0_E, L0_F, L0_SHARED = 16, 64, 352
L0_SPREAD = [[2 * f] * 64 + [2 * f + 1] * 64 for f in range(8)] + [[16] * P]
L1_E, L1_F = 8, 256
L1_SPREAD = [[e] * P for e in range(8)]
L0_H = 341


def after(eng, sem, count):
    if not isinstance(count, int) or count > 0:
        eng.wait_ge(sem, count)


def in_pairs(eng, n, step, peel=1):
    for p in range(peel):
        step(2 * p, 0)
        step(2 * p + 1, 1)
    with eng.Fori(peel, n // 2 - peel) as p:
        step(p * 2, 0)
        step(p * 2 + 1, 1)
    for p in range(n // 2 - peel, n // 2):
        step(2 * p, 0)
        step(2 * p + 1, 1)


def in_fours(eng, n, step):
    for u in range(4):
        step(u, u, u // 2)
    with eng.Fori(1, n // 4 - 1) as r:
        for i in range(4):
            step(r * 4 + i, i, r * 2 + i // 2)
    for u in range(n - 4, n):
        step(u, u % 4, u // 2)


def span(start, n):
    return slice(start, start + n) if isinstance(start, int) else bass.ds(start, n)


def cols(ap, at, n):
    ap = ap.unsqueeze(at)
    shape = list(ap.shape)
    shape[at] = n
    return ap.broadcast_to(shape)


def f32(ap):
    return ap.bitcast(F32)


class Mem:

    def __init__(self, nc, stack, name):
        self.nc, self.stack, self.name, self.sems = nc, stack, name, []

    def sb(self, name, shape, dt=F32):
        return self.stack.enter_context(self.nc.sbuf_tensor(f"{self.name}_{name}", shape, dt))

    def ps(self, name, shape, dt=F32):
        return self.stack.enter_context(self.nc.psum_tensor(f"{self.name}_{name}", shape, dt))

    def sem(self, name):
        s = self.nc.alloc_semaphore(f"{self.name}_{name}")
        self.sems.append(s)
        return s


@contextmanager
def phase(nc, name):
    with ExitStack() as stack:
        mem = Mem(nc, stack, name)
        yield mem
        nc.clear_and_free_semaphores(mem.sems)
        nc.all_engine_barrier()


def layernorm(nc, name, src, eps, ident, xnT=None, nat=None, gain=None, shift=None, add_to=None,
              loads=(), src_dram=None):
    with phase(nc, name) as m:
        stats = m.sb("stats", [P, T, 6])
        meanvar = m.sb("meanvar", [P, T, 2])
        ve = m.sb("ve", [P, T])
        power = m.sb("power", [P, TPC])
        rstd = m.sb("rstd", [P, T])
        shifts = m.sb("shifts", [P, T])
        work = None if nat is not None else m.sb("work", [P, 2, TPC, D])
        bank = m.ps("bank", [P, NC, CH])
        stats_done, aggr_done = m.sem("stats_done"), m.sem("aggr_done")
        power_set, ve_ready, rstd_ready = m.sem("power_set"), m.sem("ve_ready"), m.sem("rstd_ready")
        shifts_ready, normed, scaled, xn_ready = (m.sem("shifts_ready"), m.sem("normed"), m.sem("scaled"),
                                                  m.sem("xn_ready"))
        turned, added, loaded = m.sem("turned"), m.sem("added"), m.sem("loaded")
        src_in = [m.sem(f"src_in{k}") for k in range(NC)] if src_dram is not None else None

        def tiles(k):
            return slice(k * TPC, k * TPC + TPC)

        def xn(k):
            return nat[:, tiles(k), :] if nat is not None else work[:, k % 2]

        with nc.Block() as block:
            @block.vector
            def _(dve):
                def shift_of(k):
                    dve.wait_ge(rstd_ready, k + 1)
                    dve.scalar_tensor_tensor(out=shifts[:, tiles(k)], in0=meanvar[:, tiles(k), 0], scalar=-1.0,
                                             in1=rstd[:, tiles(k)], op0=ALU.mult, op1=ALU.mult).then_inc(shifts_ready, 1)

                def scale(k):
                    dve.wait_ge(normed, k + 1)
                    dve.tensor_tensor(xn(k), xn(k), cols(gain[:, :], 1, TPC), ALU.mult).then_inc(scaled, 1)
                    dve.wait_ge(scaled, k + 1)
                    dve.tensor_tensor(xn(k), xn(k), cols(shift[:, :], 1, TPC), ALU.add).then_inc(xn_ready, 1)
                    if add_to is not None:
                        dve.wait_ge(xn_ready, k + 1)
                        y = add_to[:, tiles(k), :]
                        dve.tensor_tensor(y, y, xn(k), ALU.add).then_inc(added, 1)

                def evacuate(k):
                    dve.wait_ge(turned, k + 1)
                    dve.tensor_copy(xnT[:, k * CH:k * CH + CH], bank[:, k, :])

                for t in range(T + 2):
                    if src_in is not None and t < T and t % TPC == 0:
                        dve.wait_ge(src_in[t // TPC], 16)
                    if t < T:
                        dve.bn_stats(stats[:, t, :], src[:, t, :]).then_inc(stats_done, 1)
                    if t >= 2:
                        dve.wait_ge(stats_done, t - 1)
                        dve.bn_aggr(meanvar[:, t - 2, :], stats[:, t - 2, :]).then_inc(aggr_done, 1)
                    if t % TPC == 3 and t // TPC >= 2:
                        shift_of(t // TPC - 2)
                shift_of(NC - 2)
                for k in range(NC):
                    if k == 1:
                        shift_of(NC - 1)
                    if gain is not None:
                        scale(k)
                    if xnT is not None and k > 0:
                        evacuate(k - 1)
                if xnT is not None:
                    evacuate(NC - 1)

            @block.gpsimd
            def _(pool):
                pool.memset(power[:, :], -0.5).then_inc(power_set, 1)
                for k in range(NC):
                    pool.wait_ge(aggr_done, k * TPC + TPC)
                    pool.tensor_scalar(ve[:, tiles(k)], meanvar[:, tiles(k), 1], eps, None, ALU.add).then_inc(ve_ready, 1)
                    pool.wait_ge(ve_ready, k + 1)
                    pool.wait_ge(power_set, 1)
                    pool.tensor_tensor(rstd[:, tiles(k)], ve[:, tiles(k)], power[:, :], ALU.pow).then_inc(rstd_ready, 1)

            @block.scalar
            def _(act):
                for k in range(NC):
                    act.wait_ge(shifts_ready, k + 1)
                    if nat is None and xnT is not None:
                        after(act, turned, k - 1)
                    if nat is None and add_to is not None:
                        after(act, added, k - 1)
                    for i in range(TPC):
                        t = k * TPC + i
                        op = act.activation(xn(k)[:, i, :], src[:, t, :], ACT.Identity,
                                            scale=rstd[:, t:t + 1], bias=shifts[:, t:t + 1])
                    op.then_inc(normed, 1)

            if xnT is not None:
                @block.tensor
                def _(pe):
                    for k in range(NC):
                        pe.wait_ge(xn_ready if gain is not None else normed, k + 1)
                        for i in range(TPC):
                            op = pe.transpose(bank[:, k, P * i:P * i + P], xn(k)[:, i, :], ident[:, :])
                        op.then_inc(turned, 1)

            if loads or src_dram is not None:
                @block.sync
                def _(sp):
                    if src_dram is not None:
                        for k in range(NC):
                            sp.dma_start(src[:, tiles(k), :], src_dram[:, tiles(k), :]).then_inc(src_in[k], 16)
                    for dst, data in loads:
                        sp.dma_start(dst, data).then_inc(loaded, 16)
                    if loads:
                        sp.wait_ge(loaded, 16 * len(loads))


def load(nc, name, pairs):
    with phase(nc, name) as m:
        loaded = m.sem("loaded")
        with nc.Block() as block:
            @block.sync
            def _(sp):
                for dst, src in pairs[0::2]:
                    sp.dma_start(dst, src).then_inc(loaded, 16)
                sp.wait_ge(loaded, 16 * len(pairs))

            @block.scalar
            def _(act):
                for dst, src in pairs[1::2]:
                    act.dma_start(dst, src).then_inc(loaded, 16)


def transpose_all(nc, name, jobs, ident):
    with phase(nc, name) as m:
        bank = m.ps("bank", [P, 2, TPC, P])
        turned, evacuated = m.sem("turned"), m.sem("evacuated")
        groups = [jobs[i:i + TPC] for i in range(0, len(jobs), TPC)]
        with nc.Block() as block:
            @block.tensor
            def _(pe):
                for n, group in enumerate(groups):
                    after(pe, evacuated, sum(map(len, groups[:n - 1])) if n > 1 else 0)
                    for i, (dst, src) in enumerate(group):
                        p, q = src.shape
                        op = pe.transpose(bank[0:q, n % 2, i, 0:p], src, ident[0:p, 0:p])
                    op.then_inc(turned, 1)

            @block.vector
            def _(dve):
                for n, group in enumerate(groups):
                    dve.wait_ge(turned, n + 1)
                    for i, (dst, src) in enumerate(group):
                        p, q = src.shape
                        dve.tensor_copy(dst, bank[0:q, n % 2, i, 0:p]).then_inc(evacuated, 1)


def split(nc, name, jobs):
    with phase(nc, name) as m:
        hi_done = m.sem("hi_done")
        with nc.Block() as block:
            @block.vector
            def _(dve):
                for n, (hi, lo, a) in enumerate(jobs):
                    dve.tensor_copy(hi, a).then_inc(hi_done, 1)
                for n, (hi, lo, a) in enumerate(jobs):
                    if lo is not None:
                        dve.wait_ge(hi_done, n + 1)
                        dve.tensor_tensor(lo, a, f32(hi), ALU.subtract)


def keys_values(nc, name, ctx, K, V, WkT, WvT, bk, bv_all, ident, mask=None):
    n = B * SK // CH
    per = CH // SK
    with phase(nc, name) as m:
        ctx_nat = m.sb("ctx_nat", [P, 2, per, D])
        ctxT = m.sb("ctxT", [P, 2, CH])
        keep = m.sb("keep", [P, 2, CH], U8)
        y = m.sb("y", [P, 2, CH])
        bank_t, bank_k, bank_v = m.ps("bank_t", [P, 2, CH]), m.ps("bank_k", [P, 2, CH]), m.ps("bank_v", [P, 2, CH])
        ctx_in = [m.sem("ctx_in0"), m.sem("ctx_in1")]
        turned, ctxT_ready, k_done, v_done = m.sem("turned"), m.sem("ctxT_ready"), m.sem("k_done"), m.sem("v_done")
        y_ready, hi_ready, lo_ready, v_stored = m.sem("y_ready"), m.sem("hi_ready"), m.sem("lo_ready"), m.sem("v_stored")
        keep_in = [m.sem("keep_in0"), m.sem("keep_in1")]
        with nc.Block() as block:
            @block.sync
            def _(sp):
                def chunk(c, par):
                    after(sp, turned, c - 1)
                    sp.dma_start(ctx_nat[:, par], ctx[span(c * per, per), :, :].rearrange("b k d -> k b d"))\
                      .then_inc(ctx_in[par], 16)
                in_pairs(sp, n, chunk)

            @block.tensor
            def _(pe):
                def turn(c, par):
                    pe.wait_ge(ctx_in[par], half(c, par) * 16)
                    after(pe, ctxT_ready, c - 1)
                    for i in range(per):
                        op = pe.transpose(bank_t[:, par, P * i:P * i + P], ctx_nat[:, par, i, :], ident[:, :])
                    op.then_inc(turned, 1)

                def chunk(c, par):
                    if not (isinstance(c, int) and c + 1 >= n):
                        turn(c + 1, 1 - par)
                    pe.wait_ge(ctxT_ready, c + 1)
                    after(pe, y_ready, c - 1)
                    pe.matmul(bank_k[:, par, :], WkT[:, :], ctxT[:, par, :], start=True, stop=True).then_inc(k_done, 1)
                    after(pe, v_stored, c - 1)
                    for i in range(per):
                        op = pe.matmul(bank_v[:, par, P * i:P * i + P], ctxT[:, par, P * i:P * i + P], WvT[:, :],
                                       start=True, stop=True)
                    op.then_inc(v_done, 1)
                turn(0, 0)
                in_pairs(pe, n, chunk)

            @block.scalar
            def _(act):
                def chunk(c, par):
                    act.wait_ge(turned, c + 1)
                    after(act, v_done, c - 1)
                    act.activation(ctxT[:, par, :], bank_t[:, par, :], ACT.Copy).then_inc(ctxT_ready, 1)
                    if not (isinstance(c, int) and c == 0):
                        high(c - 1, 1 - par)
                    if mask is not None and not (isinstance(c, int) and c + 1 >= n):
                        load_keep(c + 1, 1 - par)

                def load_keep(c, par):
                    after(act, y_ready, c - 1)
                    rows = mask[span(c * per, per), :].rearrange("b k -> (b k)").unsqueeze(0)
                    act.dma_start(keep[:, par], rows.broadcast_to([P, CH])).then_inc(keep_in[par], 16)

                def high(c, par):
                    act.wait_ge(y_ready, c + 1)
                    for v in range(2):
                        act.activation(K[hi_rows(v), v, span(c * CH, CH)], y[hi_rows(v), par, :], ACT.Copy)\
                           .then_inc(hi_ready, 1)
                if mask is not None:
                    load_keep(0, 0)
                in_pairs(act, n, chunk)
                high(n - 1, 1)

            @block.vector
            def _(dve):
                def chunk(c, par):
                    dve.wait_ge(k_done, c + 1)
                    after(dve, hi_ready, 2 * (c - 1))
                    after(dve, lo_ready, c - 1)
                    if mask is not None:
                        dve.wait_ge(keep_in[par], half(c, par) * 16)
                        dve.scalar_tensor_tensor(out=y[:, par, :], in0=bank_k[:, par, :], scalar=bk[:, 0:1],
                                                 in1=keep[:, par, :], op0=ALU.add, op1=ALU.mult).then_inc(y_ready, 1)
                    else:
                        dve.tensor_scalar(y[:, par, :], bank_k[:, par, :], bk[:, 0:1], None, ALU.add).then_inc(y_ready, 1)
                    dve.wait_ge(v_done, c + 1)
                    dve.tensor_tensor(V[:, span(c * per, per), :],
                                      bank_v[:, par, :].rearrange("p (i d) -> p i d", d=D),
                                      cols(bv_all[:, :], 1, per), ALU.add).then_inc(v_stored, 1)
                    if not (isinstance(c, int) and c == 0):
                        low(c - 1, 1 - par)

                def low(c, par):
                    for v in range(2):
                        dve.wait_ge(hi_ready, 2 * c + v + 1)
                        op = dve.tensor_tensor(K[lo_rows(v), v, span(c * CH, CH)], y[hi_rows(v), par, :],
                                               f32(K[hi_rows(v), v, span(c * CH, CH)]), ALU.subtract)
                    op.then_inc(lo_ready, 1)
                in_pairs(dve, n, chunk)
                low(n - 1, 1)


def half(c, par):
    return (c - par) // 2 + 1


def pack(dve, dst, y, k, hi_ready, lo_ready):
    at = span(k * CH, CH)
    for v in range(2):
        dve.tensor_copy(dst[hi_rows(v), v, at], y[hi_rows(v)]).then_inc(hi_ready, 1)
    for v in range(2):
        dve.wait_ge(hi_ready, 2 * k + v + 1)
        op = dve.tensor_tensor(dst[lo_rows(v), v, at], y[hi_rows(v)], f32(dst[hi_rows(v), v, at]), ALU.subtract)
    op.then_inc(lo_ready, 1)


def queries(nc, name, xnT, Q, WqT, bq):
    with phase(nc, name) as m:
        bank = m.ps("bank", [P, 2, CH])
        y = m.sb("y", [P, 2, CH])
        q_done, y_ready, hi_ready, lo_ready = m.sem("q_done"), m.sem("y_ready"), m.sem("hi_ready"), m.sem("lo_ready")
        with nc.Block() as block:
            @block.tensor
            def _(pe):
                def chunk(k, par):
                    after(pe, y_ready, k - 1)
                    pe.matmul(bank[:, par, :], WqT[:, :], xnT[:, span(k * CH, CH)], start=True, stop=True)\
                      .then_inc(q_done, 1)
                in_pairs(pe, NC, chunk)

            @block.scalar
            def _(act):
                def chunk(k, par):
                    act.wait_ge(q_done, k + 1)
                    after(act, lo_ready, k - 1)
                    act.activation(y[:, par, :], bank[:, par, :], ACT.Identity, bias=bq[:, 0:1]).then_inc(y_ready, 1)
                in_pairs(act, NC, chunk)

            @block.vector
            def _(dve):
                def chunk(k, par):
                    dve.wait_ge(y_ready, k + 1)
                    pack(dve, Q, y[:, par, :], k, hi_ready, lo_ready)
                in_pairs(dve, NC, chunk)


def attention(nc, name, K, V, Q, AT, con, nk, scale, den_eps=None, mask=None, mask_bias=None):
    own = nk < P
    n = B
    NKD = 2 * nk
    GH = CH // NKD
    KS = G // GH
    ident, sel, selm, mask4 = con["ident"], con["sel"], con["selm"], con["mask4"]
    with phase(nc, name) as m:
        Kst = m.sb("Kst", [P, 2, G, NKD], F32R)
        Qst = m.sb("Qst", [P, 4, G, J, S], F32R)
        Pr = m.sb("Pr", [P, 2, G, J * S])
        Vb = m.sb("Vb", [P, 2, D])
        mneg = m.sb("mneg", [P, 2, P])
        mx = m.sb("mx", [P, 2, PAIRS])
        mt2 = m.sb("mt2", [64, 2, P], BF16)
        sums = m.sb("sums", [P, 2, 2, S])
        ones = m.sb("ones", [P, W32])
        eps = m.sb("eps", [P, S]) if den_eps is not None else None
        ps_m = m.ps("ps_m", [P, PAIRS, P])
        ps_s = m.ps("ps_s", [P, PAIRS, P])
        ps_k, ps_q = m.ps("ps_k", [P, GH, NKD]), m.ps("ps_q", [P, G, 2 * S])
        ps_o = m.ps("ps_o", [P, 2, J, S])
        ps_t = m.ps("ps_t", [P, P])
        k_done, q_done, k_copied, q_copied = m.sem("k_done"), m.sem("q_done"), m.sem("k_copied"), m.sem("q_copied")
        mp_done, mx_done, mneg_ready = m.sem("mp_done"), m.sem("mx_done"), m.sem("mneg_ready")
        mt_done, mt_hi, mt_ready = m.sem("mt_done"), m.sem("mt_hi"), m.sem("mt_ready")
        st_done, addm_done, exp_done = m.sem("st_done"), m.sem("addm_done"), m.sem("exp_done")
        pv_done, added, summed = m.sem("pv_done"), m.sem("added"), m.sem("summed")
        eps_added, inverted, at_ready = m.sem("eps_added"), m.sem("inverted"), m.sem("at_ready")
        v_copied, set_up = m.sem("v_copied"), m.sem("set_up")
        if mask is not None:
            mrow8 = m.sb("mrow8", [1, 2, P], U8)
            mrow = m.sb("mrow", [P, 2, P], BF16)
            ones_row = m.sb("ones_row", [P, P], BF16)
            mask_in, mrow_ready = [m.sem("mask_in0"), m.sem("mask_in1")], m.sem("mrow_ready")

        def keys_of(i):
            return slice(nk * (i % 2), nk * (i % 2) + nk)

        def part(i):
            return keys_of(i) if own else slice(0, P)

        def is_first(u, few=1):
            return isinstance(u, int) and u < few

        def exists(u, count=n):
            return not isinstance(u, int) or u < count

        with nc.Block() as block:
            @block.tensor
            def _(pe):
                def key_stack(e, q, step):
                    after(pe, k_copied, e * KS + step)
                    for gi in range(GH):
                        g = step * GH + gi
                        keys = span(e * NKD, NKD)
                        op = pe.matmul(ps_k[:, gi, :], sel[:, g, 0, :], K[:, g // 2, keys], start=True, stop=True)
                    op.then_inc(k_done, 1)

                def query_stack(e):
                    after(pe, q_copied, e * 2)
                    for g in range(G):
                        tokens = span(e * 2 * S, 2 * S)
                        op = pe.matmul(ps_q[:, g, :], sel[:, g, 1, :], Q[:, g // 2, tokens], start=True, stop=True)
                    op.then_inc(q_done, 1)

                def scores_for_max(u, i, e):
                    pe.wait_ge(k_copied, e * KS + KS)
                    pe.wait_ge(q_copied, u + 1)
                    after(pe, mx_done, u)
                    if mask is not None:
                        pe.wait_ge(mrow_ready, u + 1)
                    for p in range(PAIRS):
                        q = Qst[:, i % 4, p // 2, 2 * (p % 2):2 * (p % 2) + 2, :]
                        first = p % 4 == 0
                        op = pe.matmul(ps_m[:, p, 0:nk], q, Kst[:, i // 2 % 2, p // 2, keys_of(i)],
                                       start=first or mask is None, stop=mask is None, skip_group_check=True)
                        if mask is not None and p % 4 == 3:
                            op = pe.matmul(ps_m[:, p - 3:p + 1, :], ones_row[:, :], cols(mrow[:, i % 2, :], 1, 4),
                                           start=False, stop=True, skip_group_check=True)
                    op.then_inc(mp_done, 1)

                def unit(u, i, e):
                    pe.wait_ge(mneg_ready, u + 1)
                    pe.transpose(ps_t[:, :], mneg[:, i % 2, :], ident[:, :]).then_inc(mt_done, 1)
                    after(pe, exp_done, u)
                    for g in range(G):
                        k = Kst[:, i // 2 % 2, g, :] if own else Kst[:, i // 2 % 2, g, keys_of(i)]
                        op = pe.matmul(ps_s[:, 2 * g:2 * g + 2, :], k, Qst[:, i, g, :, :],
                                       start=g % 2 == 0, stop=False, skip_group_check=True)
                    op.then_inc(st_done, 1)
                    if i % 2 == 0 and exists(e + 1, n // 2):
                        if KS == 2:
                            key_stack(e + 1, 1 - i // 2, 1)
                    if exists(u + 1):
                        scores_for_max(u + 1, i + 1, e + i % 2)
                    pe.wait_ge(mt_ready, u + 1)
                    for p in range(PAIRS):
                        op = pe.matmul(ps_s[:, p, :], selm[:, p, :], mt2[:, i % 2, :], start=False,
                                       stop=p % 4 == 3, skip_group_check=True)
                    op.then_inc(addm_done, 1)
                    if i % 2 == 1 and exists(e + 2, n // 2):
                        key_stack(e + 2, i // 2, 0)
                    if not is_first(u):
                        weigh(u - 1, i - 1, e - 1 + i % 2)
                    if i % 2 == 1 and exists(e + 2, n // 2):
                        query_stack(e + 2)

                def weigh(u, i, e):
                    pe.wait_ge(exp_done, u + 1)
                    pe.wait_ge(v_copied, e + 1 if own else u + 1)
                    vb = i // 2 % 2 if own else i % 2
                    after(pe, summed, u)
                    for g in range(G):
                        pe.matmul(ps_o[W32 * g:W32 * g + W32, 0, :, :], Vb[:, vb, W32 * g:W32 * g + W32],
                                  Pr[:, i % 2, g, :], start=True, stop=True)
                    for g in range(G):
                        op = pe.matmul(ps_o[W32 * g:W32 * g + W32, 1, :, :], ones[:, :], Pr[:, i % 2, g, :],
                                       start=True, stop=True)
                    op.then_inc(pv_done, 1)

                pe.wait_ge(set_up, 3 if own else 4 if mask is not None else 2)
                for step in range(KS):
                    key_stack(0, 0, step)
                query_stack(0)
                key_stack(1, 1, 0)
                scores_for_max(0, 0, 0)
                query_stack(1)
                in_fours(pe, n, unit)
                weigh(n - 1, 3, n // 2 - 1)

            @block.scalar
            def _(act):
                def copy_keys(e, q, step):
                    act.wait_ge(k_done, e * KS + step + 1)
                    after(act, st_done, (e - 1) * 2)
                    act.activation(Kst[:, q, step * GH:step * GH + GH, :], ps_k[:, :, :], ACT.Copy)\
                       .then_inc(k_copied, 1)

                def spread(u, i, e):
                    act.wait_ge(q_done, e + 1)
                    after(act, st_done, u - 3)
                    for j in range(J):
                        op = act.activation(Qst[:, i % 4, :, j, :], ps_q[:, :, S * (i % 2):S * (i % 2) + S],
                                            ACT.Copy, scale=mask4[:, j:j + 1])
                    op.then_inc(q_copied, 1)

                def load_mask(u, i):
                    after(act, mrow_ready, u - 1)
                    act.dma_start(mrow8[:, i % 2], mask[span(u, 1), :]).then_inc(mask_in[i % 2], 16)

                def unit(u, i, e):
                    if mask is not None and exists(u + 3):
                        load_mask(u + 3, i + 3)
                    if exists(u + 2):
                        spread(u + 2, i + 2, e + 1)
                    if KS == 2 and i % 2 == 0 and exists(e + 1, n // 2):
                        copy_keys(e + 1, 1 - i // 2, 1)
                    act.wait_ge(addm_done, u + 1)
                    after(act, pv_done, u - 1)
                    k = part(i)
                    out, src = Pr[k, i % 2], ps_s[k, :, :]
                    if mask_bias is not None:
                        act.activation(out, src, ACT.Exp, scale=scale, bias=mask_bias[:, span(u, 1)]).then_inc(exp_done, 1)
                    else:
                        act.activation(out, src, ACT.Exp, scale=scale).then_inc(exp_done, 1)
                    if i % 2 == 1 and exists(e + 2, n // 2):
                        copy_keys(e + 2, i // 2, 0)

                if own:
                    act.wait_ge(set_up, 3)
                if mask is not None:
                    for u in range(3):
                        load_mask(u, u)
                for step in range(KS):
                    copy_keys(0, 0, step)
                spread(0, 0, 0)
                copy_keys(1, 1, 0)
                spread(1, 1, 0)
                in_fours(act, n, unit)

            @block.gpsimd
            def _(pool):
                if den_eps is not None:
                    pool.memset(eps[:, :], den_eps)
                pool.memset(ones[:, :], 1.0).then_inc(set_up, 1)
                pool.memset(mneg[:, :, :], 0.0).then_inc(set_up, 1)
                if own:
                    pool.memset(Pr[:, :, :, :], 0.0).then_inc(set_up, 1)
                if mask is not None:
                    pool.memset(ones_row[:, :], 1.0).then_inc(set_up, 1)
                    pool.memset(mrow[:, :, :], 0.0).then_inc(set_up, 1)

                def values(u, i, e):
                    if own and i % 2 == 0:
                        after(pool, pv_done, u - 2)
                        pool.tensor_copy(Vb[:, i // 2 % 2, :], V[:, e, :]).then_inc(v_copied, 1)
                    if not own:
                        after(pool, pv_done, u - 1)
                        pool.tensor_copy(Vb[:, i % 2, :], V[:, u, :]).then_inc(v_copied, 1)

                def add_eps(u, i):
                    if den_eps is not None:
                        pool.wait_ge(summed, u + 1)
                        d = sums[:, i % 2, 1]
                        pool.tensor_tensor(d, d, eps[:, :], ALU.add).then_inc(eps_added, 1)

                def outputs(u, i):
                    pool.wait_ge(inverted, u + 1)
                    pool.tensor_tensor(AT[:, span(u * S, S)], sums[:, i % 2, 0], sums[:, i % 2, 1], ALU.mult)\
                        .then_inc(at_ready, 1)

                def unit(u, i, e):
                    values(u, i, e)
                    if not is_first(u, 2):
                        add_eps(u - 2, i)
                        outputs(u - 2, i)
                in_fours(pool, n, unit)
                for u in (n - 2, n - 1):
                    add_eps(u, u)
                    outputs(u, u)

            @block.vector
            def _(dve):
                def mask_row(u, i):
                    dve.wait_ge(mask_in[i % 2], half(u, i % 2) * 16)
                    after(dve, mp_done, u - 1)
                    dve.tensor_scalar(mrow[0:1, i % 2], mrow8[:, i % 2], -MASKED_UNSCALED, MASKED_UNSCALED,
                                      ALU.mult, ALU.add).then_inc(mrow_ready, 1)

                def maxima(u, i):
                    dve.wait_ge(mp_done, u + 1)
                    dve.tensor_reduce(mx[:, i % 2], ps_m[:, :, 0:nk], AX.X, ALU.max).then_inc(mx_done, 1)

                def negate(u, i):
                    dve.wait_ge(mx_done, u + 1)
                    after(dve, mt_done, u - 1)
                    dve.tensor_scalar(mneg[:, i % 2, 0:64].rearrange("p (a b) -> p a b", a=2)[:, :, 0:PAIRS],
                                      cols(mx[:, i % 2], 1, 2), -1.0, None, ALU.mult).then_inc(mneg_ready, 1)

                def minus_max_hi(u, i):
                    dve.wait_ge(mt_done, u + 1)
                    after(dve, addm_done, u - 1)
                    dve.tensor_copy(mt2[:, i % 2], ps_t[0:64, :]).then_inc(mt_hi, 1)

                def minus_max_lo(u, i):
                    dve.wait_ge(mt_hi, u + 1)
                    dve.tensor_tensor(mt2[32:64, i % 2], ps_t[32:64, :], mt2[32:64, i % 2], ALU.subtract)\
                       .then_inc(mt_ready, 1)

                def own_heads(u, i, j):
                    out, at = sums[:, i % 2], ps_o[:, :, j, :]
                    if j == 0:
                        dve.wait_ge(pv_done, u + 1)
                        after(dve, at_ready, u - 1)
                        op = dve.tensor_scalar(out, at, mask4[:, 0:1], None, ALU.mult)
                    else:
                        dve.wait_ge(added, u * (J - 1) + j)
                        op = dve.scalar_tensor_tensor(out=out, in0=at, scalar=mask4[:, j:j + 1], in1=out,
                                                      op0=ALU.mult, op1=ALU.add)
                    op.then_inc(summed if j == J - 1 else added, 1)

                def invert(u, i):
                    if den_eps is not None:
                        dve.wait_ge(eps_added, u + 1)
                    else:
                        dve.wait_ge(summed, u + 1)
                    dve.reciprocal(sums[:, i % 2, 1], sums[:, i % 2, 1]).then_inc(inverted, 1)

                def unit(u, i, e):
                    past = not is_first(u, 2)
                    if past:
                        own_heads(u - 2, i, 0)
                    minus_max_hi(u, i)
                    if past:
                        own_heads(u - 2, i, 1)
                    minus_max_lo(u, i)
                    if past:
                        own_heads(u - 2, i, 2)
                        own_heads(u - 2, i, 3)
                    if mask is not None and exists(u + 2):
                        mask_row(u + 2, i)
                    if exists(u + 1):
                        maxima(u + 1, i + 1)
                    if exists(u + 1):
                        negate(u + 1, i + 1)
                    if past:
                        invert(u - 2, i)

                dve.wait_ge(set_up, 4 if mask is not None else 2)
                if mask is not None:
                    mask_row(0, 0)
                    mask_row(1, 1)
                maxima(0, 0)
                negate(0, 0)
                in_fours(dve, n, unit)
                for u in (n - 2, n - 1):
                    for j in range(J):
                        own_heads(u, u, j)
                    invert(u, u)


def project_add(nc, name, AT, x, ident, WT=None, bias=None):
    with phase(nc, name) as m:
        bank, bank_t = m.ps("bank", [P, 2, CH]), m.ps("bank_t", [P, 2, TPC, D])
        y = m.sb("y", [P, 2, CH])
        projected, y_ready, turned, added = m.sem("projected"), m.sem("y_ready"), m.sem("turned"), m.sem("added")
        with nc.Block() as block:
            @block.tensor
            def _(pe):
                def project(k, par):
                    if WT is not None:
                        after(pe, y_ready, k - 1)
                        pe.matmul(bank[:, par, :], WT[:, :], AT[:, span(k * CH, CH)], start=True, stop=True)\
                          .then_inc(projected, 1)

                def chunk(k, par):
                    if not (isinstance(k, int) and k + 1 >= NC):
                        project(k + 1, 1 - par)
                    pe.wait_ge(y_ready, k + 1)
                    after(pe, added, k - 1)
                    for i in range(TPC):
                        op = pe.transpose(bank_t[:, par, i, :], y[:, par, P * i:P * i + P], ident[:, :])
                    op.then_inc(turned, 1)
                project(0, 0)
                in_pairs(pe, NC, chunk)

            @block.scalar
            def _(act):
                def chunk(k, par):
                    after(act, turned, k - 1)
                    if WT is not None:
                        act.wait_ge(projected, k + 1)
                        act.activation(y[:, par, :], bank[:, par, :], ACT.Identity, bias=bias[:, 0:1]).then_inc(y_ready, 1)
                    else:
                        act.activation(y[:, par, :], AT[:, span(k * CH, CH)], ACT.Copy).then_inc(y_ready, 1)
                in_pairs(act, NC, chunk)

            @block.vector
            def _(dve):
                def chunk(k, par):
                    dve.wait_ge(turned, k + 1)
                    xs = x[:, span(k * TPC, TPC), :]
                    dve.tensor_tensor(xs, xs, bank_t[:, par], ALU.add).then_inc(added, 1)
                in_pairs(dve, NC, chunk)


def route(nc, name, xnT, gateT, E, combT, ident, sigmoid_gate, shared_gate, splits=()):
    EX = E + 1 if shared_gate else E
    LOW, HIT = -3.0e38, 3.2e38
    with phase(nc, name) as m:
        bank, bank_t = m.ps("bank", [P, 2, CH]), m.ps("bank_t", [P, 2, TPC, P])
        bank_c = m.ps("bank_c", [P, 2, CH])
        lT = m.sb("lT", [P, 2, CH])
        L = m.sb("L", [P, T, EX])
        vals = m.sb("vals", [P, T, E + 8])
        best = m.sb("best", [P, T, 8])
        found = m.sb("found", [P, T, 8])
        marked = m.sb("marked", [P, T, E + 8])
        e1 = m.sb("e1", [P, T, EX])
        gap = m.sb("gap", [P, T, 1])
        den = m.sb("den", [P, T, 1])
        C = m.sb("C", [P, T, P])
        hi_done = m.sem("hi_done")
        logits_done, lT_ready, turned, L_ready = m.sem("logits_done"), m.sem("lT_ready"), m.sem("turned"), m.sem("L_ready")
        step, act_step, best_done, marked_done = m.sem("step"), m.sem("act_step"), m.sem("best_done"), m.sem("marked_done")
        prepared, comb_ready, c_turned, c_hi, c_lo = (m.sem("prepared"), m.sem("comb_ready"), m.sem("c_turned"),
                                                      m.sem("c_hi"), m.sem("c_lo"))
        with nc.Block() as block:
            @block.gpsimd
            def _(pool):
                pool.memset(vals[:, :, E:], LOW).then_inc(prepared, 1)
                pool.memset(found[:, :, :], LOW).then_inc(prepared, 1)
                pool.memset(C[:, :, :], 0.0).then_inc(prepared, 1)
                for n, (hi, lo, w) in enumerate(splits):
                    if lo is not None:
                        pool.wait_ge(hi_done, n + 1)
                        pool.tensor_tensor(lo, w, f32(hi), ALU.subtract)

            @block.tensor
            def _(pe):
                def logits(k, par):
                    after(pe, lT_ready, k - 1)
                    pe.matmul(bank[:, par, :], gateT[:, :], xnT[:, span(k * CH, CH)], start=True, stop=True)\
                      .then_inc(logits_done, 1)

                def chunk(k, par):
                    if not (isinstance(k, int) and k + 1 >= NC):
                        logits(k + 1, 1 - par)
                    pe.wait_ge(lT_ready, k + 1)
                    after(pe, L_ready, k - 1)
                    for i in range(TPC):
                        op = pe.transpose(bank_t[:, par, i, :], lT[:, par, P * i:P * i + P], ident[:, :])
                    op.then_inc(turned, 1)
                logits(0, 0)
                in_pairs(pe, NC, chunk)
                pe.wait_ge(comb_ready, 3 if shared_gate else 2)
                for k in range(NC):
                    after(pe, c_lo, k - 1)
                    for i in range(TPC):
                        op = pe.transpose(bank_c[:, k % 2, P * i:P * i + P], C[:, TPC * k + i, :], ident[:, :])
                    op.then_inc(c_turned, 1)

            @block.scalar
            def _(act):
                def chunk(k, par):
                    act.wait_ge(logits_done, k + 1)
                    after(act, turned, k - 1)
                    act.activation(lT[:, par, :], bank[:, par, :], ACT.Copy).then_inc(lT_ready, 1)
                in_pairs(act, NC, chunk)

                def split_hi():
                    for hi, lo, w in splits:
                        act.activation(hi, w, ACT.Copy).then_inc(hi_done, 1)
                if sigmoid_gate:
                    act.wait_ge(L_ready, NC)
                    act.activation(e1[:, :, :], L[:, :, :], ACT.Exp, scale=-1.0).then_inc(act_step, 1)
                    split_hi()
                else:
                    split_hi()
                    act.wait_ge(step, 3)
                    act.activation(e1[:, :, 0:E], e1[:, :, 0:E], ACT.Exp).then_inc(act_step, 1)
                    act.activation(e1[:, :, E:EX], L[:, :, E:EX], ACT.Exp, scale=-1.0).then_inc(act_step, 1)
                    act.activation(gap[:, :, :], gap[:, :, :], ACT.Exp).then_inc(act_step, 1)
                for k in range(NC):
                    act.wait_ge(c_turned, k + 1)
                    act.activation(combT[:, span(k * CH, CH)], bank_c[:, k % 2, :], ACT.Copy).then_inc(c_hi, 1)

            @block.vector
            def _(dve):
                count = [0]

                def chain(op):
                    count[0] += 1
                    op.then_inc(step, 1)

                def chained():
                    dve.wait_ge(step, count[0])

                def chunk(k, par):
                    dve.wait_ge(turned, k + 1)
                    dve.tensor_copy(L[:, span(k * TPC, TPC), :], bank_t[:, par, :, 0:EX]).then_inc(L_ready, 1)
                in_pairs(dve, NC, chunk)
                dve.wait_ge(L_ready, NC)
                dve.wait_ge(prepared, 3)
                if sigmoid_gate:
                    dve.wait_ge(act_step, 1)
                    chain(dve.tensor_scalar(e1[:, :, :], e1[:, :, :], 1.0, None, ALU.add))
                    chained()
                    chain(dve.reciprocal(vals[:, :, 0:E], e1[:, :, 0:E]))
                else:
                    chain(dve.tensor_copy(vals[:, :, 0:E], L[:, :, 0:E]))
                chained()
                for t in range(T):
                    dve.max(best[:, t, :], vals[:, t, 0:E]).then_inc(best_done, 1)
                dve.wait_ge(best_done, T)
                dve.tensor_copy(found[:, :, 0:2], best[:, :, 0:2]).then_inc(best_done, 1)
                dve.wait_ge(best_done, T + 1)
                for t in range(T):
                    dve.match_replace(marked[:, t, :], found[:, t, :], vals[:, t, :], HIT).then_inc(marked_done, 1)
                if sigmoid_gate:
                    chain(dve.tensor_tensor(den[:, :, :], best[:, :, 0:1], best[:, :, 1:2], ALU.add))
                    numerators = vals[:, :, 0:E]
                else:
                    chain(dve.tensor_tensor(e1[:, :, 0:E], L[:, :, 0:E], best[:, :, 0:1].broadcast_to([P, T, E]),
                                            ALU.subtract))
                    chain(dve.tensor_tensor(gap[:, :, :], best[:, :, 1:2], best[:, :, 0:1], ALU.subtract))
                    dve.wait_ge(act_step, 3)
                    chain(dve.tensor_scalar(den[:, :, :], gap[:, :, :], 1.0, None, ALU.add))
                    numerators = e1[:, :, 0:E]
                chained()
                chain(dve.reciprocal(den[:, :, :], den[:, :, :]))
                dve.wait_ge(marked_done, T)
                chain(dve.scalar_tensor_tensor(out=marked[:, :, 0:E], in0=marked[:, :, 0:E], scalar=HIT,
                                               in1=numerators, op0=ALU.is_equal, op1=ALU.mult))
                chained()
                for at in (0, 32):
                    dve.tensor_tensor(C[:, :, at:at + E], marked[:, :, 0:E], den[:, :, 0:1].broadcast_to([P, T, E]),
                                      ALU.mult).then_inc(comb_ready, 1)
                if shared_gate:
                    chain(dve.tensor_scalar(e1[:, :, E:EX], e1[:, :, E:EX], 1.0, None, ALU.add))
                    chained()
                    chain(dve.reciprocal(e1[:, :, E:EX], e1[:, :, E:EX]))
                    chained()
                    dve.tensor_copy(C[:, :, 0:64].rearrange("p t (a e) -> p t a e", a=2)[:, :, :, E:EX],
                                    cols(e1[:, :, E:EX], 2, 2)).then_inc(comb_ready, 1)
                for k in range(NC):
                    out = combT[:, span(k * CH, CH)]
                    dve.wait_ge(c_hi, k + 1)
                    dve.tensor_tensor(out[32:64], bank_c[32:64, k % 2, :], f32(out)[32:64], ALU.subtract).then_inc(c_lo, 1)


def gated_ffn(nc, name, xnT, blocks, x, ident, combT=None, out_bias=None, out_scale=1.0, out_dram=None):
    F = len(blocks)
    weighted = [f for f in range(F) if blocks[f][7] is not None]
    makers = [f for f in weighted if f == 0 or blocks[f][7] is not blocks[f - 1][7]]
    NM = len(makers)
    with phase(nc, name) as m:
        Xh, Xl = m.sb("Xh", [P, 2, CH], F32R), m.sb("Xl", [P, 2, CH], F32R)
        sg, hm, h = m.sb("sg", [P, 2, CH]), m.sb("hm", [P, 2, CH]), m.sb("h", [P, 2, CH])
        Hh, Hl = m.sb("Hh", [P, 2, CH], F32R), m.sb("Hl", [P, 2, CH], F32R)
        y = m.sb("y", [P, CH])
        ps_g, ps_u, ps_w = m.ps("ps_g", [P, 2, CH]), m.ps("ps_u", [P, 2, CH]), m.ps("ps_w", [P, CH])
        ps_o, ps_t = m.ps("ps_o", [P, 2, CH]), m.ps("ps_t", [P, TPC, D])
        xh_ready, x_ready = m.sem("xh_ready"), m.sem("x_ready")
        g_done, u_done, w_done, down_done = m.sem("g_done"), m.sem("u_done"), m.sem("w_done"), m.sem("down_done")
        sg_ready, hm_ready, h_ready = m.sem("sg_ready"), m.sem("hm_ready"), m.sem("h_ready")
        h_hi, h_lo = m.sem("h_hi"), m.sem("h_lo")
        y_ready, turned, added, stored = m.sem("y_ready"), m.sem("turned"), m.sem("added"), m.sem("stored")

        def slot(f, par):
            return (par * F + f) % 2

        def before(k, par, f, lag):
            if f >= lag:
                return k, par, f - lag
            return None if isinstance(k, int) and k == 0 else (k - 1, 1 - par, f - lag + F)

        with nc.Block() as block:
            @block.tensor
            def _(pe):
                def gates(k, par, f):
                    gh, gl, uh, ul, _, _, r, _, _, _ = blocks[f]
                    b = slot(f, par)
                    n = k * F + f
                    if f == 0:
                        pe.wait_ge(x_ready, k + 1)
                    after(pe, sg_ready, n - 1)
                    for w, xs, start in ((gh, Xh, True), (gl, Xh, False), (gh, Xl, False)):
                        op = pe.matmul(ps_g[0:r, b, :], w, xs[:, par, :], start=start, stop=not start and xs is Xl)
                    op.then_inc(g_done, 1)
                    after(pe, hm_ready, n - 1)
                    for w, xs, start in ((uh, Xh, True), (ul, Xh, False), (uh, Xl, False)):
                        op = pe.matmul(ps_u[0:r, b, :], w, xs[:, par, :], start=start, stop=not start and xs is Xl)
                    op.then_inc(u_done, 1)

                def weights(k, f):
                    if f == makers[0]:
                        after(pe, h_ready, (k - 1) * F + weighted[-1] + 1)
                    else:
                        after(pe, h_ready, k * F + f)
                    pe.matmul(ps_w[:, :], blocks[f][7], combT[:, span(k * CH, CH)], start=True, stop=True)\
                      .then_inc(w_done, 1)

                def down(k, par, f):
                    _, _, _, _, dh, dl, r, _, _, _ = blocks[f]
                    b = slot(f, par)
                    if f == 0:
                        after(pe, y_ready, k - 1)
                    pe.wait_ge(h_lo, k * F + f + 1)
                    pe.matmul(ps_o[:, par, :], dh, Hh[0:r, b, :], start=f == 0, stop=False)
                    pe.matmul(ps_o[:, par, :], dl, Hh[0:r, b, :], start=False, stop=False)
                    pe.matmul(ps_o[:, par, :], dh, Hl[0:r, b, :], start=False, stop=f == F - 1)\
                      .then_inc(down_done, 1)

                def turn(k):
                    pe.wait_ge(y_ready, k + 1)
                    after(pe, added, k)
                    for i in range(TPC):
                        op = pe.transpose(ps_t[:, i, :], y[:, P * i:P * i + P], ident[:, :])
                    op.then_inc(turned, 1)

                def chunk(k, par):
                    for f in range(F):
                        gates(k, par, f)
                        old = before(k, par, f, 2)
                        if old is not None:
                            down(*old)
                        if f in makers:
                            weights(k, f)
                        if f == 2 and not (isinstance(k, int) and k == 0):
                            turn(k - 1)
                in_pairs(pe, NC, chunk)
                down(NC - 1, 1, F - 2)
                down(NC - 1, 1, F - 1)
                turn(NC - 1)

            @block.scalar
            def _(act):
                def chunk(k, par):
                    for f in range(F):
                        r, bg = blocks[f][6], blocks[f][8]
                        b = slot(f, par)
                        act.wait_ge(g_done, k * F + f + 1)
                        after(act, hm_ready, k * F + f - 1)
                        if bg is None:
                            op = act.activation(sg[0:r, b, :], ps_g[0:r, b, :], ACT.Silu)
                        else:
                            op = act.activation(sg[0:r, b, :], ps_g[0:r, b, :], ACT.Silu, bias=bg)
                        op.then_inc(sg_ready, 1)
                        old = before(k, par, f, 1)
                        if old is not None:
                            high(*old)
                        if f == 1 and not (isinstance(k, int) and k == 0):
                            finish(k - 1, 1 - par)

                def high(k, par, f):
                    r, b, n = blocks[f][6], slot(f, par), k * F + f
                    act.wait_ge(h_ready, n + 1)
                    after(act, down_done, n - 1)
                    act.activation(Hh[0:r, b, :], h[0:r, b, :], ACT.Copy).then_inc(h_hi, 1)

                def finish(k, par):
                    act.wait_ge(down_done, (k + 1) * F)
                    after(act, turned, k)
                    if out_bias is None:
                        op = act.activation(y[:, :], ps_o[:, par, :], ACT.Copy)
                    else:
                        op = act.activation(y[:, :], ps_o[:, par, :], ACT.Identity, bias=out_bias[:, 0:1])
                    op.then_inc(y_ready, 1)
                in_pairs(act, NC, chunk)
                high(NC - 1, 1, F - 1)
                finish(NC - 1, 1)

            @block.vector
            def _(dve):
                def halves(k, par):
                    after(dve, u_done, (k - 1) * F)
                    src = xnT[:, span(k * CH, CH)]
                    dve.tensor_copy(Xh[:, par, :], src).then_inc(xh_ready, 1)
                    dve.wait_ge(xh_ready, k + 1)
                    dve.tensor_tensor(Xl[:, par, :], src, f32(Xh[:, par, :]), ALU.subtract).then_inc(x_ready, 1)

                def low(k, par, f):
                    r, b, n = blocks[f][6], slot(f, par), k * F + f
                    dve.wait_ge(h_hi, n + 1)
                    after(dve, down_done, n - 1)
                    dve.tensor_tensor(Hl[0:r, b, :], h[0:r, b, :], f32(Hh[0:r, b, :]), ALU.subtract).then_inc(h_lo, 1)

                def chunk(k, par):
                    for f in range(F):
                        r, bu, b, n = blocks[f][6], blocks[f][9], slot(f, par), k * F + f
                        old = before(k, par, f, 1)
                        plain = blocks[f][7] is None
                        dve.wait_ge(sg_ready, n + 1)
                        dve.wait_ge(u_done, n + 1)
                        after(dve, h_lo, n - 1)
                        dst = h[0:r, b, :] if plain else hm[0:r, b, :]
                        if bu is None:
                            op = dve.tensor_tensor(dst, sg[0:r, b, :], ps_u[0:r, b, :], ALU.mult)
                        else:
                            op = dve.scalar_tensor_tensor(out=dst, in0=ps_u[0:r, b, :], scalar=bu,
                                                          in1=sg[0:r, b, :], op0=ALU.add, op1=ALU.mult)
                        op.then_inc(hm_ready, 1)
                        if old is not None:
                            low(*old)
                        dve.wait_ge(hm_ready, n + 1)
                        if plain:
                            dve.sem_inc(h_ready, 1)
                        else:
                            made = sum(mk <= f for mk in makers)
                            dve.wait_ge(w_done, k * NM + made)
                            dve.tensor_tensor(h[0:r, b, :], hm[0:r, b, :], ps_w[0:r, :], ALU.mult).then_inc(h_ready, 1)
                        if f == 0 and not (isinstance(k, int) and k + 1 >= NC):
                            halves(k + 1, 1 - par)
                        if f == 2 and not (isinstance(k, int) and k == 0):
                            add(k - 1)

                def add(k):
                    dve.wait_ge(turned, k + 1)
                    xs = x[:, span(k * TPC, TPC), :]
                    dve.scalar_tensor_tensor(out=xs, in0=ps_t[:, :, :], scalar=out_scale, in1=xs,
                                             op0=ALU.mult, op1=ALU.add).then_inc(added, 1)
                halves(0, 0)
                in_pairs(dve, NC, chunk)
                low(NC - 1, 1, F - 1)
                add(NC - 1)

            if out_dram is not None:
                @block.sync
                def _(sp):
                    for k in range(NC):
                        at = slice(k * TPC, k * TPC + TPC)
                        sp.wait_ge(added, k + 1)
                        sp.dma_start(out_dram[:, at, :], x[:, at, :]).then_inc(stored, 16)
                    sp.wait_ge(stored, 16 * NC)


def linear_attention(nc, name, xn, xnT, x1, Wq, Wkv, bq, bkv_all):
    with phase(nc, name) as m:
        tT = m.sb("tT", [P, 2, P])
        qb, qp, kp = (m.sb(s, [P, 2, P]) for s in ("qb", "qp", "kp"))
        qka, qke = m.sb("qka", [P, 2, 2, P]), m.sb("qke", [P, 2, 2, P])
        kv = m.sb("kv", [P, 2, 2 * D + 1])
        state = m.sb("state", [P, 2, 2, D + 1])
        den = m.sb("den", [P, 2, 1])
        ps_q, ps_kv = m.ps("ps_q", [P, 2, 512]), m.ps("ps_kv", [P, 2, 512])
        ps_s, ps_n = m.ps("ps_s", [P, 2, 512]), m.ps("ps_n", [P, 2, 512])
        def exists(t):
            return not isinstance(t, int) or t < T

        set_up, tT_ready, qkv_done = m.sem("set_up"), m.sem("tT_ready"), m.sem("qkv_done")
        q_min, q_max, kv_read, k_min = m.sem("q_min"), m.sem("q_max"), m.sem("kv_read"), m.sem("k_min")
        exp_done, features, state_done = m.sem("exp_done"), m.sem("features"), m.sem("state_done")
        state_ready, num_done, den_step, x1_ready = (m.sem("state_ready"), m.sem("num_done"), m.sem("den_step"),
                                                     m.sem("x1_ready"))
        with nc.Block() as block:
            @block.gpsimd
            def _(pool):
                pool.memset(kv[:, :, 2 * D:], 1.0).then_inc(set_up, 1)

                def tile(t, par):
                    after(pool, qkv_done, t - 1)
                    pool.wait_ge(set_up, 1)
                    pool.tensor_copy(tT[:, par, :], xnT[:, span(t * P, P)]).then_inc(tT_ready, 1)
                in_pairs(pool, T, tile)

            @block.tensor
            def _(pe):
                def project(t, par):
                    pe.wait_ge(tT_ready, t + 1)
                    after(pe, q_max, t - 1)
                    after(pe, kv_read, t - 1)
                    pe.matmul(ps_q[:, par, 0:P], Wq, tT[:, par, :], start=True, stop=True)
                    pe.matmul(ps_kv[:, par, 0:2 * D], tT[:, par, :], Wkv, start=True, stop=True).then_inc(qkv_done, 1)

                def sum_keys(t, par):
                    pe.wait_ge(features, t + 1)
                    after(pe, state_ready, t)
                    for s in range(2):
                        rows = slice(S * s, S * s + S)
                        op = pe.matmul(ps_s[:, s, 0:D + 1], kp[rows, par, :], kv[rows, par, D:], start=True, stop=True)
                    op.then_inc(state_done, 1)

                def tile(t, par):
                    if exists(t + 2):
                        project(t + 2, par)
                    if exists(t + 1):
                        sum_keys(t + 1, 1 - par)
                    pe.wait_ge(state_ready, t + 1)
                    after(pe, x1_ready, t - 1)
                    for s in range(2):
                        op = pe.matmul(ps_n[S * s:S * s + S, par, 0:D + 1], qp[:, par, S * s:S * s + S],
                                       state[:, par, s, :], start=True, stop=True)
                    op.then_inc(num_done, 1)
                pe.wait_ge(set_up, 1)
                project(0, 0)
                project(1, 1)
                sum_keys(0, 0)
                in_pairs(pe, T, tile)

            @block.scalar
            def _(act):
                def exponentials(t, par):
                    act.wait_ge(k_min, t + 1)
                    after(act, features, t - 1)
                    act.activation(qke[:, par], qka[:, par], ACT.Exp).then_inc(exp_done, 1)

                def keep_sums(t, par):
                    act.wait_ge(state_done, t + 1)
                    after(act, num_done, t - 1)
                    act.activation(state[:, par, :, :], ps_s[:, :, 0:D + 1], ACT.Copy).then_inc(state_ready, 1)

                def tile(t, par):
                    if exists(t + 1):
                        keep_sums(t + 1, 1 - par)
                    if exists(t + 2):
                        exponentials(t + 2, par)
                exponentials(0, 0)
                exponentials(1, 1)
                keep_sums(0, 0)
                in_pairs(act, T, tile)

            @block.vector
            def _(dve):
                def inputs(t, par):
                    dve.wait_ge(qkv_done, t + 1)
                    after(dve, state_done, t - 1)
                    after(dve, exp_done, t - 1)
                    dve.tensor_tensor(kv[:, par, 0:2 * D], ps_kv[:, par, 0:2 * D], bkv_all[:, :], ALU.add)\
                       .then_inc(kv_read, 1)
                    dve.tensor_scalar(qka[:, par, 0], ps_q[:, par, 0:P], bq[:, 0:1], 0.0, ALU.add, ALU.min)\
                       .then_inc(q_min, 1)
                    dve.tensor_scalar(qb[:, par, :], ps_q[:, par, 0:P], bq[:, 0:1], 0.0, ALU.add, ALU.max)\
                       .then_inc(q_max, 1)
                    dve.wait_ge(kv_read, t + 1)
                    dve.tensor_scalar(qka[:, par, 1], kv[:, par, 0:D], 0.0, None, ALU.min).then_inc(k_min, 1)

                def feature_maps(t, par):
                    dve.wait_ge(q_max, t + 1)
                    dve.wait_ge(exp_done, t + 1)
                    after(dve, num_done, t - 1)
                    dve.tensor_tensor(qp[:, par, :], qb[:, par, :], qke[:, par, 0], ALU.add)
                    dve.scalar_tensor_tensor(out=kp[:, par, :], in0=kv[:, par, 0:D], scalar=0.0, in1=qke[:, par, 1],
                                             op0=ALU.max, op1=ALU.add).then_inc(features, 1)

                def add_eps(t, par):
                    dve.wait_ge(num_done, t + 1)
                    dve.tensor_scalar(den[:, par, :], ps_n[:, par, D:D + 1], 1e-6, None, ALU.add).then_inc(den_step, 1)

                def divide(t, par):
                    dve.wait_ge(den_step, 2 * t + 1)
                    dve.reciprocal(den[:, par, :], den[:, par, :]).then_inc(den_step, 1)
                    dve.wait_ge(den_step, 2 * t + 2)
                    dve.scalar_tensor_tensor(out=x1[:, t, :], in0=ps_n[:, par, 0:D], scalar=den[:, par, 0:1],
                                             in1=xn[:, t, :], op0=ALU.mult, op1=ALU.add).then_inc(x1_ready, 1)

                def tile(t, par):
                    if exists(t + 1):
                        feature_maps(t + 1, 1 - par)
                    if not (isinstance(t, int) and t == 0):
                        add_eps(t - 1, 1 - par)
                    if exists(t + 2):
                        inputs(t + 2, par)
                    if not (isinstance(t, int) and t == 0):
                        divide(t - 1, 1 - par)
                dve.wait_ge(set_up, 1)
                inputs(0, 0)
                inputs(1, 1)
                feature_maps(0, 0)
                in_pairs(dve, T, tile)
                add_eps(T - 1, 1)
                divide(T - 1, 1)


def centre(nc, name, xnT, Q):
    with phase(nc, name) as m:
        mean = m.sb("mean", [P, B])
        y = m.sb("y", [P, 2, CH])
        per = CH // S
        step, summed, y_ready, hi_ready, lo_ready = (m.sem("step"), m.sem("summed"), m.sem("y_ready"),
                                                     m.sem("hi_ready"), m.sem("lo_ready"))
        with nc.Block() as block:
            @block.vector
            def _(dve):
                def mean_of(k):
                    dve.tensor_reduce(mean[:, span(k * per, per)],
                                      xnT[:, span(k * CH, CH)].rearrange("p (b s) -> p b s", s=S),
                                      AX.X, ALU.add).then_inc(summed, 1)
                    dve.wait_ge(summed, k + 1)
                    dve.tensor_scalar(mean[:, span(k * per, per)], mean[:, span(k * per, per)], 1.0 / S, None,
                                      ALU.mult).then_inc(step, 1)

                def low(k):
                    for v in range(2):
                        dve.wait_ge(hi_ready, 2 * k + v + 1)
                        op = dve.tensor_tensor(Q[lo_rows(v), v, k * CH:k * CH + CH], y[hi_rows(v), k % 2],
                                               f32(Q[hi_rows(v), v, k * CH:k * CH + CH]), ALU.subtract)
                    op.then_inc(lo_ready, 1)

                mean_of(0)
                for k in range(NC):
                    if k > 1:
                        low(k - 2)
                    if k + 1 < NC:
                        mean_of(k + 1)
                    dve.wait_ge(step, k + 1)
                    after(dve, lo_ready, k - 1)
                    dve.tensor_tensor(y[:, k % 2].rearrange("p (b s) -> p b s", s=S),
                                      xnT[:, span(k * CH, CH)].rearrange("p (b s) -> p b s", s=S),
                                      cols(mean[:, span(k * per, per)], 2, S), ALU.subtract).then_inc(y_ready, 1)
                low(NC - 2)
                low(NC - 1)

            @block.scalar
            def _(act):
                for k in range(NC):
                    act.wait_ge(y_ready, k + 1)
                    for v in range(2):
                        act.activation(Q[hi_rows(v), v, k * CH:k * CH + CH], y[hi_rows(v), k % 2], ACT.Copy)\
                           .then_inc(hi_ready, 1)


def cross_attention(nc, tag, a, x, con, den_eps, mask=None, x_dram=None):
    with ExitStack() as stack:
        def sb(name, shape, dt=F32):
            return stack.enter_context(nc.sbuf_tensor(f"{tag}_{name}", shape, dt))

        WT = {w: sb(f"{w}T", [P, D]) for w in ("Wq", "Wk", "Wv", "Wo")}
        bq, bk, bo, bv_all = sb("bq", [P, 1]), sb("bk", [P, 1]), sb("bo", [P, 1]), sb("bv_all", [P, D])
        mask_bias = sb("mask_bias", [P, B]) if mask is not None else None
        xnT = sb("xnT", [P, B * S])
        with ExitStack() as early:
            raw = early.enter_context(nc.sbuf_tensor(f"{tag}_raw", [P, 4, D], F32))
            jobs = [(raw[:, i, :], a[f"{tag}_{w}"]) for i, w in enumerate(WT)]
            jobs += [(b[:, :], a[f"{tag}_{n}"].unsqueeze(1)) for n, b in (("bq", bq), ("bk", bk), ("bo", bo))]
            jobs += [(bv_all[:, :], a[f"{tag}_bv"].unsqueeze(0).broadcast_to([P, D]))]
            turns = [(t[:, :], raw[:, i, :]) for i, t in enumerate(WT.values())]
            if mask is not None:
                keep8 = early.enter_context(nc.sbuf_tensor(f"{tag}_keep8", [B, SK], U8))
                keep = early.enter_context(nc.sbuf_tensor(f"{tag}_keep", [B, SK], F32))
                jobs += [(keep8[:, :], mask)]
                turns += [(mask_bias[:, :], keep[:, :])]
            layernorm(nc, f"{tag}_ln", x, 1e-5, con["ident"], xnT=xnT, loads=jobs, src_dram=x_dram)
            if mask is not None:
                elementwise(nc, f"{tag}_keep_bias", lambda dve: dve.tensor_scalar(
                    keep[:, :], keep8[:, :], -MASKED, MASKED, ALU.mult, ALU.add))
            transpose_all(nc, f"{tag}_turn", turns, con["ident"])
        K = sb("K", [P, 2, B * SK], F32R)
        V = sb("V", [P, B, D])
        keys_values(nc, f"{tag}_kv", a["ctx_1024"], K, V, WT["Wk"], WT["Wv"], bk, bv_all, con["ident"], mask)
        Q = sb("Q", [P, 2, B * S], F32R)
        queries(nc, f"{tag}_q", xnT, Q, WT["Wq"], bq)
        attention(nc, f"{tag}_att", K, V, Q, xnT, con, SK, float(DH) ** -0.5, den_eps, mask, mask_bias)
        project_add(nc, f"{tag}_out", xnT, x, con["ident"], WT["Wo"], bo)


def elementwise(nc, name, op):
    with nc.Block() as block:
        @block.vector
        def _(dve):
            op(dve)


def linear_block(nc, a, x, con):
    pre = "L0_attn_"
    with ExitStack() as stack:
        def sb(name, shape, dt=F32):
            return stack.enter_context(nc.sbuf_tensor(f"la_{name}", shape, dt))

        rows = [P, P, L0_H - 2 * P]
        Wqkv = sb("Wqkv", [P, 3 * D])
        Wg, Wu, Wd = sb("Wg", [P, L0_H]), sb("Wu", [P, L0_H]), sb("Wd", [P, 3, D])
        dh, dl = sb("dh", [P, 3, D], F32R), sb("dl", [P, 3, D], F32R)
        gh, gl, uh, ul = (sb(n, [P, L0_H], F32R) for n in ("gh", "gl", "uh", "ul"))
        bq, bkv_all = sb("bq", [P, 1]), sb("bkv_all", [P, 2 * D])
        bg, bu, bd = sb("bg", [P, 3]), sb("bu", [P, 3]), sb("bd", [P, 1])
        vecs = {n: sb(n, [P, D]) for n in ("g1", "b1", "g2", "b2")}
        jobs = [(Wqkv[:, :], a[pre + "Wqkv"]), (Wg[:, :], a[pre + "Wg"]), (Wu[:, :], a[pre + "Wu"]),
                (bq[:, :], a[pre + "bqkv"][0:D].unsqueeze(1)),
                (bkv_all[:, :], a[pre + "bqkv"][D:3 * D].unsqueeze(0).broadcast_to([P, 2 * D])),
                (bd[:, :], a[pre + "bd"].unsqueeze(1))]
        for i, r in enumerate(rows):
            at = slice(P * i, P * i + r)
            jobs += [(Wd[0:r, i, :], a[pre + "Wd"][at, :]), (bg[0:r, i:i + 1], a[pre + "bg"][at].unsqueeze(1)),
                     (bu[0:r, i:i + 1], a[pre + "bu"][at].unsqueeze(1))]
        jobs += [(v[:, :], a[pre + n].unsqueeze(0).broadcast_to([P, D])) for n, v in vecs.items()]
        xn, xnT, x1 = sb("xn", [P, T, D]), sb("xnT", [P, B * S]), sb("x1", [P, T, D])
        layernorm(nc, "la_ln", x, 1e-5, con["ident"], xnT=xnT, nat=xn, loads=jobs)
        split(nc, "la_split", [(gh[:, :], gl[:, :], Wg[:, :]), (uh[:, :], ul[:, :], Wu[:, :])] +
              [(dh[0:r, i, :], dl[0:r, i, :], Wd[0:r, i, :]) for i, r in enumerate(rows)])
        linear_attention(nc, "la_att", xn, xnT, x1, Wqkv[:, 0:D], Wqkv[:, D:3 * D], bq, bkv_all)
        layernorm(nc, "la_ln1", x1, 1e-5, con["ident"], xnT=xnT, nat=xn, gain=vecs["g1"], shift=vecs["b1"])
        blocks = []
        for i, r in enumerate(rows):
            at = slice(P * i, P * i + r)
            blocks.append((gh[:, at], gl[:, at], uh[:, at], ul[:, at], dh[0:r, i, :], dl[0:r, i, :], r, None,
                           bg[0:r, i:i + 1], bu[0:r, i:i + 1]))
        gated_ffn(nc, "la_ffn", xnT, blocks, xn, con["ident"], out_bias=bd)
        layernorm(nc, "la_ln2", xn, 1e-5, con["ident"], gain=vecs["g2"], shift=vecs["b2"], add_to=x)


def moe0(nc, a, x, con):
    pre = "L0_ffn_"
    NB = L0_E * L0_F // P
    rows = [P, P, L0_SHARED - 2 * P]
    with ExitStack() as stack:
        def sb(name, shape, dt=F32):
            return stack.enter_context(nc.sbuf_tensor(f"m0_{name}", shape, dt))

        gh, gl, uh, ul = (sb(n, [P, NB + 3, P], F32R) for n in ("gh", "gl", "uh", "ul"))
        xnT, combT = sb("xnT", [P, B * S]), sb("combT", [P, B * S], F32R)
        dh, dl = sb("dh", [P, NB + 3, D], F32R), sb("dl", [P, NB + 3, D], F32R)
        gateT = sb("gateT", [P, P])
        spread = sb("spread", [P, len(L0_SPREAD), P], F32R)
        with ExitStack() as early:
            def eb(name, shape, dt=F32):
                return early.enter_context(nc.sbuf_tensor(f"m0_{name}", shape, dt))

            wgu = eb("wgu", [P, L0_E, 2 * L0_F])
            wd = eb("wd", [P, NB + 3, D])
            raw = eb("raw", [P, 3, 2, D])
            rawd = eb("rawd", [P, L0_SHARED])
            shT = eb("shT", [P, 2, 3 * P])
            gates = eb("gates", [P, D])
            spread_raw = eb("spread_raw", [P, len(L0_SPREAD) * P])
            jobs = [(wgu[:, :, :], a[pre + "w_gate_up"].rearrange("e d f -> d e f")),
                    (wd[:, 0:NB, :], a[pre + "w_down"].rearrange("e f d -> (e f) d").rearrange("(b r) d -> r b d", r=P)),
                    (rawd[:, :], a[pre + "shared_w_down"]),
                    (gates[0:L0_E, :], a[pre + "gate_w"]), (gates[L0_E:L0_E + 1, :], a[pre + "shared_gate_w"]),
                    (spread_raw[:, :], a["c_spread0"])]
            for i, r in enumerate(rows):
                at = slice(P * i, P * i + r)
                jobs += [(raw[0:r, i, 0, :], a[pre + "shared_w_gate"][at, :]),
                         (raw[0:r, i, 1, :], a[pre + "shared_w_up"][at, :])]
            elementwise(nc, "m0_zero", lambda dve: dve.memset(gates[:, :], 0.0))
            layernorm(nc, "m0_ln", x, 1e-5, con["ident"], xnT=xnT, loads=jobs)
            turns = [(gateT[:, :], gates[:, :])]
            for i, r in enumerate(rows):
                at = slice(P * i, P * i + r)
                turns += [(shT[:, 0, at], raw[0:r, i, 0, :]), (shT[:, 1, at], raw[0:r, i, 1, :]),
                          (wd[0:r, NB + i, :], rawd[:, at])]
            transpose_all(nc, "m0_turn", turns, con["ident"])
            pick = wgu[:, :, :].rearrange("p (b e) (s f) -> p s b e f", e=2, s=2)
            jobs = []
            for b in range(NB):
                for s, (hi, lo) in enumerate(((gh, gl), (uh, ul))):
                    jobs.append((hi[:, b, :].rearrange("p (e f) -> p e f", e=2),
                                 lo[:, b, :].rearrange("p (e f) -> p e f", e=2), pick[:, s, b]))
            for s, (hi, lo) in enumerate(((gh, gl), (uh, ul))):
                flat = [v[:, NB:, :].rearrange("p b r -> p (b r)")[:, 0:L0_SHARED] for v in (hi, lo)]
                jobs.append((flat[0], flat[1], shT[:, s, 0:L0_SHARED]))
            jobs.append((spread[:, :, :].rearrange("p b r -> p (b r)"), None, spread_raw[:, :]))
            jobs += [(dh[:, 0:NB, :], dl[:, 0:NB, :], wd[:, 0:NB, :])]
            jobs += [(dh[0:r, NB + i, :], dl[0:r, NB + i, :], wd[0:r, NB + i, :]) for i, r in enumerate(rows)]
            route(nc, "m0_route", xnT, gateT, L0_E, combT, con["ident"], False, True, splits=jobs)
        spreads = [spread[:, f, :] for f in range(NB + 1)]
        blocks = [(gh[:, f, 0:r], gl[:, f, 0:r], uh[:, f, 0:r], ul[:, f, 0:r], dh[0:r, f, :], dl[0:r, f, :], r,
                   spreads[min(f, NB)], None, None) for f, r in enumerate([P] * NB + rows)]
        gated_ffn(nc, "m0_ffn", xnT, blocks, x, con["ident"], combT=combT)


def moe1(nc, a, x, con, out_dram):
    pre = "L1_ffn_"
    FB = L1_F // P
    NB = L1_E * FB
    with ExitStack() as stack:
        def sb(name, shape, dt=F32):
            return stack.enter_context(nc.sbuf_tensor(f"m1_{name}", shape, dt))

        gh, gl, uh, ul = (sb(n, [P, NB + FB, P], F32R) for n in ("gh", "gl", "uh", "ul"))
        xnT, combT = sb("xnT", [P, B * S]), sb("combT", [P, B * S], F32R)
        dh, dl = sb("dh", [P, NB + FB, D], F32R), sb("dl", [P, NB + FB, D], F32R)
        gateT = sb("gateT", [P, P])
        spread = sb("spread", [P, L1_E, P], F32R)
        with ExitStack() as early:
            def eb(name, shape, dt=F32):
                return early.enter_context(nc.sbuf_tensor(f"m1_{name}", shape, dt))

            raw_g, raw_u = eb("raw_g", [P, NB + FB, P]), eb("raw_u", [P, NB + FB, P])
            wd = eb("wd", [P, NB + FB, D])
            spread_raw = eb("spread_raw", [P, L1_E * P])
            jobs = [(gateT[:, 0:L1_E], a[pre + "Wg"]), (spread_raw[:, :], a["c_spread1"])]
            for raw, we, ws in ((raw_g, "We1", "Ws1"), (raw_u, "We3", "Ws3")):
                v = raw[:, :, :].rearrange("p (e b) r -> p e (b r)", b=FB)
                jobs += [(v[:, 0:L1_E, :], a[pre + we].rearrange("e d f -> d e f")), (v[:, L1_E, :], a[pre + ws])]
            jobs += [(wd[:, 0:NB, :], a[pre + "We2"].rearrange("e f d -> (e f) d").rearrange("(b r) d -> r b d", r=P)),
                     (wd[:, NB:, :], a[pre + "Ws2"].rearrange("(b r) d -> r b d", r=P))]
            elementwise(nc, "m1_zero", lambda dve: dve.memset(gateT[:, :], 0.0))
            layernorm(nc, "m1_ln", x, 1e-5, con["ident"], xnT=xnT, loads=jobs)
            route(nc, "m1_route", xnT, gateT, L1_E, combT, con["ident"], True, False, splits=[(gh[:, :, :], gl[:, :, :], raw_g[:, :, :]), (uh[:, :, :], ul[:, :, :], raw_u[:, :, :]),
                                   (dh[:, :, :], dl[:, :, :], wd[:, :, :]),
                                   (spread[:, :, :].rearrange("p b r -> p (b r)"), None, spread_raw[:, :])])
        spreads = [spread[:, e, :] for e in range(L1_E)] + [None]
        blocks = [(gh[:, f, :], gl[:, f, :], uh[:, f, :], ul[:, f, :], dh[:, f, :], dl[:, f, :], P,
                   spreads[f // FB], None, None) for f in range(NB + FB)]
        gated_ffn(nc, "m1_ffn", xnT, blocks, x, con["ident"], combT=combT, out_scale=1.0 / 3.0, out_dram=out_dram)


def self_attention(nc, x, con):
    with ExitStack() as stack:
        def sb(name, shape, dt=F32):
            return stack.enter_context(nc.sbuf_tensor(f"sa_{name}", shape, dt))

        xn, xnT, AT = sb("xn", [P, T, D]), sb("xnT", [P, B * S]), sb("AT", [P, B * S])
        Q = sb("Q", [P, 2, B * S], F32R)
        layernorm(nc, "sa_ln", x, 1e-5, con["ident"], xnT=xnT, nat=xn)
        centre(nc, "sa_centre", xnT, Q)
        attention(nc, "sa_att", Q, xn, Q, AT, con, S, 1.0)
        project_add(nc, "sa_out", AT, x, con["ident"])


def perceiver_kernel(nc, a, out):
    x_dram = a["x"].rearrange("b s d -> (b s) d").rearrange("(t p) d -> p t d", p=P)
    out_dram = out.rearrange("b s d -> (b s) d").rearrange("(t p) d -> p t d", p=P)
    with ExitStack() as stack:
        def sb(name, shape, dt=F32):
            return stack.enter_context(nc.sbuf_tensor(name, shape, dt))

        x = sb("x", [P, T, D])
        ident = sb("ident", [P, P])
        mask4 = sb("mask4", [P, J])
        sel, selm = sb("sel", [P, G, 2, P], F32R), sb("selm", [64, PAIRS, P], BF16)
        with nc.sbuf_tensor("sel_raw", [P, G * 2 * P], F32) as sel_raw, \
                nc.sbuf_tensor("selm_raw", [64, PAIRS * P], F32) as selm_raw:
            load(nc, "first", [(ident[:, :], a["c_ident"]), (mask4[:, :], a["c_mask4"]),
                               (sel_raw[:, :], a["c_sel"]), (selm_raw[:, :], a["c_selm"])])
            split(nc, "sels", [(sel[:, :, :, :].rearrange("p a b c -> p (a b c)"), None, sel_raw[:, :]),
                               (selm[:, :, :].rearrange("p a b -> p (a b)"), None, selm_raw[:, :])])
        con = {"ident": ident, "sel": sel, "selm": selm, "mask4": mask4}
        cross_attention(nc, "L0_xattn", a, x, con, 1e-9, x_dram=x_dram)
        linear_block(nc, a, x, con)
        moe0(nc, a, x, con)
        cross_attention(nc, "L1_xattn", a, x, con, None, a["mask_BxS2_bf1"])
        self_attention(nc, x, con)
        moe1(nc, a, x, con, out_dram)


_INS = ['x', 'ctx_1024', 'mask_BxS2_bf1', 'L0_xattn_Wq', 'L0_xattn_bq', 'L0_xattn_Wk', 'L0_xattn_bk',
        'L0_xattn_Wv', 'L0_xattn_bv', 'L0_xattn_Wo', 'L0_xattn_bo', 'L0_attn_Wqkv', 'L0_attn_bqkv', 'L0_attn_Wg',
        'L0_attn_bg', 'L0_attn_Wu', 'L0_attn_bu', 'L0_attn_Wd', 'L0_attn_bd', 'L0_attn_g1', 'L0_attn_b1',
        'L0_attn_g2', 'L0_attn_b2', 'L0_ffn_gate_w', 'L0_ffn_w_gate_up', 'L0_ffn_w_down', 'L0_ffn_shared_w_gate',
        'L0_ffn_shared_w_up', 'L0_ffn_shared_w_down', 'L0_ffn_shared_gate_w', 'L1_xattn_Wq', 'L1_xattn_bq',
        'L1_xattn_Wk', 'L1_xattn_bk', 'L1_xattn_Wv', 'L1_xattn_bv', 'L1_xattn_Wo', 'L1_xattn_bo', 'L1_ffn_Wg',
        'L1_ffn_Ws1', 'L1_ffn_Ws3', 'L1_ffn_Ws2', 'L1_ffn_We1', 'L1_ffn_We3', 'L1_ffn_We2']


def kernel(**inputs):
    import numpy as _np
    import concourse.bacc as _bacc
    from concourse import mybir as _mybir
    from concourse.bass_utils import run_bass_kernel_spmd as _run

    nc = _bacc.Bacc("TRN2", target_bir_lowering=False, num_devices=1)
    sel, selm, mask4 = head_constants()
    constants = {"c_ident": _np.eye(P, dtype=_np.float32), "c_sel": sel, "c_selm": selm, "c_mask4": mask4,
                 "c_spread0": spread_constants(L0_SPREAD), "c_spread1": spread_constants(L1_SPREAD)}
    arrays, args = {}, {}
    for name in _INS:
        v = _np.ascontiguousarray(inputs[name])
        if v.dtype == _np.bool_:
            v = v.view(_np.uint8)
        arrays[f"in_{name}_dram"] = v
        args[name] = nc.dram_tensor(f"in_{name}_dram", v.shape, _mybir.dt.from_np(v.dtype), kind="ExternalInput").ap()
    for name, v in constants.items():
        arrays[f"in_{name}_dram"] = v
        args[name] = nc.dram_tensor(f"in_{name}_dram", v.shape, _mybir.dt.from_np(v.dtype), kind="ExternalInput").ap()
    out = nc.dram_tensor("out_0_dram", (B, S, D), F32, kind="ExternalOutput").ap()
    perceiver_kernel(nc, args, out)
    r = _run(nc, [arrays], core_ids=[0])
    return r.results[0]["out_0_dram"]
```
